# Optimizing a Trainium2 kernel written in Bass

```python
import numpy as np
import jax
import jax.numpy as jnp

def _softmax(x, axis=-1):
    return jax.nn.softmax(x, axis=axis)

def _gelu(x):
    return jax.nn.gelu(x, approximate=True)

def _silu(x):
    return jax.nn.silu(x)

def _sigmoid(x):
    return jax.nn.sigmoid(x)

def _layernorm(x, axis=-1, eps=1e-05):
    m = jnp.mean(x, axis=axis, keepdims=True)
    v = jnp.var(x, axis=axis, keepdims=True)
    return (x - m) / jnp.sqrt(v + eps)

def _scatter_add(tgt, idx, src, axis=0):
    return tgt.at[idx].add(src)

def _segment_sum(src, seg, n):
    return jax.ops.segment_sum(src, seg, n)
kernel_name = 'mk_flamingo_gated_d4_seqx_r8_bbe60a'

def setup_inputs(seed: int=0):
    np.random.seed(seed)
    _w = jnp.asarray

    def _rec_inputs():
        import jax
        import jax.numpy as jnp
        _rk = jax.random.key(seed)
        x = 7.22e-05 + 1 * jax.random.normal(jax.random.fold_in(_rk, 1), (32, 128, 128), jnp.float32)
        _lenS = 128 - jax.random.randint(jax.random.fold_in(_rk, 7), (32,), 0, max(1, 128 // 4) + 1, jnp.int32)
        _lenS2 = 128 - jax.random.randint(jax.random.fold_in(_rk, 8), (32,), 0, max(1, 128 // 4) + 1, jnp.int32)
        _ctx_1024P = jax.random.normal(jax.random.fold_in(_rk, 11), (32, 16, 128), jnp.float32)
        _ctx_1024c = jax.random.dirichlet(jax.random.fold_in(_rk, 511), 0.3 * jnp.ones((16,), jnp.float32), (32, 128))
        _ctx_1024t = jnp.einsum('bsk,bkd->bsd', _ctx_1024c, _ctx_1024P)
        _ctx_1024t = _ctx_1024t * jax.lax.rsqrt(jnp.mean(jnp.square(_ctx_1024t)) + 1e-12) * 0.953939
        ctx_1024 = 4.13588e-05 + 0.999923 * (_ctx_1024t + 0.3 * jax.random.normal(jax.random.fold_in(_rk, 611), (32, 128, 128), jnp.float32))
        _g = jax.random.normal(jax.random.fold_in(_rk, 9001), (2, 4), jnp.float32)
        _g = jnp.sign(_g) * jnp.maximum(jnp.abs(_g), 1.0) + (_g == 0) * 1.0
        g_xattn = _g[0]
        g_ffn = _g[1]
        return (x, ctx_1024, g_xattn, g_ffn)
    x, ctx_1024, g_xattn, g_ffn = _rec_inputs()

    def _L0_xattn_setup():
        import jax, jax.numpy as jnp
        import numpy as np
        import math
        N_HEADS = 16
        N_HIDDEN = 128
        N_EMBD = 128
        GROUP = 4
        D_HEAD = N_HIDDEN // N_HEADS
        B, T, V = (2, 512, 512)
        key = jax.random.key(seed)
        ks = jax.random.split(key, 10)
        s = 0.02
        return {'x': jax.random.normal(ks[0], (B, T, N_HIDDEN), jnp.float32), 'adj': jax.random.normal(ks[1], (B, V, N_EMBD), jnp.float32), 'Wq': jax.random.normal(ks[2], (N_HIDDEN, N_HIDDEN), jnp.float32) * s, 'bq': jnp.zeros((N_HIDDEN,), jnp.float32), 'Wk': jax.random.normal(ks[3], (N_EMBD, GROUP * D_HEAD), jnp.float32) * s, 'bk': jnp.zeros((GROUP * D_HEAD,), jnp.float32), 'Wv': jax.random.normal(ks[4], (N_EMBD, GROUP * D_HEAD), jnp.float32) * s, 'bv': jnp.zeros((GROUP * D_HEAD,), jnp.float32), 'Wo': jax.random.normal(ks[5], (N_HIDDEN, N_HIDDEN), jnp.float32) * s, 'bo': jnp.zeros((N_HIDDEN,), jnp.float32)}
    _L0_xattn_all = _L0_xattn_setup()
    _L0_xattn_in = {k: v for k, v in _L0_xattn_all.items() if k in ('Wq', 'bq', 'Wk', 'bk', 'Wv', 'bv', 'Wo', 'bo')}
    del _L0_xattn_all

    def _L0_ffn_setup():
        import jax, jax.numpy as jnp
        import numpy as np
        from jax import lax
        H = 128
        E = 8
        E_MLP = E - 4
        TOP_K = 2
        I = 64
        KC = 4
        SHARED_SCALE = 1.0
        key = jax.random.key(seed)
        ks = jax.random.split(key, 8)
        B, S = (4, 512)
        s_h = 1.0 / np.sqrt(H)
        s_i = 1.0 / np.sqrt(I)
        return {'hidden_states': jax.random.normal(ks[0], (B, S, H), dtype=jnp.float32), 'Wr': jax.random.normal(ks[1], (H, E), dtype=jnp.float32) * s_h, 'router_bias': jnp.zeros((E,), dtype=jnp.float32), 'Wg': jax.random.normal(ks[2], (E_MLP, H, I), dtype=jnp.float32) * s_h, 'Wu': jax.random.normal(ks[3], (E_MLP, H, I), dtype=jnp.float32) * s_h, 'Wd': jax.random.normal(ks[4], (E_MLP, I, H), dtype=jnp.float32) * s_i, 'conv_w': jax.random.normal(ks[5], (KC, 1, H), dtype=jnp.float32) * (1.0 / np.sqrt(KC)), 'conv_b': jnp.zeros((H,), dtype=jnp.float32)}
    _L0_ffn_all = _L0_ffn_setup()
    _L0_ffn_in = {k: v for k, v in _L0_ffn_all.items() if k in ('Wr', 'router_bias', 'Wg', 'Wu', 'Wd', 'conv_w', 'conv_b')}
    del _L0_ffn_all

    def _L1_xattn_setup():
        import jax, jax.numpy as jnp
        import numpy as np
        SEQD, EMBD, HEAD = (256, 128, 128)
        BATCH = 4
        key = jax.random.key(seed)
        ks = jax.random.split(key, 6)
        q = jax.random.normal(ks[0], (BATCH, SEQD, EMBD), dtype=jnp.float32)
        k = jax.random.normal(ks[1], (BATCH, SEQD, EMBD), dtype=jnp.float32)
        v = jax.random.normal(ks[2], (BATCH, SEQD, EMBD), dtype=jnp.float32)
        s = 1.0 / np.sqrt(EMBD)
        Wq = jax.random.uniform(ks[3], (HEAD, EMBD), jnp.float32, -s, s)
        Wk = jax.random.uniform(ks[4], (HEAD, EMBD), jnp.float32, -s, s)
        Wv = jax.random.uniform(ks[5], (HEAD, EMBD), jnp.float32, -s, s)
        return {'q': q, 'k': k, 'v': v, 'Wq': Wq, 'Wk': Wk, 'Wv': Wv}
    _L1_xattn_all = _L1_xattn_setup()
    _L1_xattn_in = {k: v for k, v in _L1_xattn_all.items() if k in ('Wq', 'Wk', 'Wv')}
    del _L1_xattn_all

    def _L1_ffn_setup():
        import jax, jax.numpy as jnp
        import numpy as np
        B, S, D_MODEL, D_HIDDEN = (4, 256, 128, 512)

        def act_quant(x):
            scale = 127.0 / jnp.clip(jnp.max(jnp.abs(x), axis=-1, keepdims=True), 1e-05)
            return jnp.clip(jnp.round(x * scale), -128, 127) / scale

        def weight_quant(w):
            scale = 1.0 / jnp.clip(jnp.mean(jnp.abs(w)), 1e-05)
            return jnp.clip(jnp.round(w * scale), -1, 1) / scale

        def bit_linear(x, w):
            xq = x + jax.lax.stop_gradient(act_quant(x) - x)
            wq = w + jax.lax.stop_gradient(weight_quant(w) - w)
            return jnp.einsum('bsd,hd->bsh', xq, wq)

        def depthwise_conv1d(x_bcl, w, b):
            y = jax.lax.conv_general_dilated(x_bcl, w, window_strides=(1,), padding=[(1, 1)], dimension_numbers=('NCH', 'OIH', 'NCH'), feature_group_count=x_bcl.shape[1])
            return y + b[None, :, None]
        key = jax.random.key(seed)
        ks = jax.random.split(key, 5)
        lim1 = 1.0 / np.sqrt(D_MODEL)
        lim2 = 1.0 / np.sqrt(D_HIDDEN)
        limc = 1.0 / np.sqrt(3.0)
        return {'x': jax.random.normal(ks[0], (B, S, D_MODEL), dtype=jnp.float32), 'w1': jax.random.uniform(ks[1], (D_HIDDEN, D_MODEL), jnp.float32, -lim1, lim1), 'conv_w': jax.random.uniform(ks[2], (D_HIDDEN, 1, 3), jnp.float32, -limc, limc), 'conv_b': jax.random.uniform(ks[3], (D_HIDDEN,), jnp.float32, -limc, limc), 'w2': jax.random.uniform(ks[4], (D_MODEL, D_HIDDEN), jnp.float32, -lim2, lim2)}
    _L1_ffn_all = _L1_ffn_setup()
    _L1_ffn_in = {k: v for k, v in _L1_ffn_all.items() if k in ('w1', 'conv_w', 'conv_b', 'w2')}
    del _L1_ffn_all

    def _L2_xattn_setup():
        import jax, jax.numpy as jnp
        import numpy as np
        EMBED_DIM = 128
        N, L = (4, 512)
        key = jax.random.key(seed)
        ks = jax.random.split(key, 9)
        s = 1.0 / np.sqrt(EMBED_DIM)
        return {'q': jax.random.normal(ks[0], (N, L, EMBED_DIM), jnp.float32), 'k': jax.random.normal(ks[1], (N, L, EMBED_DIM), jnp.float32), 'v': jax.random.normal(ks[2], (N, L, EMBED_DIM), jnp.float32), 'Wq': jax.random.normal(ks[3], (EMBED_DIM, EMBED_DIM), jnp.float32) * s, 'bq': jax.random.normal(ks[4], (EMBED_DIM,), jnp.float32) * s, 'Wk': jax.random.normal(ks[5], (EMBED_DIM, EMBED_DIM), jnp.float32) * s, 'bk': jax.random.normal(ks[6], (EMBED_DIM,), jnp.float32) * s, 'Wv': jax.random.normal(ks[7], (EMBED_DIM, EMBED_DIM), jnp.float32) * s, 'bv': jax.random.normal(ks[8], (EMBED_DIM,), jnp.float32) * s}
    _L2_xattn_all = _L2_xattn_setup()
    _L2_xattn_in = {k: v for k, v in _L2_xattn_all.items() if k in ('Wq', 'bq', 'Wk', 'bk', 'Wv', 'bv')}
    del _L2_xattn_all

    def _L2_ffn_setup():
        import jax, jax.numpy as jnp
        import numpy as np
        B, S, D, E = (4, 512, 128, 8)
        key = jax.random.key(seed)
        k1, k2, k3, k4, k5 = jax.random.split(key, 5)
        scale = 1.0 / np.sqrt(D)
        return {'x': jax.random.normal(k1, (B, S, D), dtype=jnp.float32), 'Wg': jax.random.normal(k2, (D, D), dtype=jnp.float32) * scale, 'bg': jnp.zeros((D,), dtype=jnp.float32), 'We': jax.random.normal(k3, (E, D, D), dtype=jnp.float32) * scale, 'be': jnp.zeros((E, D), dtype=jnp.float32)}
    _L2_ffn_all = _L2_ffn_setup()
    _L2_ffn_in = {k: v for k, v in _L2_ffn_all.items() if k in ('Wg', 'bg', 'We', 'be')}
    del _L2_ffn_all

    def _L3_xattn_setup():
        import jax, jax.numpy as jnp
        import numpy as np
        DIM = 128
        NUM_HEADS = 16
        DIM_HEAD = 64
        INNER = NUM_HEADS * DIM_HEAD
        SCALE = DIM_HEAD ** (-0.5)

        def _layernorm(x, gamma, beta, eps=1e-05):
            mu = jnp.mean(x, axis=-1, keepdims=True)
            var = jnp.mean(jnp.square(x - mu), axis=-1, keepdims=True)
            return (x - mu) * jax.lax.rsqrt(var + eps) * gamma + beta
        key = jax.random.key(seed)
        ks = jax.random.split(key, 8)
        B, SQ, SK = (2, 256, 512)
        x = jax.random.normal(ks[0], (B, SQ, DIM), dtype=jnp.float32)
        context = jax.random.normal(ks[1], (B, SK, DIM), dtype=jnp.float32)
        ln_gamma = jnp.ones((DIM,), jnp.float32)
        ln_beta = jnp.zeros((DIM,), jnp.float32)
        w_q = jax.random.normal(ks[2], (DIM, INNER), dtype=jnp.float32) / np.sqrt(DIM)
        w_kv = jax.random.normal(ks[3], (DIM, 2 * INNER), dtype=jnp.float32) / np.sqrt(DIM)
        w_out = jax.random.normal(ks[4], (INNER, DIM), dtype=jnp.float32) / np.sqrt(INNER)
        b_out = jnp.zeros((DIM,), jnp.float32)
        gate = jnp.array([0.5], jnp.float32)
        return {'x': x, 'context': context, 'ln_gamma': ln_gamma, 'ln_beta': ln_beta, 'w_q': w_q, 'w_kv': w_kv, 'w_out': w_out, 'b_out': b_out, 'gate': gate}
    _L3_xattn_all = _L3_xattn_setup()
    _L3_xattn_in = {k: v for k, v in _L3_xattn_all.items() if k in ('ln_gamma', 'ln_beta', 'w_q', 'w_kv', 'w_out', 'b_out', 'gate')}
    del _L3_xattn_all

    def _L3_ffn_setup():
        import jax, jax.numpy as jnp
        import numpy as np
        B, L, D = (4, 64, 128)
        E, TOP_K = (16, 4)
        F = 4 * D
        key = jax.random.key(seed)
        ks = jax.random.split(key, 6)
        scale = 0.02
        return {'x': jax.random.normal(ks[0], (B, L, D), jnp.float32), 'keys': jax.random.normal(ks[1], (E, D), jnp.float32), 'w1': jax.random.normal(ks[2], (E, F, D), jnp.float32) * scale, 'b1': jnp.zeros((E, F), jnp.float32), 'w2': jax.random.normal(ks[3], (E, D, F), jnp.float32) * scale, 'b2': jnp.zeros((E, D), jnp.float32), 'rw': jax.random.normal(ks[4], (E, D), jnp.float32) * scale, 'rb': jnp.zeros((E,), jnp.float32)}
    _L3_ffn_all = _L3_ffn_setup()
    _L3_ffn_in = {k: v for k, v in _L3_ffn_all.items() if k in ('keys', 'w1', 'b1', 'w2', 'b2', 'rw', 'rb')}
    del _L3_ffn_all
    return {'x': x, 'ctx_1024': ctx_1024, 'g_xattn': g_xattn, 'g_ffn': g_ffn, 'L0_xattn_Wq': _L0_xattn_in['Wq'], 'L0_xattn_bq': _L0_xattn_in['bq'], 'L0_xattn_Wk': _L0_xattn_in['Wk'], 'L0_xattn_bk': _L0_xattn_in['bk'], 'L0_xattn_Wv': _L0_xattn_in['Wv'], 'L0_xattn_bv': _L0_xattn_in['bv'], 'L0_xattn_Wo': _L0_xattn_in['Wo'], 'L0_xattn_bo': _L0_xattn_in['bo'], 'L0_ffn_Wr': _L0_ffn_in['Wr'], 'L0_ffn_router_bias': _L0_ffn_in['router_bias'], 'L0_ffn_Wg': _L0_ffn_in['Wg'], 'L0_ffn_Wu': _L0_ffn_in['Wu'], 'L0_ffn_Wd': _L0_ffn_in['Wd'], 'L0_ffn_conv_w': _L0_ffn_in['conv_w'], 'L0_ffn_conv_b': _L0_ffn_in['conv_b'], 'L1_xattn_Wq': _L1_xattn_in['Wq'], 'L1_xattn_Wk': _L1_xattn_in['Wk'], 'L1_xattn_Wv': _L1_xattn_in['Wv'], 'L1_ffn_w1': _L1_ffn_in['w1'], 'L1_ffn_conv_w': _L1_ffn_in['conv_w'], 'L1_ffn_conv_b': _L1_ffn_in['conv_b'], 'L1_ffn_w2': _L1_ffn_in['w2'], 'L2_xattn_Wq': _L2_xattn_in['Wq'], 'L2_xattn_bq': _L2_xattn_in['bq'], 'L2_xattn_Wk': _L2_xattn_in['Wk'], 'L2_xattn_bk': _L2_xattn_in['bk'], 'L2_xattn_Wv': _L2_xattn_in['Wv'], 'L2_xattn_bv': _L2_xattn_in['bv'], 'L2_ffn_Wg': _L2_ffn_in['Wg'], 'L2_ffn_bg': _L2_ffn_in['bg'], 'L2_ffn_We': _L2_ffn_in['We'], 'L2_ffn_be': _L2_ffn_in['be'], 'L3_xattn_ln_gamma': _L3_xattn_in['ln_gamma'], 'L3_xattn_ln_beta': _L3_xattn_in['ln_beta'], 'L3_xattn_w_q': _L3_xattn_in['w_q'], 'L3_xattn_w_kv': _L3_xattn_in['w_kv'], 'L3_xattn_w_out': _L3_xattn_in['w_out'], 'L3_xattn_b_out': _L3_xattn_in['b_out'], 'L3_xattn_gate': _L3_xattn_in['gate'], 'L3_ffn_keys': _L3_ffn_in['keys'], 'L3_ffn_w1': _L3_ffn_in['w1'], 'L3_ffn_b1': _L3_ffn_in['b1'], 'L3_ffn_w2': _L3_ffn_in['w2'], 'L3_ffn_b2': _L3_ffn_in['b2'], 'L3_ffn_rw': _L3_ffn_in['rw'], 'L3_ffn_rb': _L3_ffn_in['rb']}

def reference(x, ctx_1024, g_xattn, g_ffn, L0_xattn_Wq, L0_xattn_bq, L0_xattn_Wk, L0_xattn_bk, L0_xattn_Wv, L0_xattn_bv, L0_xattn_Wo, L0_xattn_bo, L0_ffn_Wr, L0_ffn_router_bias, L0_ffn_Wg, L0_ffn_Wu, L0_ffn_Wd, L0_ffn_conv_w, L0_ffn_conv_b, L1_xattn_Wq, L1_xattn_Wk, L1_xattn_Wv, L1_ffn_w1, L1_ffn_conv_w, L1_ffn_conv_b, L1_ffn_w2, L2_xattn_Wq, L2_xattn_bq, L2_xattn_Wk, L2_xattn_bk, L2_xattn_Wv, L2_xattn_bv, L2_ffn_Wg, L2_ffn_bg, L2_ffn_We, L2_ffn_be, L3_xattn_ln_gamma, L3_xattn_ln_beta, L3_xattn_w_q, L3_xattn_w_kv, L3_xattn_w_out, L3_xattn_b_out, L3_xattn_gate, L3_ffn_keys, L3_ffn_w1, L3_ffn_b1, L3_ffn_w2, L3_ffn_b2, L3_ffn_rw, L3_ffn_rb):
    import jax
    import jax.numpy as jnp

    def _L0_xattn_ref(x, adj, Wq, bq, Wk, bk, Wv, bv, Wo, bo):
        import jax, jax.numpy as jnp
        import numpy as np
        import math
        N_HEADS = 16
        N_HIDDEN = 128
        N_EMBD = 128
        GROUP = 4
        D_HEAD = N_HIDDEN // N_HEADS
        B, T, V = (2, 512, 512)
        b, t, _ = x.shape
        v_len = adj.shape[1]
        q = x @ Wq + bq
        k = adj @ Wk + bk
        v = adj @ Wv + bv
        q = q.reshape(b, t, N_HEADS, D_HEAD).transpose(0, 2, 1, 3)
        k = k.reshape(b, v_len, GROUP, D_HEAD).transpose(0, 2, 1, 3)
        v = v.reshape(b, v_len, GROUP, D_HEAD).transpose(0, 2, 1, 3)
        weight = jnp.einsum('bhtd,bgvd->bhtv', q, k) / math.sqrt(D_HEAD)
        weight = jax.nn.softmax(weight, axis=-1)
        out = jnp.einsum('bhtv,bgvd->bhtd', weight, v)
        out = out.transpose(0, 2, 1, 3).reshape(b, t, N_HIDDEN)
        return out @ Wo + bo

    def _L0_ffn_ref(hidden_states, Wr, router_bias, Wg, Wu, Wd, conv_w, conv_b):
        import jax, jax.numpy as jnp
        import numpy as np
        from jax import lax
        H = 128
        E = 8
        E_MLP = E - 4
        TOP_K = 2
        I = 64
        KC = 4
        SHARED_SCALE = 1.0
        B, S, Hd = hidden_states.shape
        T = B * S
        x = hidden_states.reshape(T, Hd)
        scores = jax.nn.sigmoid(x @ Wr)
        _, idx = lax.top_k(scores + router_bias, TOP_K)
        w = jnp.take_along_axis(scores, idx, axis=-1)
        w = w / (jnp.sum(w, axis=-1, keepdims=True) + 1e-09)
        cw = jnp.zeros((T, E), dtype=x.dtype).at[jnp.arange(T)[:, None], idx].add(w)
        g = jnp.einsum('th,ehi->tei', x, Wg)
        u = jnp.einsum('th,ehi->tei', x, Wu)
        hid = jax.nn.silu(g) * u
        mlp_out = jnp.einsum('tei,eih->teh', hid, Wd)
        routed = jnp.einsum('te,teh->th', cw[:, :E_MLP], mlp_out)
        routed = routed + cw[:, E_MLP:E_MLP + 1] * x
        routed = routed + cw[:, E_MLP + 2:E_MLP + 3] * x
        routed = routed + cw[:, E_MLP + 3:E_MLP + 4] * jax.nn.relu(x)
        routed = routed.reshape(B, S, Hd)
        shared = lax.conv_general_dilated(hidden_states, conv_w, window_strides=(1,), padding=[(KC - 1, 0)], dimension_numbers=('NHC', 'HIO', 'NHC'), feature_group_count=Hd) + conv_b
        return routed + SHARED_SCALE * shared

    def _L1_xattn_ref(q, k, v, Wq, Wk, Wv):
        import jax, jax.numpy as jnp
        import numpy as np
        SEQD, EMBD, HEAD = (256, 128, 128)
        BATCH = 4
        seqd = q.shape[1]
        qh = jnp.einsum('bse,he->bsh', q, Wq)
        kh = jnp.einsum('bse,he->bsh', k, Wk)
        vh = jnp.einsum('bse,he->bsh', v, Wv)
        scores = jnp.einsum('bqh,bkh->bqk', qh, kh) / jnp.sqrt(jnp.float32(HEAD))
        causal = jnp.tril(jnp.ones((seqd, seqd), dtype=bool))
        scores = jnp.where(causal, scores, -jnp.inf)
        probs = jax.nn.softmax(scores, axis=1)
        return jnp.einsum('bqk,bkh->bqh', probs, vh)

    def _L1_ffn_ref(x, w1, conv_w, conv_b, w2):
        import jax, jax.numpy as jnp
        import numpy as np
        B, S, D_MODEL, D_HIDDEN = (4, 256, 128, 512)

        def act_quant(x):
            scale = 127.0 / jnp.clip(jnp.max(jnp.abs(x), axis=-1, keepdims=True), 1e-05)
            return jnp.clip(jnp.round(x * scale), -128, 127) / scale

        def weight_quant(w):
            scale = 1.0 / jnp.clip(jnp.mean(jnp.abs(w)), 1e-05)
            return jnp.clip(jnp.round(w * scale), -1, 1) / scale

        def bit_linear(x, w):
            xq = x + jax.lax.stop_gradient(act_quant(x) - x)
            wq = w + jax.lax.stop_gradient(weight_quant(w) - w)
            return jnp.einsum('bsd,hd->bsh', xq, wq)

        def depthwise_conv1d(x_bcl, w, b):
            y = jax.lax.conv_general_dilated(x_bcl, w, window_strides=(1,), padding=[(1, 1)], dimension_numbers=('NCH', 'OIH', 'NCH'), feature_group_count=x_bcl.shape[1])
            return y + b[None, :, None]
        h = bit_linear(x, w1)
        h = depthwise_conv1d(h.transpose(0, 2, 1), conv_w, conv_b)
        h = h.transpose(0, 2, 1)
        h = jax.nn.silu(h)
        return bit_linear(h, w2)

    def _L2_xattn_ref(q, k, v, Wq, bq, Wk, bk, Wv, bv):
        import jax, jax.numpy as jnp
        import numpy as np
        EMBED_DIM = 128
        N, L = (4, 512)
        scale = 1.0 / q.shape[-1] ** 0.5
        pq = jnp.einsum('nle,fe->nlf', q, Wq) + bq
        pk = jnp.einsum('nle,fe->nlf', k, Wk) + bk
        pv = jnp.einsum('nle,fe->nlf', v, Wv) + bv
        scores = jnp.einsum('nle,nme->nlm', pq, pk) * scale
        attn = jax.nn.softmax(scores, axis=-1)
        return jnp.einsum('nlm,nme->nle', attn, pv)

    def _L2_ffn_ref(x, Wg, bg, We, be):
        import jax, jax.numpy as jnp
        import numpy as np
        B, S, D, E = (4, 512, 128, 8)
        probs = jax.nn.softmax(x @ Wg + bg, axis=-1)
        idx = jnp.argmax(probs, axis=-1)
        p = jnp.take_along_axis(probs, idx[..., None], axis=-1)[..., 0]
        e_idx = idx % We.shape[0]
        h = jax.nn.relu(jnp.einsum('bsd,edf->besf', x, We) + be[None, :, None, :])
        onehot = jax.nn.one_hot(e_idx, We.shape[0], dtype=x.dtype)
        out = jnp.einsum('besf,bse->bsf', h, onehot) * p[..., None]
        return out

    def _L3_xattn_ref(x, context, ln_gamma, ln_beta, w_q, w_kv, w_out, b_out, gate):
        import jax, jax.numpy as jnp
        import numpy as np
        DIM = 128
        NUM_HEADS = 16
        DIM_HEAD = 64
        INNER = NUM_HEADS * DIM_HEAD
        SCALE = DIM_HEAD ** (-0.5)

        def _layernorm(x, gamma, beta, eps=1e-05):
            mu = jnp.mean(x, axis=-1, keepdims=True)
            var = jnp.mean(jnp.square(x - mu), axis=-1, keepdims=True)
            return (x - mu) * jax.lax.rsqrt(var + eps) * gamma + beta
        B, SQ, _ = x.shape
        SK = context.shape[1]
        xn = _layernorm(x, ln_gamma, ln_beta)
        q = (xn @ w_q).reshape(B, SQ, NUM_HEADS, DIM_HEAD)
        kv = context @ w_kv
        k, v = jnp.split(kv, 2, axis=-1)
        k = k.reshape(B, SK, NUM_HEADS, DIM_HEAD)
        v = v.reshape(B, SK, NUM_HEADS, DIM_HEAD)
        scores = jnp.einsum('bqhd,bkhd->bhqk', q * SCALE, k)
        attn = jax.nn.softmax(scores, axis=-1)
        out = jnp.einsum('bhqk,bkhd->bqhd', attn, v).reshape(B, SQ, INNER)
        out = out @ w_out + b_out
        return out * jnp.tanh(gate[0])

    def _L3_ffn_ref(x, keys, w1, b1, w2, b2, rw, rb):
        import jax, jax.numpy as jnp
        import numpy as np
        B, L, D = (4, 64, 128)
        E, TOP_K = (16, 4)
        F = 4 * D
        diff = x[:, :, None, :] - keys
        dist2 = jnp.sum(diff * diff, axis=-1)
        logits = -dist2 + jnp.einsum('bld,ed->ble', x, rw) + rb
        topv, topi = jax.lax.top_k(logits, TOP_K)
        w = jax.nn.softmax(topv, axis=-1)
        hidden = jax.nn.gelu(jnp.einsum('bld,efd->blef', x, w1) + b1, approximate=False)
        exp_out = jnp.einsum('blef,edf->bled', hidden, w2) + b2
        sel = jnp.take_along_axis(exp_out, topi[..., None], axis=2)
        fused = jnp.sum(w[..., None] * sel, axis=2)
        return fused
    x = x + jnp.tanh(g_xattn[0]) * _L0_xattn_ref(_layernorm(x, axis=-1), ctx_1024, L0_xattn_Wq, L0_xattn_bq, L0_xattn_Wk, L0_xattn_bk, L0_xattn_Wv, L0_xattn_bv, L0_xattn_Wo, L0_xattn_bo)
    x = x + jnp.tanh(g_ffn[0]) * _L0_ffn_ref(_layernorm(x, axis=-1), L0_ffn_Wr, L0_ffn_router_bias, L0_ffn_Wg, L0_ffn_Wu, L0_ffn_Wd, L0_ffn_conv_w, L0_ffn_conv_b)
    x = x + jnp.tanh(g_xattn[1]) * _L1_xattn_ref(_layernorm(x, axis=-1), ctx_1024, ctx_1024, L1_xattn_Wq, L1_xattn_Wk, L1_xattn_Wv)
    x = x + jnp.tanh(g_ffn[1]) * _L1_ffn_ref(_layernorm(x, axis=-1), L1_ffn_w1, L1_ffn_conv_w, L1_ffn_conv_b, L1_ffn_w2)
    x = x + jnp.tanh(g_xattn[2]) * _L2_xattn_ref(_layernorm(x, axis=-1), ctx_1024, ctx_1024, L2_xattn_Wq, L2_xattn_bq, L2_xattn_Wk, L2_xattn_bk, L2_xattn_Wv, L2_xattn_bv)
    x = x + jnp.tanh(g_ffn[2]) * _L2_ffn_ref(_layernorm(x, axis=-1), L2_ffn_Wg, L2_ffn_bg, L2_ffn_We, L2_ffn_be)
    x = x + jnp.tanh(g_xattn[3]) * _L3_xattn_ref(_layernorm(x, axis=-1), ctx_1024, L3_xattn_ln_gamma, L3_xattn_ln_beta, L3_xattn_w_q, L3_xattn_w_kv, L3_xattn_w_out, L3_xattn_b_out, L3_xattn_gate)
    x = x + jnp.tanh(g_ffn[3]) * _L3_ffn_ref(_layernorm(x, axis=-1), L3_ffn_keys, L3_ffn_w1, L3_ffn_b1, L3_ffn_w2, L3_ffn_b2, L3_ffn_rw, L3_ffn_rb)
    return x

_drawn_inputs = setup_inputs


def setup_inputs(seed=0):
    import zlib

    import numpy as np

    out = dict(_drawn_inputs(seed))
    spreads = {'L0_xattn_bq': (0.0, 0.703),
     'L0_xattn_bk': (0.0, 2.0),
     'L0_xattn_bv': (0.0, 0.1),
     'L0_xattn_bo': (0.0, 0.1),
     'L0_ffn_router_bias': (0.0, 0.1),
     'L0_ffn_conv_b': (0.0, 0.1),
     'L2_ffn_bg': (0.0, 0.766),
     'L2_ffn_be': (0.0, 0.8),
     'L3_xattn_ln_gamma': (1.0, 0.6),
     'L3_xattn_ln_beta': (0.0, 0.8),
     'L3_xattn_b_out': (0.0, 0.295),
     'L3_ffn_b1': (0.0, 0.523),
     'L3_ffn_b2': (0.0, 0.1),
     'L3_ffn_rb': (0.0, 2.0)}
    factors = {'g_ffn': 8.0,
     'L0_xattn_Wq': 7.637,
     'L0_xattn_Wk': 7.6,
     'L2_xattn_bq': 4.765,
     'L2_xattn_bk': 64.0,
     'L3_ffn_rw': 8.0}
    for name, (base, spread) in spreads.items():
        noise = np.random.default_rng([zlib.crc32(name.encode()), seed]).standard_normal(out[name].shape)
        drawn = base * np.exp(spread * noise) if base else spread * noise
        out[name] = jnp.asarray(drawn.astype(out[name].dtype))
    for name, factor in factors.items():
        out[name] = (out[name] * factor).astype(out[name].dtype)
    return out
```

```python
from contextlib import ExitStack

import concourse.bass as bass
from concourse import mybir

F32 = mybir.dt.float32
BF16 = mybir.dt.bfloat16
U32 = mybir.dt.uint32
ACT = mybir.ActivationFunctionType
ALU = mybir.AluOpType
AX = mybir.AxisListType.X

P = 128
B = 32
CB = 4
NC = B // CB
W = CB * P
HEADS = 16
D0 = P // HEADS
D3 = 64
VW0 = P + HEADS
VROW = P + HEADS * (VW0 + 1)
QUARTERS = 4
HQ = HEADS // QUARTERS
UNITS = CB * QUARTERS
STEPS = UNITS + 5
E0, I0 = 4, 64
R0 = 8
H1 = 512
K1 = H1 // P
E2 = 8
E3, H3, TOP3 = 16, 512, 4
K3 = H3 // P
EPS = 1e-5
ROUND = 1.5 * 2.0 ** 23
MASKED = -1e30
CRED = QUARTERS + 1


class Steps:

    def __init__(self, eng, sem):
        self.eng, self.sem, self.base, self.off, self.k, self.at = eng, sem, 0, 0, 0, None

    def loop(self, per):
        self.base, self.off, self.per = self.base + self.k, 0, per
        self.k = 0

    def turn(self, i):
        assert self.k in (0, self.per), self.k
        self.off, self.k = self.per * i, 0

    def end(self, n):
        assert self.k == self.per, self.k
        self.base, self.off, self.k = self.base + self.per * n, 0, 0

    def __call__(self, ins):
        self.k += 1
        ins.then_inc(self.sem, 1)
        self.eng.wait_ge(self.sem, self.off + (self.base + self.k))

    def held(self, ins, mark):
        self(ins)
        self.eng.sem_inc(mark, 1)


def slices_at(u, kA):
    if kA <= 5:
        return [u - 4] if 4 <= u < 4 + kA else []
    first = 4
    lo = (u - first) * kA // (STEPS - first) if u >= first else 0
    hi = (u - first + 1) * kA // (STEPS - first) if u >= first else 0
    return list(range(lo, hi))


def flamingo(nc, a, out):
    ctx = ExitStack()
    with ctx:
        def sb(name, shape, dt=F32):
            return ctx.enter_context(nc.sbuf_tensor(name, shape, dt))

        sems = {}

        def sem(name):
            if name not in sems:
                sems[name] = ctx.enter_context(nc.semaphore(name))
            return sems[name]

        bank = [ctx.enter_context(nc.psum_tensor(f"bank{i}", [P, W], F32)) for i in range(8)]

        def b4(i):
            return bank[i][:, :].rearrange("p (j t) -> p j t", j=CB)

        x = sb("x", [P, B, P])
        ident = sb("ident", [P, P])
        ident16 = sb("ident16", [P, P], BF16)
        ones = sb("ones", [P, P])
        iota8 = sb("iota8", [P, E3])
        gates = sb("gates", [P, 9])
        gate3 = sb("gate3", [P, 1])
        graw = sb("graw", [P, 9])

        stats = sb("stats", [P, CB, 6])
        mv = sb("mv", [P, CB, 2])
        ve = sb("ve", [P, CB])
        mhalf = sb("mhalf", [P, CB])
        rstd = sb("rstd", [P, CB])
        xn = sb("xn", [P, CB, P])
        xnT = sb("xnT", [P, W])
        cx = sb("cx", [P, CB, P])
        cxT = sb("cxT", [P, 2, W])
        sm = sb("sm", [P, 2, CB, P])
        pr = sb("pr", [P, 2, CB, P])
        pT = sb("pT", [P, 2, CB, P])
        nm = sb("nm", [P, 2, CB])
        sums = sb("sums", [P, CB])
        rs = sb("rs", [P, HEADS])
        tmp = sb("tmp", [P, CB, P])
        tmp2 = sb("tmp2", [P, CB, P])

        arena = sb("arena", [P, 28800])
        used = [0]

        def fresh():
            used[0] = 0

        def ar(shape, dt=F32):
            n = 1
            for s in shape[1:]:
                n *= s
            words = n if dt != BF16 else (n + 1) // 2
            v = arena[0:shape[0], used[0]:used[0] + words]
            used[0] += words
            assert used[0] <= 28800
            v = v if dt == F32 else v.bitcast(dt)
            if len(shape) == 3:
                v = v.rearrange("p (a b) -> p a b", a=shape[1])
            if len(shape) == 4:
                v = v.rearrange("p (a b c) -> p a b c", a=shape[1], b=shape[2])
            return v

        wq0, wkv0 = sb("wq0", [P, P]), sb("wkv0", [P, 2, 4 * D0])
        wkr0, wvs0 = sb("wkr0", [P, P]), sb("wvs0", [P, D0])
        wo0, bo0 = sb("wo0", [P, P]), sb("bo0", [P, P])
        bq0, bk0g, bk0, bv0g, bv0 = sb("bq0", [P, 1]), sb("bk0g", [P, 4]), sb("bk0", [P, 1]), sb("bv0g", [P, 4 * D0]), sb("bv0", [P, D0])
        headmask = sb("headmask", [P, HEADS])
        wr0, rb0 = sb("wr0", [P, R0]), sb("rb0", [P, R0])
        wg0, wu0 = sb("wg0", [P, E0 * I0]), sb("wu0", [P, E0 * I0])
        wd0 = sb("wd0", [P, 2, 2 * P])
        cw0, cb0 = sb("cw0", [P, 4]), sb("cb0", [P, 1])
        wT1 = sb("wT1", [P, 3, P])
        causal = sb("causal", [P, P])
        w1q, w2q = sb("w1q", [P, H1], BF16), sb("w2q", [P, K1, P], BF16)
        wsc1, wsc2 = sb("wsc1", [P, 1]), sb("wsc2", [P, 1])
        cw1, cb1 = sb("cw1", [P, K1, 3]), sb("cb1", [P, K1])
        wT2 = sb("wT2", [P, 3, P])
        bq2, bk2, bv2 = sb("bq2", [P, 1]), sb("bk2", [P, 1]), sb("bv2", [P, P])
        wg2, bg2 = sb("wg2", [P, P]), sb("bg2", [P, P])
        we2, be2 = sb("we2", [P, E2 * P]), sb("be2", [E2, P])
        gam3, bet3 = sb("gam3", [P, 1]), sb("bet3", [P, 1])
        m3 = sb("m3", [P, HEADS, P])
        wv3, wo3, bo3 = sb("wv3", [P, HEADS * D3]), sb("wo3", [P, 8, P]), sb("bo3", [P, P])
        wr3, rb3 = sb("wr3", [P, E3]), sb("rb3", [P, E3])
        b13, b23 = sb("b13", [P, E3, K3]), sb("b23", [E3, P])

        fresh()
        raw1, raw2 = ar([P, 3, P]), ar([P, 3, P])
        w1n, w2n = ar([P, K1, P]), ar([P, H1])
        wabs = ar([P, 2, H1])
        wqkn3 = ar([P, 2, HEADS * D3])
        wqkT3 = ar([P, 2, 8, P])
        kr3 = ar([E3, 2, P])
        keyT = ar([P, 2, E3])
        keysq = ar([P, E3])
        part = ar([P, 2])

        fresh()
        qT0, kT0 = ar([P, 2, W]), ar([P, 2, W])
        v0 = ar([P, 2, CB * D0])
        kbd0 = ar([P, 2, HEADS, P])
        vpad0 = ar([P, 2, VROW])
        on0, oT0 = ar([P, 2, P]), ar([P, 2, P])
        fresh()
        xall0 = ar([P, B, P])
        sg0 = ar([P, 2, W])
        hid0 = ar([P, 2, W])
        conv0, ctap0 = ar([P, CB, P]), ar([P, CB, P])
        lg0, sel0 = ar([P, CB, R0]), ar([P, CB, R0])
        top0, idx0, idf0 = ar([P, CB, 8]), ar([P, CB, 8], U32), ar([P, CB, 8])
        oh0 = ar([P, 2, CB, R0])
        wsel0, wsum0 = ar([P, 2, CB]), ar([P, CB])
        cwt0 = ar([P, CB, R0])
        ccp0 = ar([P, CB])
        fresh()
        qT1, kT1 = ar([P, W]), ar([P, W])
        v1 = ar([P, CB, P])
        fresh()
        am1, sc1 = ar([P, CB]), ar([P, CB])
        xr1 = ar([P, CB, P])
        xq1 = ar([P, CB, P], BF16)
        xqT1 = ar([P, W], BF16)
        iscb1 = ar([P, CB, P])
        sbc1 = ar([P, W])
        hs1, hc1 = ar([P, 2, CB, P]), ar([P, 2, CB, P])
        h1 = ar([P, K1, W])
        am2, sc2, isc2 = ar([P, CB]), ar([P, CB]), ar([P, CB])
        hr1 = ar([P, 2, H1])
        hq1 = ar([P, CB, H1], BF16)
        hqT1 = ar([P, 2, K1 * P], BF16)
        fresh()
        lg2, top2, idx2, idf2 = ar([P, CB, P]), ar([P, CB, 8]), ar([P, CB, 8], U32), ar([P, CB])
        ex2, pg2, oh2 = ar([P, CB, P]), ar([P, CB]), ar([P, CB, E2])
        ohT2 = ar([E2, W])
        acc2 = ar([P, CB, P])
        fresh()
        g3 = ar([P, 2, HEADS, W])
        v3 = [ar([P, CB, HEADS, D3 + 1]) for _ in range(2)]
        on3 = ar([P, 2, HEADS * D3])
        oT3 = ar([P, 8, P])
        fresh()
        xall3 = ar([P, B * P])
        lgT3 = ar([E3, W])
        lg3 = ar([P, CB, E3])
        x23 = ar([P, CB])
        top3, idx3, idf3 = ar([P, CB, 8]), ar([P, CB, 8], U32), ar([P, CB, 8])
        ex3, es3, oh3 = ar([P, CB, TOP3]), ar([P, CB]), ar([P, CB, E3])
        wt3 = ar([P, B, E3])
        wtc3 = ar([P, CB, E3])
        wtT3 = ar([E3, W])
        w1n3, w2n3 = ar([P, 2, K3, P]), ar([P, 2, H3])
        w1T3, w2T3 = ar([P, 2, H3]), ar([P, 2, K3, P])
        h3 = ar([P, 2, K3, W])

        rows = lambda ap, n=P: ap.rearrange("(a n) -> a n", a=1)[0].partition_broadcast(n)
        col = lambda ap: ap.rearrange("(p a) -> p a", a=1)

        SETUP_LOADS = [
            (x[:, :, :], a["x"].rearrange("b t d -> t b d")),
            (graw[:, 0:4], rows(a["g_xattn"])), (graw[:, 4:8], rows(a["g_ffn"])), (graw[:, 8:9], rows(a["L3_xattn_gate"])),
            (wq0[:, :], a["L0_xattn_Wq"]), (wkv0[:, 0, :], a["L0_xattn_Wk"]), (wkv0[:, 1, :], a["L0_xattn_Wv"]),
            (wo0[:, :], a["L0_xattn_Wo"]), (bo0[:, :], rows(a["L0_xattn_bo"])), (bq0[:, :], col(a["L0_xattn_bq"])),
            (bv0g[:, :], rows(a["L0_xattn_bv"])),
            (wr0[:, :], a["L0_ffn_Wr"]), (rb0[:, :], rows(a["L0_ffn_router_bias"])),
            (wg0[:, :].rearrange("p (e i) -> p e i", e=E0), a["L0_ffn_Wg"].rearrange("e h i -> h e i")),
            (wu0[:, :].rearrange("p (e i) -> p e i", e=E0), a["L0_ffn_Wu"].rearrange("e h i -> h e i")),
            (cw0[:, :], a["L0_ffn_conv_w"].rearrange("k a h -> h (k a)")), (cb0[:, :], col(a["L0_ffn_conv_b"])),
            (raw1[:, 0, :], a["L1_xattn_Wq"]), (raw1[:, 1, :], a["L1_xattn_Wk"]), (raw1[:, 2, :], a["L1_xattn_Wv"]),
            (w1n[:, :, :], a["L1_ffn_w1"].rearrange("(k p) d -> p k d", p=P)), (w2n[:, :], a["L1_ffn_w2"]),
            (cw1[:, :, :], a["L1_ffn_conv_w"].rearrange("(k p) a t -> p k (a t)", p=P)),
            (cb1[:, :], a["L1_ffn_conv_b"].rearrange("(k p) -> p k", p=P)),
            (raw2[:, 0, :], a["L2_xattn_Wq"]), (raw2[:, 1, :], a["L2_xattn_Wk"]), (raw2[:, 2, :], a["L2_xattn_Wv"]),
            (bq2[:, :], col(a["L2_xattn_bq"])), (bk2[:, :], col(a["L2_xattn_bk"])), (bv2[:, :], rows(a["L2_xattn_bv"])),
            (wg2[:, :], a["L2_ffn_Wg"]), (bg2[:, :], rows(a["L2_ffn_bg"])),
            (we2[:, :].rearrange("p (e f) -> p e f", e=E2), a["L2_ffn_We"].rearrange("e d f -> d e f")), (be2[:, :], a["L2_ffn_be"]),
            (gam3[:, :], col(a["L3_xattn_ln_gamma"])), (bet3[:, :], col(a["L3_xattn_ln_beta"])),
            (wqkn3[:, 0, :], a["L3_xattn_w_q"]), (wqkn3[:, 1, :], a["L3_xattn_w_kv"][:, 0:HEADS * D3]),
            (wv3[:, :], a["L3_xattn_w_kv"][:, HEADS * D3:2 * HEADS * D3]),
            (wo3[:, :, :], a["L3_xattn_w_out"].rearrange("(k p) d -> p k d", p=P)), (bo3[:, :], rows(a["L3_xattn_b_out"])),
            (kr3[:, 0, :], a["L3_ffn_keys"]), (kr3[:, 1, :], a["L3_ffn_rw"]), (rb3[:, :], rows(a["L3_ffn_rb"])),
            (b13[:, :, :], a["L3_ffn_b1"].rearrange("e (k p) -> p e k", p=P)), (b23[:, :], a["L3_ffn_b2"]),
        ]
        WD = []
        for e in range(E0):
            pair, u = divmod(e, 2)
            WD.append((wd0[I0 * u:I0 * u + I0, pair, P * u:P * u + P], a["L0_ffn_Wd"][e]))

        s_load, s_wd, s_zero = sem("setup_loaded"), sem("wd0_loaded"), sem("wd0_zeroed")
        s_const = sem("constants_ready")
        s_xdone = sem("x_done")
        block = ctx.enter_context(nc.Block())

        def stage_start(eng, s):
            eng.wait_ge(s_xdone, NC * s + 1)

        ATT = ("A0", "A1", "A2", "A3")
        VAR0 = {"A0": 0, "F0": NC, "A1": 2 * NC, "F1": 3 * NC, "A2": 4 * NC, "F2": 5 * NC, "A3": 6 * NC, "F3": 8 * NC}
        XN0 = {"A0": 0, "F0": NC, "A1": 2 * NC, "A2": 3 * NC, "F2": 4 * NC, "A3": 5 * NC, "F3": 6 * NC}
        CX0 = {st: i * NC for i, st in enumerate(ATT)}
        s_var, s_rstd, s_xn = sem("variance"), sem("inverse_deviation"), sem("normalised")
        s_cx, s_cT = sem("context_loaded"), sem("context_transposed")
        STAGE = {n: i for i, n in enumerate(("A0", "F0", "A1", "F1", "A2", "F2", "A3", "F3"))}
        n_loads = len(SETUP_LOADS) + HEADS

        @block.sync
        def _(sp):
            with nc.allow_non_contiguous_dma(reason="small vectors laid along the partitions"):
                for dst, src in SETUP_LOADS:
                    sp.dma_start(dst, src).then_inc(s_load, 16)
                for h in range(HEADS):
                    sp.dma_start(bk0g[D0 * h:D0 * h + D0, :], a["L0_xattn_bk"].rearrange("(g d) -> d g", g=4)).then_inc(s_load, 16)
            sp.wait_ge(s_zero, 1)
            for dst, src in WD:
                sp.dma_start(dst, src).then_inc(s_wd, 16)
            cview = a["ctx_1024"].rearrange("b s e -> s b e")
            for st in ATT:
                if STAGE[st]:
                    stage_start(sp, STAGE[st])
                    sp.wait_ge(s_cT, CX0[st])
                sp.dma_start(cx[:, :, :], cview[:, 0:CB, :]).then_inc(s_cx, 16)
                with sp.Fori(1, NC) as c:
                    sp.wait_ge(s_cT, c + CX0[st])
                    sp.dma_start(cx[:, :, :], cview[:, bass.ds(c * CB, CB), :]).then_inc(s_cx, 16)
            stage_start(sp, STAGE["F3"])
            s_w, s_wT = [sem("F3_weights_loaded0"), sem("F3_weights_loaded1")], sem("F3_weights_transposed")

            def load_expert(e, p):
                sp.dma_start(w1n3[:, p, :, :], a["L3_ffn_w1"][e].rearrange("(k p) d -> p k d", p=P)).then_inc(s_w[p], 16)

            def load_expert2(e, p):
                sp.dma_start(w2n3[:, p, :], a["L3_ffn_w2"][e]).then_inc(s_w[p], 16)

            for p in range(2):
                load_expert(p, p)
                load_expert2(p, p)
            with sp.Fori(1, E3 // 2) as i:
                for p in range(2):
                    sp.wait_ge(s_wT, 4 * i + (2 * p - 2))
                    sp.dma_start(w1n3[:, p, :, :], a["L3_ffn_w1"][bass.ds(i * 2 + p, 1)].rearrange("e (k p) d -> p (e k) d", p=P)).then_inc(s_w[p], 16)
                    sp.dma_start(w2n3[:, p, :], a["L3_ffn_w2"][bass.ds(i * 2 + p, 1)].rearrange("e d f -> d (e f)")).then_inc(s_w[p], 16)
            s_y = sem("F3_outputs_added")
            s_out = sem("out_stored")
            sp.wait_ge(s_y, NC * (E3 + 1))
            for q in range(4):
                sp.dma_start(out[8 * q:8 * q + 8].rearrange("b t d -> t b d"), x[:, 8 * q:8 * q + 8, :]).then_inc(s_out, 16)
            sp.wait_ge(s_out, 64)

        @block.gpsimd
        def _(pl):
            step = Steps(pl, sem("pool_steps"))
            s_held = sem("pool_held")
            step(pl.memset(wd0[:, :, :], 0.0))
            pl.memset(rstd[:, :], 0.0).then_inc(s_zero, 1)
            step(pl.memset(ident[:, :], 0.0))
            step(pl.affine_select(out=ident[:, :], in_=ident[:, :], compare_op=ALU.not_equal, fill=1.0, base=0,
                                  pattern=[[-1, P]], channel_multiplier=1))
            pl.tensor_copy(ident16[:, :], ident[:, :])
            pl.memset(ones[:, :], 1.0)
            pl.memset(mhalf[:, :], -0.5)
            step(pl.memset(headmask[:, :], 1.0))
            step(pl.affine_select(out=headmask[:, :], in_=headmask[:, :], compare_op=ALU.is_ge, fill=0.0, base=0,
                                  pattern=[[-D0, HEADS]], channel_multiplier=1))
            step(pl.affine_select(out=headmask[:, :], in_=headmask[:, :], compare_op=ALU.is_ge, fill=0.0, base=D0 - 1,
                                  pattern=[[D0, HEADS]], channel_multiplier=-1))
            step(pl.memset(causal[:, :], 0.0))
            step(pl.affine_select(out=causal[:, :], in_=causal[:, :], compare_op=ALU.is_ge, fill=MASKED, base=0,
                                  pattern=[[1, P]], channel_multiplier=-1))
            pl.iota(iota8[:, :], pattern=[[1, E3]], base=0, channel_multiplier=0, allow_small_or_imprecise_dtypes=True).then_inc(s_const, 1)

            def power(st, n):
                pl.wait_ge(s_var, n + (1 + VAR0[st]))
                pl.tensor_tensor(rstd[:, :], ve[:, :], mhalf[:, :], ALU.pow).then_inc(s_rstd, 1)

            pl.wait_ge(sem("setup_done"), 1)
            step(pl.memset(vpad0[:, :, :], 0.0))
            for s in range(2):
                pl.memset(vpad0[:, s, P:P + HEADS * (VW0 + 1)].rearrange("p (h r) -> p h r", r=VW0 + 1)[:, :, 0:1], 1.0)
            power("A0", 0)

            def spread(c, p):
                for j in range(CB):
                    s = j % 2
                    if j == 0:
                        pl.wait_ge(sem("A0_kv_ready"), c + 1)
                    pl.wait_ge(sem("A0_pv_done"), (c * UNITS + QUARTERS * j) + (CRED - QUARTERS))
                    pl.tensor_tensor(kbd0[:, s, :, :], kT0[:, p, j * P:j * P + P].unsqueeze(1).to_broadcast([P, HEADS, P]),
                                     headmask[:, :].unsqueeze(2).to_broadcast([P, HEADS, P]), ALU.mult)
                    pl.tensor_tensor(vpad0[:, s, 0:HEADS * (VW0 + D0)].rearrange("p (h r) -> p h r", r=VW0 + D0)[:, :, 0:D0],
                                     v0[:, p, j * D0:j * D0 + D0].unsqueeze(1).to_broadcast([P, HEADS, D0]),
                                     bv0[:, :].unsqueeze(1).to_broadcast([P, HEADS, D0]), ALU.add).then_inc(sem("A0_spread"), 1)

            with pl.Fori(0, NC // 2 - 1) as i:
                for p in range(2):
                    power("A0", i * 2 + (p + 1))
                    spread(i * 2 + p, p)
            power("A0", NC - 1)
            spread(NC - 2, 0)
            spread(NC - 1, 1)

            stage_start(pl, STAGE["F0"])
            with pl.Fori(0, NC) as c:
                pl.wait_ge(s_var, c + (1 + VAR0["F0"]))
                pl.tensor_tensor(rstd[:, :], ve[:, :], mhalf[:, :], ALU.pow).then_inc(s_rstd, 1)
                pl.wait_ge(s_xn, c + (1 + XN0["F0"]))
                pl.tensor_copy(xall0[:, bass.ds(c * CB, CB), :], xn[:, :, :]).then_inc(sem("F0_xn_kept"), 1)
                pl.wait_ge(sem("F0_xnT"), c + 1)
                pl.wait_ge(sem("F0_convT"), c + 1)
                pl.sem_inc(s_held, 1)
                xv = xnT[:, :].rearrange("p (j t) -> p j t", j=CB)
                pl.tensor_scalar(conv0[:, :, :], xv, cw0[:, 3:4], cb0[:, 0:1], ALU.mult, ALU.add)
                for k in range(3):
                    lag = 3 - k
                    n = P - lag
                    pl.tensor_scalar(ctap0[:, :, 0:n], xv[:, :, 0:n], cw0[:, k:k + 1], None, ALU.mult).then_inc(sem("F0_tap"), 1)
                    pl.wait_ge(sem("F0_tap"), c * 6 + (2 * k + 1))
                    t = pl.tensor_tensor(conv0[:, :, lag:P], conv0[:, :, lag:P], ctap0[:, :, 0:n], ALU.add)
                    t.then_inc(sem("F0_tap") if k < 2 else sem("F0_conv"), 1)
                    if k < 2:
                        pl.wait_ge(sem("F0_tap"), c * 6 + (2 * k + 2))
                        pl.sem_inc(s_held, 1)
                    else:
                        pl.sem_inc(sem("F0_tap"), 1)

            with pl.Fori(0, NC) as c:
                power("A1", c)
            with pl.Fori(0, NC) as c:
                power("F1", c)
                pl.wait_ge(sem("F1_scale1"), c + 1)
                pl.wait_ge(sem("F1_scaleT"), c + 1)
                pl.sem_inc(s_held, 1)
                pl.tensor_copy(iscb1[:, :, :], am1[:, :].unsqueeze(2).to_broadcast([P, CB, P])).then_inc(sem("F1_scale_spread"), 1)
            with pl.Fori(0, NC) as c:
                power("A2", c)
            with pl.Fori(0, NC) as c:
                power("F2", c)
            with pl.Fori(0, 2 * NC) as c:
                power("A3", c)
            with pl.Fori(0, NC) as c:
                power("F3", c)

        @block.tensor
        def _(pe):
            pe.wait_ge(s_const, 1)
            pe.wait_ge(s_load, 16 * n_loads)
            s_bk, s_gone = sem("setup_bank_full"), sem("setup_bank_gone")
            n = [0]

            def group(pairs):
                i = n[0]
                if i >= 8:
                    pe.wait_ge(s_gone, i - 7)
                for q, (src, parts) in enumerate(pairs):
                    last = nc.tensor.transpose(bank[i % 8][:, q * parts:(q + 1) * parts], src, ident[0:parts, 0:parts])
                last.then_inc(s_bk, 1)
                n[0] += 1

            group([(raw1[:, i, :], P) for i in range(3)])
            group([(raw2[:, i, :], P) for i in range(3)])
            for t in range(2):
                for half in range(2):
                    group([(wqkn3[:, t, (4 * half + q) * P:(4 * half + q + 1) * P], P) for q in range(4)])
            group([(kr3[:, t, :], E3) for t in range(2)])
            pe.wait_ge(s_gone, 6)
            for qd in range(4):
                i = n[0]
                if i >= 8:
                    pe.wait_ge(s_gone, i - 7)
                for u in range(HQ):
                    h = 8 * (qd // 2) + 2 * u + qd % 2
                    r = slice(D3 * (h % 2), D3 * (h % 2) + D3)
                    last = nc.tensor.matmul(bank[i % 8][:, u * P:u * P + P], wqkT3[r, 0, h // 2, :], wqkT3[r, 1, h // 2, :], start=True, stop=True)
                last.then_inc(s_bk, 1)
                n[0] += 1
            pe.wait_ge(sem("setup_abs"), 1)
            pe.wait_ge(s_gone, n[0] - 7)
            nc.tensor.matmul(bank[n[0] % 8][:, 0:2], ones[:, :], part[:, :], start=True, stop=True).then_inc(s_bk, 1)
            n[0] += 1
            pe.wait_ge(sem("setup_keysq"), 1)
            pe.wait_ge(s_gone, n[0] - 7)
            nc.tensor.matmul(bank[n[0] % 8][:, 0:E3], ones[:, :], keysq[:, :], start=True, stop=True).then_inc(s_bk, 1)
            n[0] += 1
            pe.wait_ge(sem("setup_ternary"), 1)
            group([(wabs[:, 0, q * P:(q + 1) * P], P) for q in range(4)])
            group([(wabs[:, 1, q * P:(q + 1) * P], P) for q in range(4)])
            pe.wait_ge(sem("setup_done"), 1)

            def transpose_x(st, c):
                pe.wait_ge(s_xn, c + (1 + XN0[st]))
                for j in range(CB):
                    last = nc.tensor.transpose(bank[0][:, j * P:j * P + P], xn[:, j, :], ident[:, :])
                return last

            def heads(st):
                l0 = st == "A0"
                kA = 5 if l0 else 2 + HEADS + 2 * CB
                A = bank[6]

                def piece(c, p, s):
                    pe.wait_ge(sem(st + "_slice_gone"), c * kA + (s + 1))
                    if s == 0:
                        pe.wait_ge(s_xn, c + (1 + XN0[st]))
                        for j in range(CB):
                            last = nc.tensor.transpose(A[:, j * P:j * P + P], xn[:, j, :], ident[:, :])
                        last.then_inc(sem(st + "_slice"), 1)
                        return
                    if s == 1:
                        pe.wait_ge(s_cx, c * 16 + (16 + 16 * CX0[st]))
                        for j in range(CB):
                            last = nc.tensor.transpose(A[:, j * P:j * P + P], cx[:, j, :], ident[:, :])
                        last.then_inc(sem(st + "_slice"), 1)
                        return
                    pe.wait_ge(sem(st + "_xnT"), c + 1)
                    if l0 and s == 2:
                        last = nc.tensor.matmul(A[:, :], wq0[:, :], xnT[:, :], start=True, stop=True)
                    elif l0 and s == 3:
                        pe.wait_ge(sem(st + "_cxT"), c + 1)
                        last = nc.tensor.matmul(A[:, :], wkr0[:, :], cxT[:, p, :], start=True, stop=True)
                    elif l0:
                        for j in range(CB):
                            last = nc.tensor.matmul(A[:, j * D0:j * D0 + D0], cxT[:, p, j * P:j * P + P], wvs0[:, :], start=True, stop=True)
                    elif s < 2 + HEADS:
                        last = nc.tensor.matmul(A[:, :], m3[:, s - 2, :], xnT[:, :], start=True, stop=True)
                    else:
                        j, half = divmod(s - 2 - HEADS, 2)
                        pe.wait_ge(sem(st + "_cxT"), c + 1)
                        last = nc.tensor.matmul(A[:, :], cxT[:, p, j * P:j * P + P], wv3[:, half * W:half * W + W], start=True, stop=True)
                    last.then_inc(sem(st + "_slice"), 1)

                def body(c, p, more):
                    n0 = c * UNITS
                    for u in range(STEPS):
                        if u < UNITS:
                            j, qd = divmod(u, QUARTERS)
                            pe.wait_ge(sem(st + "_less_max"), n0 + (u - 1 + CRED))
                            if u == 0:
                                pe.wait_ge(sem(st + "_slices_ready"), c + 1)
                            if l0:
                                if qd == 0:
                                    pe.wait_ge(sem("A0_spread"), c * CB + (j + 1))
                                nc.tensor.matmul(bank[u % 2][:, :], qT0[:, p, j * P:j * P + P], kbd0[:, j % 2, qd * HQ:(qd + 1) * HQ, :],
                                                 start=True, stop=True).then_inc(sem(st + "_scores"), 1)
                            else:
                                for i in range(HQ):
                                    last = nc.tensor.matmul(bank[u % 2][:, i * P:i * P + P], g3[:, p, qd * HQ + i, j * P:j * P + P],
                                                            cxT[:, p, j * P:j * P + P], start=True, stop=True)
                                last.then_inc(sem(st + "_scores"), 1)
                        if 1 <= u <= UNITS:
                            v = u - 1
                            pe.wait_ge(sem(st + "_exp"), n0 + (v + 1 + CRED))
                            pe.wait_ge(sem(st + "_pT"), n0 + (v - 1 + CRED))
                            for i in range(HQ):
                                last = nc.tensor.transpose(bank[2 + v % 2][:, i * P:i * P + P], pr[:, v % 2, i, :], ident[:, :])
                            last.then_inc(sem(st + "_pT_full"), 1)
                        mine = slices_at(u, kA) if more else []
                        if mine:
                            piece(c + 1, 1 - p, mine[0])
                        if 2 <= u < UNITS + 2:
                            v = u - 2
                            j, qd = divmod(v, QUARTERS)
                            pe.wait_ge(sem(st + "_pT"), n0 + (v + 1 + CRED))
                            if l0:
                                if qd == 0:
                                    pe.wait_ge(sem("A0_normal"), c * CB + (j + 1))
                                for i in range(HQ):
                                    h = qd * HQ + i
                                    last = nc.tensor.matmul(bank[4][:, 0:VW0], pT[:, v % 2, i, :], vpad0[:, j % 2, h * VW0:h * VW0 + VW0],
                                                            start=(h == 0), stop=(h == HEADS - 1))
                            else:
                                pe.wait_ge(sem("A3_normal"), n0 + (v + 1))
                                for i in range(HQ):
                                    last = nc.tensor.matmul(bank[4][:, i * (D3 + 1):(i + 1) * (D3 + 1)], pT[:, v % 2, i, :],
                                                            v3[p][:, j, qd * HQ + i, :], start=True, stop=True)
                            last.then_inc(sem(st + "_pv_done"), 1)
                        for s in mine[1:]:
                            piece(c + 1, 1 - p, s)
                        for part_, lag in enumerate((6,) if l0 else (6, 7)):
                            if u >= lag and (u - lag) % QUARTERS == 0 and (u - lag) // QUARTERS < CB:
                                j = (u - lag) // QUARTERS
                                if l0:
                                    pe.wait_ge(sem("A0_normal"), c * CB + (j + 2))
                                    pe.wait_ge(sem("A0_oT"), c * CB + (j + 1))
                                    nc.tensor.transpose(bank[5][:, 0:P], on0[:, j % 2, :], ident[:, :]).then_inc(sem("A0_oT_full"), 1)
                                else:
                                    pe.wait_ge(sem("A3_normal"), n0 + (QUARTERS * (j + 1) + 1))
                                    pe.wait_ge(sem("A3_oT"), c * (2 * CB) + (2 * j + part_ + 1))
                                    for q in range(4):
                                        k = 4 * part_ + q
                                        last = nc.tensor.transpose(bank[5][:, q * P:q * P + P], on3[:, j % 2, k * P:k * P + P], ident[:, :])
                                    last.then_inc(sem("A3_oT_full"), 1)
                        lag = 7 if l0 else 8
                        if u >= lag and (u - lag) % QUARTERS == 0 and (u - lag) // QUARTERS < CB:
                            j = (u - lag) // QUARTERS
                            if j == 0:
                                pe.wait_ge(s_xdone, c + (NC * STAGE[st] + 1))
                            if l0:
                                pe.wait_ge(sem("A0_oT"), c * CB + (j + 2))
                                nc.tensor.matmul(bank[7][:, j * P:j * P + P], oT0[:, j % 2, :], wo0[:, :], start=True, stop=True)\
                                    .then_inc(sem(st + "_y"), 1)
                            else:
                                pe.wait_ge(sem("A3_oT"), c * (2 * CB) + (2 * j + 3))
                                for k in range(8):
                                    last = nc.tensor.matmul(bank[7][:, j * P:j * P + P], oT3[:, k, :], wo3[:, k, :], start=(k == 0), stop=(k == 7))
                                last.then_inc(sem(st + "_y"), 1)

                for s in range(kA):
                    piece(0, 0, s)
                with pe.Fori(0, NC // 2 - 1) as i:
                    for p in range(2):
                        body(i * 2 + p, p, True)
                body(NC - 2, 0, True)
                body(NC - 1, 1, False)

            heads("A0")

            stage_start(pe, STAGE["F0"])

            def f0(c):
                transpose_x("F0", c).then_inc(sem("F0_xT"), 1)
                pe.wait_ge(sem("F0_xnT"), c + 1)
                pe.wait_ge(sem("F0_tanh"), c + 1)
                for j in range(CB):
                    last = nc.tensor.matmul(bank[5][:, j * R0:j * R0 + R0], xnT[:, j * P:j * P + P], wr0[:, :], start=True, stop=True)
                last.then_inc(sem("F0_router"), 1)
                for k in range(2):
                    pe.wait_ge(sem("F0_silu"), c * 2 + (k + 1))
                    nc.tensor.matmul(bank[1 + 2 * k][:, :], wg0[:, k * P:k * P + P], xnT[:, :], start=True, stop=True).then_inc(sem("F0_gate"), 1)
                    pe.wait_ge(sem("F0_hid"), c * 2 + (k + 1))
                    nc.tensor.matmul(bank[2 + 2 * k][:, :], wu0[:, k * P:k * P + P], xnT[:, :], start=True, stop=True).then_inc(sem("F0_up"), 1)
                pe.wait_ge(sem("F0_conv"), c + 2)
                for j in range(CB):
                    last = nc.tensor.transpose(bank[0][:, j * P:j * P + P], conv0[:, j, :], ident[:, :])
                last.then_inc(sem("F0_convT"), 1)
                pe.wait_ge(sem("F0_hid"), c * 2 + 4)
                for j in range(CB):
                    pe.wait_ge(sem("F0_down_read"), c * CB + (j + 1))
                    for k in range(2):
                        last = nc.tensor.matmul(bank[6 + j % 2][:, k * 2 * P:(k + 1) * 2 * P], hid0[:, k, j * P:j * P + P], wd0[:, k, :],
                                                start=True, stop=True)
                    last.then_inc(sem("F0_down"), 1)

            pe.wait_ge(s_wd, 64)
            f0(0)
            with pe.Fori(1, NC) as c:
                pe.wait_ge(sem("F0_conv_read"), c)
                f0(c)

            def single(st):
                stage_start(pe, STAGE[st])
                wT = wT1 if st == "A1" else wT2

                def front(c, first, back):
                    if not first:
                        pe.wait_ge(sem(st + "_xnT"), c)
                    transpose_x(st, c).then_inc(sem(st + "_xT"), 1)
                    pe.wait_ge(s_cx, c * 16 + (16 + 16 * CX0[st]))
                    if not first:
                        pe.wait_ge(sem(st + "_cxT"), c)
                    for j in range(CB):
                        last = nc.tensor.transpose(bank[1][:, j * P:j * P + P], cx[:, j, :], ident[:, :])
                    last.then_inc(s_cT, 1)
                    if back and st == "A2":
                        probs_T(c - 1)
                    pe.wait_ge(sem(st + "_xnT"), c + 1)
                    if not first:
                        pe.wait_ge(sem(st + "_qT"), c)
                    nc.tensor.matmul(bank[2][:, :], wT[:, 0, :], xnT[:, :], start=True, stop=True).then_inc(sem(st + "_q"), 1)
                    pe.wait_ge(sem(st + "_cxT"), c + 1)
                    if not first:
                        pe.wait_ge(sem(st + "_kT"), c)
                    nc.tensor.matmul(bank[3][:, :], wT[:, 1, :], cxT[:, 0, :], start=True, stop=True).then_inc(sem(st + "_k"), 1)
                    if back:
                        pv(c - 1)
                    if not first:
                        pe.wait_ge(sem(st + "_v_sb"), c)
                    for j in range(CB):
                        last = nc.tensor.matmul(bank[4][:, j * P:j * P + P], cxT[:, 0, j * P:j * P + P], wT[:, 2, :], start=True, stop=True)
                    last.then_inc(sem(st + "_v"), 1)
                    pe.wait_ge(sem(st + "_qT"), c + 1)
                    pe.wait_ge(sem(st + "_kT"), c + 1)
                    if not first:
                        pe.wait_ge(sem(st + "_less_max"), c)
                    for j in range(CB):
                        js = slice(j * P, j * P + P)
                        lhs, rhs = (kT1, qT1) if st == "A1" else (qT1, kT1)
                        last = nc.tensor.matmul(bank[7][:, js], lhs[:, js], rhs[:, js], start=True, stop=True)
                    last.then_inc(sem(st + "_scores"), 1)

                def probs_T(c):
                    pe.wait_ge(sem(st + "_exp"), c + 1)
                    for j in range(CB):
                        last = nc.tensor.transpose(bank[5][:, j * P:j * P + P], pr[:, 0, j, :], ident[:, :])
                    last.then_inc(sem(st + "_pT_full"), 1)

                def pv(c):
                    pe.wait_ge(sem(st + "_v_sb"), c + 1)
                    if st == "A1":
                        pe.wait_ge(sem(st + "_normal"), c + 1)
                        src = pr
                    else:
                        pe.wait_ge(sem(st + "_pT"), c + 1)
                        src = pT
                    for j in range(CB):
                        last = nc.tensor.matmul(bank[6][:, j * P:j * P + P], src[:, 0, j, :], v1[:, j, :], start=True, stop=True)
                    last.then_inc(sem(st + "_pv_done"), 1)

                front(0, True, False)
                with pe.Fori(1, NC) as c:
                    front(c, False, True)
                if st == "A2":
                    probs_T(NC - 1)
                pv(NC - 1)

            single("A1")

            stage_start(pe, STAGE["F1"])

            def f1(c, first):
                b0h = bank[0][:, 0:W // 2].bitcast(BF16)
                pe.wait_ge(sem("F1_xq"), c + 1)
                for j in range(CB):
                    last = nc.tensor.transpose(b0h[:, j * P:j * P + P], xq1[:, j, :], ident16[:, :])
                last.then_inc(sem("F1_xT"), 1)
                pe.wait_ge(sem("F1_scale_spread"), c + 1)
                for j in range(CB):
                    last = nc.tensor.transpose(bank[5][:, j * P:j * P + P], iscb1[:, j, :], ident[:, :])
                last.then_inc(sem("F1_scaleT"), 1)
                pe.wait_ge(sem("F1_xqT"), c + 1)
                for k in range(K1):
                    if not first:
                        pe.wait_ge(sem("F1_hs"), c * K1 + (k + 1 - K1))
                    nc.tensor.matmul(bank[1 + k][:, :], w1q[:, k * P:k * P + P], xqT1[:, :], start=True, stop=True).then_inc(sem("F1_h"), 1)
                pe.wait_ge(sem("F1_silu"), c * K1 + K1)
                for j in range(CB):
                    pe.wait_ge(sem("F1_round2"), c * CB + (j + 1))
                    for k in range(K1):
                        last = nc.tensor.transpose(bank[6 + j % 2][:, k * P:k * P + P], h1[:, k, j * P:j * P + P], ident[:, :])
                    last.then_inc(sem("F1_hT"), 1)
                for j in range(CB):
                    pe.wait_ge(sem("F1_hq"), c * CB + (j + 3))
                    pe.wait_ge(sem("F1_hqT"), c * CB + (j + 1))
                    if j == 0:
                        pe.wait_ge(sem("F1_xqT"), c + 1)
                    for k in range(K1):
                        last = nc.tensor.transpose(b0h[:, k * P:k * P + P], hq1[:, j, k * P:k * P + P], ident16[:, :])
                    last.then_inc(sem("F1_hqT_full"), 1)
                    pe.wait_ge(sem("F1_hqT"), c * CB + (j + 2))
                    if j == 0:
                        pe.wait_ge(sem("F1_sbc"), c + 1)
                    for k in range(K1):
                        last = nc.tensor.matmul(bank[5][:, j * P:j * P + P], hqT1[:, j % 2, k * P:k * P + P], w2q[:, k, :],
                                                start=(k == 0), stop=(k == K1 - 1))
                    last.then_inc(sem("F1_y"), 1)

            f1(0, True)
            with pe.Fori(1, NC) as c:
                pe.wait_ge(s_xdone, c + (NC * STAGE["F1"] + 1))
                f1(c, False)

            single("A2")

            stage_start(pe, STAGE["F2"])

            def f2(c):
                transpose_x("F2", c).then_inc(sem("F2_xT"), 1)
                pe.wait_ge(sem("F2_xnT"), c + 1)
                pe.wait_ge(sem("F2_logits_read"), c + 1)
                for j in range(CB):
                    last = nc.tensor.matmul(bank[1][:, j * P:j * P + P], xnT[:, j * P:j * P + P], wg2[:, :], start=True, stop=True)
                last.then_inc(sem("F2_logits"), 1)
                pe.wait_ge(sem("F2_onehot"), c + 1)
                for j in range(CB):
                    last = nc.tensor.transpose(bank[6][0:E2, j * P:j * P + P], oh2[:, j, :], ident[:, :])
                last.then_inc(sem("F2_ohT_full"), 1)
                pe.wait_ge(sem("F2_ohT"), c + 1)
                for j in range(CB):
                    last = nc.tensor.matmul(bank[7][:, j * P:j * P + P], ohT2[:, j * P:j * P + P], be2[:, :], start=True, stop=True)
                last.then_inc(sem("F2_bias"), 1)
                for j in range(CB):
                    for half in range(2):
                        pe.wait_ge(sem("F2_z_read"), c * (2 * CB) + (2 * j + half + 1))
                        nc.tensor.matmul(bank[2 + (2 * j + half) % 4][:, :], xnT[:, j * P:j * P + P], we2[:, half * W:half * W + W],
                                         start=True, stop=True).then_inc(sem("F2_z"), 1)

            f2(0)
            with pe.Fori(1, NC) as c:
                pe.wait_ge(sem("F2_xnT"), c)
                f2(c)

            stage_start(pe, STAGE["A3"])
            heads("A3")

            stage_start(pe, STAGE["F3"])

            def route(c):
                transpose_x("F3", c).then_inc(sem("F3_xT"), 1)
                pe.wait_ge(sem("F3_xnT"), c * 2 + 2)
                nc.tensor.matmul(bank[1][0:E3, :], wr3[:, :], xnT[:, :], start=True, stop=True).then_inc(sem("F3_lgT_full"), 1)
                pe.wait_ge(sem("F3_lgT"), c + 1)
                pe.sem_inc(sem("tensor_held"), 1)
                for j in range(CB):
                    last = nc.tensor.transpose(bank[2][:, j * E3:j * E3 + E3], lgT3[:, j * P:j * P + P], ident[0:E3, 0:E3])
                last.then_inc(sem("F3_lg"), 1)
                pe.wait_ge(sem("F3_wt"), c + 1)
                for j in range(CB):
                    last = nc.tensor.transpose(bank[3][0:E3, j * P:j * P + P], wtc3[:, j, :], ident[:, :])
                last.then_inc(sem("F3_wtT_full"), 1)
                pe.wait_ge(sem("F3_wtT"), c + 1)
                for j in range(CB):
                    last = nc.tensor.matmul(bank[4][:, j * P:j * P + P], wtT3[:, j * P:j * P + P], b23[:, :], start=True, stop=True)
                last.then_inc(sem("F3_b2"), 1)

            with pe.Fori(0, NC) as c:
                route(c)
            pe.wait_ge(sem("F3_outputs_added"), NC)

            def expert_T(e, p):
                pe.wait_ge(sem(f"F3_weights_loaded{p}"), e * 16 + (32 - 16 * p))
                pe.wait_ge(sem("F3_w_sb"), e * 2 + 1)
                for k in range(K3):
                    last = nc.tensor.transpose(bank[6][:, k * P:k * P + P], w1n3[:, p, k, :], ident[:, :])
                last.then_inc(sem("F3_weights_transposed"), 1)
                pe.wait_ge(sem("F3_w_sb"), e * 2 + 1)
                for k in range(K3):
                    last = nc.tensor.transpose(bank[7][:, k * P:k * P + P], w2n3[:, p, k * P:k * P + P], ident[:, :])
                last.then_inc(sem("F3_weights_transposed"), 1)

            def up(e, c, p):
                for k in range(K3):
                    pe.wait_ge(sem("F3_gelu"), e * (NC * K3) + (c * K3 + (k + 1)))
                    nc.tensor.matmul(bank[k][:, :], w1T3[:, p, k * P:k * P + P], xall3[:, bass.ds(c * W, W)], start=True, stop=True)\
                        .then_inc(sem("F3_up"), 1)

            def down(e, c, p, b):
                pe.wait_ge(sem("F3_gelu"), e * (NC * K3) + (c * K3 + 2 * K3))
                pe.wait_ge(sem("F3_outputs_added"), e * NC + (c + (NC - 1)))
                for j in range(CB):
                    for k in range(K3):
                        last = nc.tensor.matmul(bank[b][:, j * P:j * P + P], h3[:, b - 4, k, j * P:j * P + P], w2T3[:, p, k, :],
                                                start=(k == 0), stop=(k == K3 - 1))
                last.then_inc(sem("F3_down"), 1)

            def expert(e, p, more):
                pe.wait_ge(sem("F3_w_sb"), e * 2 + 3)
                up(e, 0, p)
                with pe.Fori(0, NC // 2 - 1) as i:
                    up(e, i * 2 + 1, p)
                    down(e, i * 2, p, 4)
                    up(e, i * 2 + 2, p)
                    down(e, i * 2 + 1, p, 5)
                up(e, NC - 1, p)
                down(e, NC - 2, p, 4)
                if more:
                    expert_T(e + 1, 1 - p)
                down(e, NC - 1, p, 5)

            expert_T(0, 0)
            with pe.Fori(0, E3 // 2 - 1) as i:
                for p in range(2):
                    expert(i * 2 + p, p, True)
            expert(E3 - 2, 0, True)
            expert(E3 - 1, 1, False)

        @block.scalar
        def _(act):
            copy = lambda o, i: nc.scalar.activation(o, i, ACT.Copy)
            aff = lambda o, i, s, b: nc.scalar.activation(o, i, ACT.Identity, bias=b, scale=s)
            exp = lambda o, i: nc.scalar.activation(o, i, ACT.Exp)
            act.wait_ge(s_load, 16 * n_loads)
            s_bk, s_gone = sem("setup_bank_full"), sem("setup_bank_gone")
            nc.scalar.activation(gates[:, :], graw[:, :], ACT.Tanh).then_inc(sem("setup_gates"), 1)
            n = [0]

            def out_of_bank(dst, cols, scale=1.0):
                act.wait_ge(s_bk, n[0] + 1)
                src = bank[n[0] % 8][:, 0:cols]
                if len(dst.shape) == 3:
                    src = src.rearrange("p (a b) -> p a b", a=dst.shape[1])
                nc.scalar.activation(dst, src, ACT.Copy, scale=scale).then_inc(s_gone, 1)
                n[0] += 1

            out_of_bank(wT1[:, :, :], 3 * P)
            out_of_bank(wT2[:, :, :], 3 * P)
            for t in range(2):
                for half in range(2):
                    out_of_bank(wqkT3[:, t, 4 * half:4 * half + 4, :], W)
            out_of_bank(keyT[:, :, :], 2 * E3)
            for qd in range(4):
                out_of_bank(m3[:, 8 * (qd // 2) + qd % 2:8 * (qd // 2) + 8:2, :], W, scale=float(D3) ** -0.5)
            act.wait_ge(sem("setup_wscale"), 1)
            n[0] += 2
            out_of_bank(w1q[:, :], W)
            out_of_bank(w2q[:, :, :], W)
            act.wait_ge(sem("setup_done"), 1)

            def heads(st):
                l0 = st == "A0"
                kA = 5 if l0 else 2 + HEADS + 2 * CB
                A = bank[6]

                def piece(c, p, s):
                    act.wait_ge(sem(st + "_slice"), c * kA + (s + 1))
                    gone = sem(st + "_slice_gone")
                    if s == 0:
                        if l0:
                            copy(xnT[:, :], A[:, :]).then_inc(sem(st + "_xnT"), 1)
                        else:
                            aff(xnT[:, :], A[:, :], gam3[:, 0:1], bet3[:, 0:1]).then_inc(sem(st + "_xnT"), 1)
                        act.wait_ge(sem(st + "_xnT"), c + 1)
                        act.sem_inc(gone, 1)
                        return
                    if s == 1:
                        copy(cxT[:, p, :], A[:, :]).then_inc(sem(st + "_cxT"), 1)
                        act.wait_ge(sem(st + "_cxT"), c + 1)
                        act.sem_inc(gone, 1)
                        act.sem_inc(s_cT, 1)
                        return
                    if l0 and s == 2:
                        i = aff(qT0[:, p, :], A[:, :], float(D0) ** -0.5, bq0[:, 0:1])
                    elif l0 and s == 3:
                        i = aff(kT0[:, p, :], A[:, :], 1.0, bk0[:, 0:1])
                    elif l0:
                        i = copy(v0[:, p, :], A[:, 0:CB * D0])
                    elif s < 2 + HEADS:
                        i = copy(g3[:, p, s - 2, :], A[:, :])
                    else:
                        j, half = divmod(s - 2 - HEADS, 2)
                        i = copy(v3[p][:, j, 8 * half:8 * half + 8, 0:D3], A[:, :].rearrange("p (h d) -> p h d", d=D3))
                    i.then_inc(gone, 1)
                    if s == kA - 1:
                        act.wait_ge(gone, c * kA + (kA + 1))
                        act.sem_inc(sem(st + "_slices_ready"), 1)
                        if l0:
                            act.sem_inc(sem("A0_kv_ready"), 1)

                def body(c, p, more):
                    n0 = c * UNITS
                    for u in range(STEPS):
                        if 1 <= u <= UNITS:
                            v = u - 1
                            act.wait_ge(sem(st + "_pT_full"), n0 + (v + 1))
                            act.wait_ge(sem(st + "_pv_done"), n0 + (v - 1 + CRED))
                            copy(pT[:, v % 2, :, :], b4(2 + v % 2)).then_inc(sem(st + "_pT"), 1)
                        mine = slices_at(u, kA) if more else []
                        if mine:
                            piece(c + 1, 1 - p, mine[0])
                        if u < UNITS:
                            act.wait_ge(sem(st + "_less_max"), n0 + (u + 1 + CRED))
                            if u >= 2:
                                act.wait_ge(sem(st + "_pT_full"), n0 + (u - 1))
                            exp(pr[:, u % 2, :, :], sm[:, u % 2, :, :]).then_inc(sem(st + "_exp"), 1)
                        for s in mine[1:]:
                            piece(c + 1, 1 - p, s)
                        for part_, lag in enumerate((6,) if l0 else (6, 7)):
                            if u >= lag and (u - lag) % QUARTERS == 0 and (u - lag) // QUARTERS < CB:
                                j = (u - lag) // QUARTERS
                                if l0:
                                    act.wait_ge(sem("A0_oT_full"), c * CB + (j + 1))
                                    copy(oT0[:, j % 2, :], bank[5][:, 0:P]).then_inc(sem("A0_oT"), 1)
                                else:
                                    act.wait_ge(sem("A3_oT_full"), c * (2 * CB) + (2 * j + part_ + 5))
                                    act.wait_ge(sem("A3_y"), c * CB + (j + 1))
                                    copy(oT3[:, 4 * part_:4 * part_ + 4, :], b4(5)).then_inc(sem("A3_oT"), 1)

                act.sem_inc(sem(st + "_slice_gone"), 1)
                act.sem_inc(sem(st + "_pT"), CRED)
                act.sem_inc(sem(st + "_exp"), CRED)
                act.sem_inc(sem(st + "_pv_done"), CRED)
                act.sem_inc(sem(st + "_oT"), 1)
                if not l0:
                    act.sem_inc(sem("A3_y"), 1)
                    act.sem_inc(sem("A3_oT_full"), 4)
                for s in range(kA):
                    piece(0, 0, s)
                with act.Fori(0, NC // 2 - 1) as i:
                    for p in range(2):
                        body(i * 2 + p, p, True)
                body(NC - 2, 0, True)
                body(NC - 1, 1, False)

            heads("A0")

            stage_start(act, STAGE["F0"])
            act.sem_inc(sem("F0_tanh"), 1)
            act.sem_inc(sem("F0_silu"), 2)
            with act.Fori(0, NC) as c:
                act.wait_ge(sem("F0_xT"), c + 1)
                act.wait_ge(sem("F0_up"), c * 2 + 1)
                act.wait_ge(sem("F0_conv"), c + 1)
                copy(xnT[:, :], bank[0][:, :]).then_inc(sem("F0_xnT"), 1)
                act.wait_ge(sem("F0_router"), c + 1)
                act.wait_ge(sem("F0_weights"), c + 1)
                nc.scalar.activation(lg0[:, :, :], bank[5][:, 0:CB * R0].rearrange("p (j r) -> p j r", j=CB), ACT.Tanh, scale=0.5)\
                    .then_inc(sem("F0_tanh"), 1)
                for k in range(2):
                    act.wait_ge(sem("F0_gate"), c * 2 + (k + 1))
                    act.wait_ge(sem("F0_hid"), c * 2 + (k + 1))
                    nc.scalar.activation(sg0[:, k, :], bank[1 + 2 * k][:, :], ACT.Silu).then_inc(sem("F0_silu"), 1)

            def single(st):
                stage_start(act, STAGE[st])

                def front(c, first, back):
                    act.wait_ge(sem(st + "_xT"), c + 1)
                    if not first:
                        act.wait_ge(sem(st + "_q"), c)
                    copy(xnT[:, :], bank[0][:, :]).then_inc(sem(st + "_xnT"), 1)
                    act.wait_ge(s_cT, c + (1 + CX0[st]))
                    if not first:
                        act.wait_ge(sem(st + "_v"), c)
                    copy(cxT[:, 0, :], bank[1][:, :]).then_inc(sem(st + "_cxT"), 1)
                    if back and st == "A2":
                        probs_T(c - 1)
                    if not first:
                        act.wait_ge(sem(st + "_scores"), c)
                    act.wait_ge(sem(st + "_q"), c + 1)
                    bias = bq2[:, 0:1] if st == "A2" else 0.0
                    aff(qT1[:, :], bank[2][:, :], float(P) ** -0.5, bias).then_inc(sem(st + "_qT"), 1)
                    act.wait_ge(sem(st + "_k"), c + 1)
                    aff(kT1[:, :], bank[3][:, :], 1.0, bk2[:, 0:1] if st == "A2" else 0.0).then_inc(sem(st + "_kT"), 1)
                    act.wait_ge(sem(st + "_less_max"), c + 1)
                    if not first:
                        act.wait_ge(sem(st + "_pv_done"), c)
                        act.wait_ge(sem(st + "_summed"), c)
                    exp(pr[:, 0, :, :], sm[:, 0, :, :]).then_inc(sem(st + "_exp"), 1)

                def probs_T(c):
                    act.wait_ge(sem(st + "_pT_full"), c + 1)
                    if not isinstance(c, int):
                        act.wait_ge(sem(st + "_pv_done"), c)
                    copy(pT[:, 0, :, :], b4(5)).then_inc(sem(st + "_pT"), 1)

                front(0, True, False)
                if st == "A2":
                    with act.Fori(1, NC) as c:
                        front(c, False, True)
                    act.wait_ge(sem(st + "_pv_done"), NC - 1)
                    probs_T(NC - 1)
                else:
                    with act.Fori(1, NC) as c:
                        front(c, False, True)

            single("A1")

            stage_start(act, STAGE["F1"])
            act.sem_inc(sem("F1_round2"), 2)
            act.sem_inc(sem("F1_hqT"), 1)

            def f1(c, first):
                act.wait_ge(sem("F1_xT"), c + 1)
                if not first:
                    act.wait_ge(sem("F1_h"), c * K1)
                copy(xqT1[:, :], bank[0][:, 0:W // 2].bitcast(BF16)).then_inc(sem("F1_xqT"), 1)
                act.wait_ge(sem("F1_scaleT"), c + 2)
                if not first:
                    act.wait_ge(sem("F1_hs"), c * K1)
                nc.scalar.activation(sbc1[:, :], bank[5][:, :], ACT.Copy, scale=1.0).then_inc(sem("F1_sbc"), 1)
                for k in range(K1):
                    act.wait_ge(sem("F1_conv"), c * K1 + (k + 1))
                    if k == 0 and not first:
                        act.wait_ge(sem("F1_hT"), c * CB)
                    nc.scalar.activation(h1[:, k, :].rearrange("p (j t) -> p j t", j=CB), hc1[:, k % 2, :, :], ACT.Silu,
                                         bias=cb1[:, k:k + 1]).then_inc(sem("F1_silu"), 1)
                for j in range(CB):
                    act.wait_ge(sem("F1_scale2"), c * CB + (j + 1))
                    act.wait_ge(sem("F1_hq"), c * CB + (j + 1))
                    nc.scalar.activation(hr1[:, j % 2, :], bank[6 + j % 2][:, :], ACT.Copy, scale=sc2[:, j:j + 1]).then_inc(sem("F1_round2"), 1)
                for j in range(CB):
                    act.wait_ge(sem("F1_hqT_full"), c * CB + (j + 1))
                    act.wait_ge(sem("F1_y"), c * CB + (j + 1))
                    copy(hqT1[:, j % 2, :], bank[0][:, 0:W // 2].bitcast(BF16)).then_inc(sem("F1_hqT"), 1)

            f1(0, True)
            with act.Fori(1, NC) as c:
                f1(c, False)

            single("A2")

            stage_start(act, STAGE["F2"])

            def f2(c, first):
                act.wait_ge(sem("F2_xT"), c + 1)
                if not first:
                    act.wait_ge(sem("F2_z"), c * (2 * CB))
                copy(xnT[:, :], bank[0][:, :]).then_inc(sem("F2_xnT"), 1)
                act.wait_ge(sem("F2_less_max"), c + 1)
                exp(ex2[:, :, :], lg2[:, :, :]).then_inc(sem("F2_exp"), 1)
                act.wait_ge(sem("F2_ohT_full"), c + 1)
                copy(ohT2[:, :], bank[6][0:E2, :]).then_inc(sem("F2_ohT"), 1)
                act.wait_ge(sem("F2_bias"), c + 1)
                if not first:
                    act.wait_ge(s_xdone, c + (NC * STAGE["F2"] + 1))
                copy(acc2[:, :, :], b4(7)).then_inc(sem("F2_acc"), 1)

            f2(0, True)
            with act.Fori(1, NC) as c:
                f2(c, False)

            stage_start(act, STAGE["A3"])
            heads("A3")

            stage_start(act, STAGE["F3"])

            def route(c):
                act.wait_ge(sem("F3_xT"), c + 1)
                copy(xnT[:, :], bank[0][:, :]).then_inc(sem("F3_xnT"), 1)
                copy(xall3[:, bass.ds(c * W, W)], bank[0][:, :]).then_inc(sem("F3_xnT"), 1)
                act.wait_ge(sem("F3_lgT_full"), c + 1)
                copy(lgT3[:, :], bank[1][0:E3, :]).then_inc(sem("F3_lgT"), 1)
                act.wait_ge(sem("F3_less_max"), c + 1)
                exp(ex3[:, :, :], top3[:, :, 0:TOP3]).then_inc(sem("F3_exp"), 1)
                act.wait_ge(sem("F3_wtT_full"), c + 1)
                copy(wtT3[:, :], bank[3][0:E3, :]).then_inc(sem("F3_wtT"), 1)

            with act.Fori(0, NC) as c:
                route(c)
            act.sem_inc(sem("F3_w_sb"), 1)
            act.sem_inc(sem("F3_gelu"), K3)

            def expert_T(e, p):
                act.wait_ge(sem("F3_weights_transposed"), e * 2 + 1)
                copy(w1T3[:, p, :], bank[6][:, :]).then_inc(sem("F3_w_sb"), 1)
                act.wait_ge(sem("F3_weights_transposed"), e * 2 + 2)
                copy(w2T3[:, p, :, :], b4(7)).then_inc(sem("F3_w_sb"), 1)

            def up(e, c, p, s):
                for k in range(K3):
                    act.wait_ge(sem("F3_up"), e * (NC * K3) + (c * K3 + (k + 1)))
                    if k == 0:
                        act.wait_ge(sem("F3_down"), e * NC + (c + 1))
                    act.sem_inc(sem("scalar_held"), 1)
                    nc.scalar.activation(h3[:, s, k, :], bank[k][:, :], ACT.Gelu, bias=b1_at(e, k)).then_inc(sem("F3_gelu"), 1)

            def b1_at(e, k):
                if isinstance(e, int):
                    return b13[:, e, k:k + 1]
                return b13[:, bass.ds(e, 1), k:k + 1].rearrange("p a b -> p (a b)")

            act.sem_inc(sem("F3_down"), 2)

            def expert(e, p, more):
                up(e, 0, p, 0)
                with act.Fori(0, NC // 2 - 1) as i:
                    up(e, i * 2 + 1, p, 1)
                    up(e, i * 2 + 2, p, 0)
                up(e, NC - 1, p, 1)
                if more:
                    expert_T(e + 1, 1 - p)

            expert_T(0, 0)
            with act.Fori(0, E3 // 2 - 1) as i:
                for p in range(2):
                    expert(i * 2 + p, p, True)
            expert(E3 - 2, 0, True)
            expert(E3 - 1, 1, False)

        @block.vector
        def _(dve):
            v = nc.vector
            step = Steps(dve, sem("vector_steps"))
            s_held = sem("vector_held")
            dve.sem_inc(s_xdone, 1)
            dve.wait_ge(s_load, 16 * n_loads)
            dve.wait_ge(s_const, 1)
            step(v.tensor_reduce(wkr0[:, 0:D0], wkv0[:, 0, :].rearrange("p (g d) -> p d g", g=4), AX, ALU.add))
            v.tensor_copy(wkr0[:, D0:P].rearrange("p (h d) -> p h d", d=D0), wkr0[:, 0:D0].unsqueeze(1).to_broadcast([P, HEADS - 1, D0]))
            v.tensor_reduce(wvs0[:, :], wkv0[:, 1, :].rearrange("p (g d) -> p d g", g=4), AX, ALU.add)
            v.tensor_reduce(bv0[:, :], bv0g[:, :].rearrange("p (g d) -> p d g", g=4), AX, ALU.add)
            v.tensor_reduce(bk0[:, :], bk0g[:, :], AX, ALU.add)
            step(v.tensor_scalar(bq0[:, :], bq0[:, :], float(D0) ** -0.5, None, ALU.mult))
            step(v.tensor_scalar(bq2[:, :], bq2[:, :], float(P) ** -0.5, None, ALU.mult))
            dve.wait_ge(sem("setup_gates"), 1)
            step(v.tensor_tensor(gate3[:, :], gates[:, 3:4], gates[:, 8:9], ALU.mult))
            v.tensor_reduce(part[:, 0:1], w1n[:, :, :].rearrange("p k d -> p (k d)"), AX, ALU.add, apply_absolute_value=True)
            v.tensor_reduce(part[:, 1:2], w2n[:, :], AX, ALU.add, apply_absolute_value=True).then_inc(sem("setup_abs"), 1)
            s_bk, s_gone = sem("setup_bank_full"), sem("setup_bank_gone")
            dve.wait_ge(s_gone, 7)
            step(v.scalar_tensor_tensor(wr3[:, :], keyT[:, 0, :], 2.0, keyT[:, 1, :], ALU.mult, ALU.add))
            v.tensor_tensor(keysq[:, :], keyT[:, 0, :], keyT[:, 0, :], ALU.mult).then_inc(sem("setup_keysq"), 1)
            dve.wait_ge(s_bk, 12)
            step(v.tensor_scalar(wsc1[:, :], bank[11 % 8][:, 0:1], 1.0 / (H1 * P), EPS, ALU.mult, ALU.max))
            step(v.tensor_scalar(wsc2[:, :], bank[11 % 8][:, 1:2], 1.0 / (H1 * P), EPS, ALU.mult, ALU.max))
            dve.wait_ge(s_bk, 13)
            step(v.tensor_tensor(rb3[:, :], rb3[:, :], bank[12 % 8][:, 0:E3], ALU.subtract))
            dve.wait_ge(s_gone, 11)
            dve.sem_inc(s_gone, 2)
            dve.sem_inc(sem("setup_wscale"), 1)
            for t, (src, wsc) in enumerate(((w1n[:, :, :].rearrange("p k d -> p (k d)"), wsc1), (w2n[:, :], wsc2))):
                step(v.reciprocal(rs[:, t:t + 1], wsc[:, :]))
                step(v.tensor_scalar(wabs[:, t, :], src, rs[:, t:t + 1], ROUND, ALU.mult, ALU.add))
                step(v.tensor_scalar(wabs[:, t, :], wabs[:, t, :], ROUND, 1.0, ALU.subtract, ALU.min))
                step(v.tensor_scalar(wabs[:, t, :], wabs[:, t, :], -1.0, None, ALU.max))
                step(v.tensor_scalar(wsc[:, :], wsc[:, :], 1.0 / 127, None, ALU.mult))
            dve.sem_inc(sem("setup_ternary"), 1)
            dve.wait_ge(s_gone, 15)
            dve.sem_inc(sem("setup_done"), 1)

            def norm_stats(src):
                for j in range(CB):
                    last = v.bn_stats(stats[:, j, :], src[:, j, :])
                step.held(last, s_held)
                for j in range(CB):
                    last = v.bn_aggr(mv[:, j, :], stats[:, j, :])
                step(last)

            def norm_var(st):
                v.tensor_scalar(ve[:, :].unsqueeze(2), mv[:, :, 1:2], EPS, None, ALU.add).then_inc(s_var, 1)

            def norm_apply(st, c, src, n=None, ready=True, free=None):
                dve.wait_ge(s_rstd, (c if n is None else n) + (1 + VAR0[st]))
                if free is not None:
                    dve.wait_ge(*free)
                for j in range(CB):
                    last = v.tensor_scalar(xn[:, j, :], src[:, j, :], mv[:, j, 0:1], rstd[:, j:j + 1], ALU.subtract, ALU.mult)
                if ready:
                    last.then_inc(s_xn, 1)
                else:
                    step(last)

            def xc(c):
                return x[:, bass.ds(c * CB, CB), :]

            def less_max(src, slot, st):
                step(v.tensor_reduce(nm[:, slot, :], src, AX, ALU.max))
                v.tensor_tensor(sm[:, slot, :, :], src, nm[:, slot, :].unsqueeze(2).to_broadcast([P, CB, P]), ALU.subtract)\
                    .then_inc(sem(st + "_less_max"), 1)

            def heads(st):
                l0 = st == "A0"
                kA = 5 if l0 else 2 + HEADS + 2 * CB
                bias, gate = (bo0, gates[:, 0:1]) if l0 else (bo3, gate3[:, 0:1])

                def softmax(n0, u):
                    dve.wait_ge(sem(st + "_scores"), n0 + (u + 1))
                    dve.wait_ge(sem(st + "_exp"), n0 + (u - 1 + CRED))
                    less_max(b4(u % 2), u % 2, st)

                def normal(c, p, n0, u):
                    j, qd = divmod(u, QUARTERS)
                    if l0:
                        if qd != QUARTERS - 1:
                            return
                        dve.wait_ge(sem(st + "_pv_done"), n0 + (u + 1 + CRED))
                        step(v.reciprocal(rs[:, :], bank[4][:, P:VW0]))
                        v.tensor_tensor(on0[:, j % 2, :].rearrange("p (h d) -> p h d", d=D0), bank[4][:, 0:P].rearrange("p (h d) -> p h d", d=D0),
                                        rs[:, :].unsqueeze(2).to_broadcast([P, HEADS, D0]), ALU.mult).then_inc(sem("A0_normal"), 1)
                        return
                    dve.wait_ge(sem(st + "_pv_done"), n0 + (u + 1 + CRED))
                    if qd == 0:
                        dve.wait_ge(sem("A3_oT_full"), c * (2 * CB) + (2 * j + 2))
                    o = bank[4][:, 0:HQ * (D3 + 1)].rearrange("p (h d) -> p h d", d=D3 + 1)
                    step(v.reciprocal(rs[:, 0:HQ].unsqueeze(2), o[:, :, D3:D3 + 1]))
                    v.tensor_tensor(on3[:, j % 2, qd * HQ * D3:(qd + 1) * HQ * D3].rearrange("p (h d) -> p h d", d=D3), o[:, :, 0:D3],
                                    rs[:, 0:HQ].unsqueeze(2).to_broadcast([P, HQ, D3]), ALU.mult).then_inc(sem("A3_normal"), 1)

                def front(c, k):
                    if l0:
                        if k == 0:
                            norm_stats(xc(c))
                            norm_var(st)
                        if k == 2:
                            norm_apply(st, c, xc(c), free=(sem(st + "_xnT"), c) if not isinstance(c, int) or c else None)
                        return
                    if k == 0:
                        norm_stats(xc(c))
                        norm_var(st)
                    if k == 1:
                        norm_apply(st, c, xc(c), n=c * 2, ready=False, free=(sem(st + "_xnT"), c) if not isinstance(c, int) or c else None)
                    if k == 2:
                        norm_stats(xn)
                        norm_var(st)
                    if k == 3:
                        norm_apply(st, c, xn, n=c * 2 + 1)

                def body(c, p, more):
                    n0 = c * UNITS
                    for u in range(STEPS):
                        if more and u < 4:
                            front(c + 1, u)
                        if u < UNITS:
                            softmax(n0, u)
                        if 2 <= u < UNITS + 2:
                            normal(c, p, n0, u - 2)
                    dve.wait_ge(sem(st + "_y"), c * CB + (CB + (0 if l0 else 1)))
                    step(v.tensor_tensor(tmp[:, :, :], b4(7), bias[:, :].unsqueeze(1).to_broadcast([P, CB, P]), ALU.add))
                    v.scalar_tensor_tensor(xc(c), tmp[:, :, :], gate, xc(c), ALU.mult, ALU.add).then_inc(s_xdone, 1)

                dve.sem_inc(sem(st + "_less_max"), CRED)
                dve.sem_inc(sem(st + "_normal"), 1)
                if not l0:
                    for s in range(2):
                        v.memset(v3[s][:, :, :, D3:D3 + 1], 1.0)
                for k in range(4):
                    front(0, k)
                per = 2 * (UNITS + (CB if l0 else UNITS) + 1 + (2 if l0 else 5))
                step.loop(per)
                with dve.Fori(0, NC // 2 - 1) as i:
                    step.turn(i)
                    for p in range(2):
                        body(i * 2 + p, p, True)
                step.end(NC // 2 - 1)
                body(NC - 2, 0, True)
                body(NC - 1, 1, False)

            heads("A0")

            stage_start(dve, STAGE["F0"])
            dve.sem_inc(sem("F0_hid"), 2)
            dve.sem_inc(sem("F0_weights"), 1)
            dve.sem_inc(sem("F0_down_read"), 2)
            dve.sem_inc(sem("F0_up"), 1)
            dve.sem_inc(sem("F0_conv"), 1)
            dve.sem_inc(sem("F0_convT"), 1)

            def f0_norm(c, first):
                norm_stats(xc(c))
                norm_var("F0")
                dve.wait_ge(s_rstd, c + (1 + VAR0["F0"]))
                if not first:
                    dve.wait_ge(sem("F0_xT"), c)
                    dve.wait_ge(sem("F0_xn_kept"), c)
                for j in range(CB):
                    last = v.tensor_scalar(xn[:, j, :], xc(c)[:, j, :], mv[:, j, 0:1], rstd[:, j:j + 1], ALU.subtract, ALU.mult)
                last.then_inc(s_xn, 1)

            def f0(c, more):
                dve.wait_ge(sem("F0_tanh"), c + 2)
                step(v.tensor_scalar(lg0[:, :, :], lg0[:, :, :], 0.5, 0.5, ALU.mult, ALU.add))
                step.held(v.tensor_tensor(sel0[:, :, :], lg0[:, :, :], rb0[:, :].unsqueeze(1).to_broadcast([P, CB, R0]), ALU.add), s_held)
                for j in range(CB):
                    last = v.max(top0[:, j, :], sel0[:, j, :])
                step.held(last, s_held)
                for j in range(CB):
                    last = v.max_index(idx0[:, j, :], top0[:, j, :], sel0[:, j, :])
                step(last)
                step(v.tensor_copy(idf0[:, :, :], idx0[:, :, :]))
                for r in range(2):
                    step(v.tensor_tensor(oh0[:, r, :, :], iota8[:, 0:R0].unsqueeze(1).to_broadcast([P, CB, R0]),
                                         idf0[:, :, r:r + 1].to_broadcast([P, CB, R0]), ALU.is_equal))
                step(v.tensor_tensor(oh0[:, 0, :, :], oh0[:, 0, :, :], oh0[:, 1, :, :], ALU.add))
                step(v.tensor_tensor(cwt0[:, :, :], oh0[:, 0, :, :], lg0[:, :, :], ALU.mult))
                step(v.tensor_reduce(wsum0[:, :], cwt0[:, :, :], AX, ALU.add))
                step(v.tensor_scalar(wsum0[:, :], wsum0[:, :], 1e-9, None, ALU.add))
                step(v.reciprocal(wsum0[:, :], wsum0[:, :]))
                step(v.tensor_tensor(cwt0[:, :, :], cwt0[:, :, :], wsum0[:, :].unsqueeze(2).to_broadcast([P, CB, R0]), ALU.mult))
                v.tensor_tensor(ccp0[:, :].unsqueeze(2), cwt0[:, :, E0:E0 + 1], cwt0[:, :, E0 + 2:E0 + 3], ALU.add).then_inc(sem("F0_weights"), 1)
                for k in range(2):
                    dve.wait_ge(sem("F0_up"), c * 2 + (k + 2))
                    dve.wait_ge(sem("F0_silu"), c * 2 + (k + 3))
                    if k == 0:
                        dve.wait_ge(sem("F0_down"), c * CB) if not (isinstance(c, int) and c == 0) else None
                    v.tensor_tensor(hid0[:, k, :], bank[2 + 2 * k][:, :], sg0[:, k, :], ALU.mult).then_inc(sem("F0_hid"), 1)
                if more:
                    f0_norm(c + 1, False)
                dve.wait_ge(sem("F0_weights"), c + 2)
                dve.wait_ge(sem("F0_xn_kept"), c + 1)
                xk = xall0[:, bass.ds(c * CB, CB), :]
                for j in range(CB):
                    last = v.tensor_scalar(tmp2[:, j, :], xk[:, j, :], 0.0, cwt0[:, j, R0 - 1:R0], ALU.max, ALU.mult)
                step(last)
                for j in range(CB):
                    last = v.scalar_tensor_tensor(tmp[:, j, :], xk[:, j, :], ccp0[:, j:j + 1], tmp2[:, j, :], ALU.mult, ALU.add)
                step(last)
                dve.wait_ge(sem("F0_convT"), c + 2)
                v.tensor_tensor(tmp[:, :, :], b4(0), tmp[:, :, :], ALU.add).then_inc(sem("F0_conv_read"), 1)
                dve.wait_ge(sem("F0_conv_read"), c + 1)
                for j in range(CB):
                    dve.wait_ge(sem("F0_down"), c * CB + (j + 1))
                    o = b4(6 + j % 2)
                    for e in range(E0):
                        last = v.scalar_tensor_tensor(tmp[:, j, :], o[:, e, :], cwt0[:, j, e:e + 1], tmp[:, j, :], ALU.mult, ALU.add)
                        if e < E0 - 1:
                            step(last)
                    last.then_inc(sem("F0_down_read"), 1)
                dve.wait_ge(sem("F0_down_read"), c * CB + (CB + 2))
                v.scalar_tensor_tensor(xc(c), tmp[:, :, :], gates[:, 4:5], xc(c), ALU.mult, ALU.add).then_inc(s_xdone, 1)

            f0_norm(0, True)
            f0(0, True)
            step.loop(13 + 2 + 2 + CB * (E0 - 1))
            with dve.Fori(1, NC - 1) as c:
                step.turn(c - 1)
                f0(c, True)
            step.end(NC - 2)
            f0(NC - 1, False)

            def single(st):
                stage_start(dve, STAGE[st])
                gate = gates[:, 1:2] if st == "A1" else gates[:, 2:3]

                def ln(c, first):
                    norm_stats(xc(c))
                    norm_var(st)
                    norm_apply(st, c, xc(c), free=None if first else (sem(st + "_xT"), c))

                def summed(c):
                    dve.wait_ge(sem(st + "_exp"), c + 1)
                    step(v.tensor_reduce(sums[:, :], pr[:, 0, :, :], AX, ALU.add))
                    step(v.reciprocal(sums[:, :], sums[:, :]))
                    dve.sem_inc(sem(st + "_summed"), 1)
                    if st == "A1":
                        v.tensor_tensor(pr[:, 0, :, :], pr[:, 0, :, :], sums[:, :].unsqueeze(2).to_broadcast([P, CB, P]), ALU.mult)\
                            .then_inc(sem(st + "_normal"), 1)

                def residual(c):
                    dve.wait_ge(sem(st + "_pv_done"), c + 1)
                    if st == "A1":
                        v.scalar_tensor_tensor(xc(c), b4(6), gate, xc(c), ALU.mult, ALU.add).then_inc(s_xdone, 1)
                    else:
                        step(v.tensor_tensor(tmp[:, :, :], b4(6), sums[:, :].unsqueeze(2).to_broadcast([P, CB, P]), ALU.mult))
                        v.scalar_tensor_tensor(xc(c), tmp[:, :, :], gate, xc(c), ALU.mult, ALU.add).then_inc(s_xdone, 1)

                def scores(c, first):
                    dve.wait_ge(sem(st + "_v"), c + 1)
                    if st == "A1":
                        v.tensor_copy(v1[:, :, :], b4(4)).then_inc(sem(st + "_v_sb"), 1)
                    else:
                        v.tensor_tensor(v1[:, :, :], b4(4), bv2[:, :].unsqueeze(1).to_broadcast([P, CB, P]), ALU.add).then_inc(sem(st + "_v_sb"), 1)
                    dve.wait_ge(sem(st + "_scores"), c + 1)
                    if not first:
                        dve.wait_ge(sem(st + "_exp"), c)
                    if st == "A1":
                        step(v.tensor_tensor(sm[:, 0, :, :], b4(7), causal[:, :].unsqueeze(1).to_broadcast([P, CB, P]), ALU.add))
                        less_max(sm[:, 0, :, :], 0, st)
                    else:
                        less_max(b4(7), 0, st)

                per = 2 + 2 + 1 + 1
                ln(0, True)
                ln(1, False)
                scores(0, True)
                step.loop(per)
                with dve.Fori(1, NC - 1) as c:
                    step.turn(c - 1)
                    summed(c - 1)
                    ln(c + 1, False)
                    residual(c - 1)
                    scores(c, False)
                step.end(NC - 2)
                summed(NC - 2)
                residual(NC - 2)
                scores(NC - 1, False)
                summed(NC - 1)
                residual(NC - 1)

            single("A1")

            stage_start(dve, STAGE["F1"])
            dve.sem_inc(sem("F1_hq"), 2)
            dve.sem_inc(sem("F1_scaleT"), 1)
            dve.sem_inc(sem("F1_y"), 2)

            def f1_norm(c, first):
                norm_stats(xc(c))
                norm_var("F1")
                norm_apply("F1", c, xc(c), ready=False)
                if not first:
                    dve.wait_ge(sem("F1_scale_spread"), c)
                step(v.tensor_reduce(am1[:, :], xn[:, :, :], AX, ALU.max, apply_absolute_value=True))
                step(v.tensor_scalar(am1[:, :], am1[:, :], EPS, None, ALU.max))
                step(v.reciprocal(sc1[:, :], am1[:, :]))
                v.tensor_scalar(sc1[:, :], sc1[:, :], 127.0, None, ALU.mult).then_inc(sem("F1_scale1"), 1)
                dve.wait_ge(sem("F1_scale1"), c + 1)
                for j in range(CB):
                    last = v.tensor_scalar(xr1[:, j, :], xn[:, j, :], sc1[:, j:j + 1], ROUND, ALU.mult, ALU.add)
                step(last)
                step(v.tensor_scalar(xr1[:, :, :], xr1[:, :, :], ROUND, 127.0, ALU.subtract, ALU.min))
                if not first:
                    dve.wait_ge(sem("F1_xT"), c)
                v.tensor_scalar(xq1[:, :, :], xr1[:, :, :], -128.0, None, ALU.max).then_inc(sem("F1_xq"), 1)

            def f1(c, more, first):
                dve.wait_ge(sem("F1_sbc"), c + 1)
                for k in range(K1):
                    dve.wait_ge(sem("F1_h"), c * K1 + (k + 1))
                    step(v.tensor_scalar(hs1[:, k % 2, :, :], b4(1 + k), wsc1[:, 0:1], None, ALU.mult))
                    v.tensor_tensor(hs1[:, k % 2, :, :], hs1[:, k % 2, :, :], sbc1[:, :].rearrange("p (j t) -> p j t", j=CB), ALU.mult)\
                        .then_inc(sem("F1_hs"), 1)
                    dve.wait_ge(sem("F1_hs"), c * K1 + (k + 1))
                    if not (first and k < 2):
                        dve.wait_ge(sem("F1_silu"), c * K1 + (k - 1))
                    h, o = hs1[:, k % 2, :, :], hc1[:, k % 2, :, :]
                    step(v.tensor_scalar(o, h, cw1[:, k, 1:2], None, ALU.mult))
                    step(v.scalar_tensor_tensor(o[:, :, 1:P], h[:, :, 0:P - 1], cw1[:, k, 0:1], o[:, :, 1:P], ALU.mult, ALU.add))
                    v.scalar_tensor_tensor(o[:, :, 0:P - 1], h[:, :, 1:P], cw1[:, k, 2:3], o[:, :, 0:P - 1], ALU.mult, ALU.add)\
                        .then_inc(sem("F1_conv"), 1)
                if more:
                    f1_norm(c + 1, False)
                for j in range(CB):
                    dve.wait_ge(sem("F1_hT"), c * CB + (j + 1))
                    step(v.tensor_reduce(am2[:, j:j + 1], bank[6 + j % 2][:, :], AX, ALU.max, apply_absolute_value=True))
                    step(v.tensor_scalar(am2[:, j:j + 1], am2[:, j:j + 1], EPS, None, ALU.max))
                    step(v.reciprocal(sc2[:, j:j + 1], am2[:, j:j + 1]))
                    v.tensor_scalar(sc2[:, j:j + 1], sc2[:, j:j + 1], 127.0, None, ALU.mult).then_inc(sem("F1_scale2"), 1)
                    if j:
                        hq(c, j - 1)
                hq(c, CB - 1)
                step(v.tensor_scalar(isc2[:, :], am2[:, :], wsc2[:, 0:1], gates[:, 5:6], ALU.mult, ALU.mult))
                dve.wait_ge(sem("F1_y"), c * CB + (CB + 2))
                for j in range(CB):
                    last = v.scalar_tensor_tensor(xc(c)[:, j, :], bank[5][:, j * P:j * P + P], isc2[:, j:j + 1], xc(c)[:, j, :], ALU.mult, ALU.add)
                last.then_inc(s_xdone, 1)

            def hq(c, j):
                dve.wait_ge(sem("F1_round2"), c * CB + (j + 3))
                step(v.tensor_scalar(hr1[:, j % 2, :], hr1[:, j % 2, :], ROUND, ROUND, ALU.add, ALU.subtract))
                v.tensor_scalar(hq1[:, j, :], hr1[:, j % 2, :], 127.0, -128.0, ALU.min, ALU.max).then_inc(sem("F1_hq"), 1)

            f1_norm(0, True)
            f1(0, True, True)
            step.loop(2 + 1 + 5 + K1 * 3 + CB * 3 + CB + 1)
            with dve.Fori(1, NC - 1) as c:
                step.turn(c - 1)
                f1(c, True, False)
            step.end(NC - 2)
            f1(NC - 1, False, False)

            single("A2")

            stage_start(dve, STAGE["F2"])
            dve.sem_inc(sem("F2_z_read"), 4)
            dve.sem_inc(sem("F2_logits_read"), 1)

            def f2(c, more, first):
                dve.wait_ge(sem("F2_logits"), c + 1)
                v.tensor_tensor(lg2[:, :, :], b4(1), bg2[:, :].unsqueeze(1).to_broadcast([P, CB, P]), ALU.add).then_inc(sem("F2_logits_read"), 1)
                dve.wait_ge(sem("F2_logits_read"), c + 2)
                dve.sem_inc(s_held, 1)
                for j in range(CB):
                    last = v.max(top2[:, j, :], lg2[:, j, :])
                step.held(last, s_held)
                for j in range(CB):
                    last = v.max_index(idx2[:, j, :], top2[:, j, :], lg2[:, j, :])
                step(last)
                v.tensor_tensor(lg2[:, :, :], lg2[:, :, :], top2[:, :, 0:1].to_broadcast([P, CB, P]), ALU.subtract).then_inc(sem("F2_less_max"), 1)
                step(v.tensor_single_scalar(idx2[:, :, 0:1], idx2[:, :, 0:1], E2 - 1, ALU.bitwise_and))
                step(v.tensor_copy(idf2[:, :].unsqueeze(2), idx2[:, :, 0:1]))
                if not first:
                    dve.wait_ge(sem("F2_ohT_full"), c)
                v.tensor_tensor(oh2[:, :, :], iota8[:, 0:E2].unsqueeze(1).to_broadcast([P, CB, E2]),
                                idf2[:, :].unsqueeze(2).to_broadcast([P, CB, E2]), ALU.is_equal).then_inc(sem("F2_onehot"), 1)
                dve.wait_ge(sem("F2_exp"), c + 1)
                step(v.tensor_reduce(pg2[:, :], ex2[:, :, :], AX, ALU.add))
                step(v.reciprocal(pg2[:, :], pg2[:, :]))
                step(v.tensor_scalar(pg2[:, :], pg2[:, :], gates[:, 6:7], None, ALU.mult))
                if more:
                    norm_stats(xc(c + 1))
                    norm_var("F2")
                    norm_apply("F2", c + 1, xc(c + 1), free=(sem("F2_xT"), c + 1))
                dve.wait_ge(sem("F2_acc"), c + 1)
                for j in range(CB):
                    for half in range(2):
                        dve.wait_ge(sem("F2_z"), c * (2 * CB) + (2 * j + half + 1))
                        z = b4(2 + (2 * j + half) % 4)
                        for q in range(4):
                            e = 4 * half + q
                            last = v.scalar_tensor_tensor(acc2[:, j, :], z[:, q, :], oh2[:, j, e:e + 1], acc2[:, j, :], ALU.mult, ALU.add)
                            if q < 3:
                                step(last)
                        last.then_inc(sem("F2_z_read"), 1)
                        dve.wait_ge(sem("F2_z_read"), c * (2 * CB) + (2 * j + half + 5))
                step(v.tensor_scalar(acc2[:, :, :], acc2[:, :, :], 0.0, None, ALU.max))
                for j in range(CB):
                    last = v.scalar_tensor_tensor(xc(c)[:, j, :], acc2[:, j, :], pg2[:, j:j + 1], xc(c)[:, j, :], ALU.mult, ALU.add)
                last.then_inc(s_xdone, 1)

            norm_stats(xc(0))
            norm_var("F2")
            norm_apply("F2", 0, xc(0))
            f2(0, True, True)
            step.loop(2 + 2 + 3 + 2 + 2 * CB * 3 + 1)
            with dve.Fori(1, NC - 1) as c:
                step.turn(c - 1)
                f2(c, True, False)
            step.end(NC - 2)
            f2(NC - 1, False, False)

            stage_start(dve, STAGE["A3"])
            heads("A3")

            stage_start(dve, STAGE["F3"])

            def route(c):
                norm_stats(xc(c))
                norm_var("F3")
                norm_apply("F3", c, xc(c))
                dve.wait_ge(s_xn, c + (1 + XN0["F3"]))
                step(v.tensor_tensor(tmp[:, :, :], xn[:, :, :], xn[:, :, :], ALU.mult))
                step(v.tensor_reduce(x23[:, :], tmp[:, :, :], AX, ALU.add))
                dve.wait_ge(sem("F3_lg"), c + 1)
                lgp = bank[2][:, 0:CB * E3].rearrange("p (j e) -> p j e", j=CB)
                step(v.tensor_tensor(lg3[:, :, :], lgp, rb3[:, :].unsqueeze(1).to_broadcast([P, CB, E3]), ALU.add))
                step.held(v.tensor_tensor(lg3[:, :, :], lg3[:, :, :], x23[:, :].unsqueeze(2).to_broadcast([P, CB, E3]), ALU.subtract), s_held)
                for j in range(CB):
                    last = v.max(top3[:, j, :], lg3[:, j, :])
                step.held(last, s_held)
                for j in range(CB):
                    last = v.max_index(idx3[:, j, :], top3[:, j, :], lg3[:, j, :])
                step(last)
                step(v.tensor_copy(idf3[:, :, :], idx3[:, :, :]))
                step(v.tensor_copy(es3[:, :].unsqueeze(2), top3[:, :, 0:1]))
                v.tensor_tensor(top3[:, :, 0:TOP3], top3[:, :, 0:TOP3], es3[:, :].unsqueeze(2).to_broadcast([P, CB, TOP3]), ALU.subtract)\
                    .then_inc(sem("F3_less_max"), 1)
                dve.wait_ge(sem("F3_exp"), c + 1)
                step(v.tensor_reduce(es3[:, :], ex3[:, :, :], AX, ALU.add))
                step(v.reciprocal(es3[:, :], es3[:, :]))
                step(v.tensor_scalar(es3[:, :], es3[:, :], gates[:, 7:8], None, ALU.mult))
                step(v.tensor_tensor(ex3[:, :, :], ex3[:, :, :], es3[:, :].unsqueeze(2).to_broadcast([P, CB, TOP3]), ALU.mult))
                for r in range(TOP3):
                    dst = wtc3 if r == 0 else oh3
                    step(v.tensor_tensor(dst[:, :, :], iota8[:, :].unsqueeze(1).to_broadcast([P, CB, E3]),
                                         idf3[:, :, r:r + 1].to_broadcast([P, CB, E3]), ALU.is_equal))
                    step(v.tensor_tensor(dst[:, :, :], dst[:, :, :], ex3[:, :, r:r + 1].to_broadcast([P, CB, E3]), ALU.mult))
                    if r:
                        step(v.tensor_tensor(wtc3[:, :, :], wtc3[:, :, :], oh3[:, :, :], ALU.add))
                v.tensor_copy(wt3[:, bass.ds(c * CB, CB), :], wtc3[:, :, :]).then_inc(sem("F3_wt"), 1)
                dve.wait_ge(sem("F3_b2"), c + 1)
                v.tensor_tensor(xc(c), b4(4), xc(c), ALU.add).then_inc(sem("F3_outputs_added"), 1)

            step.loop(2 + 2 + 2 + 2 + 2 + 4 + 2 * TOP3 + TOP3 - 1)
            with dve.Fori(0, NC) as c:
                step.turn(c)
                route(c)
            step.end(NC)

            def add(e, c, b):
                dve.wait_ge(sem("F3_down"), e * NC + (c + 3))
                for j in range(CB):
                    if isinstance(e, int):
                        w = wt3[:, bass.ds(c * CB + j, 1), e:e + 1].rearrange("p a b -> p (a b)")
                    else:
                        w = wt3[:, :, :].rearrange("p b e -> p (b e)")[:, bass.ds(c * (CB * E3) + (e + j * E3), 1)]
                    last = v.scalar_tensor_tensor(xc(c)[:, j, :], b4(b)[:, j, :], w, xc(c)[:, j, :], ALU.mult, ALU.add)
                last.then_inc(sem("F3_outputs_added"), 1)

            with dve.Fori(0, E3) as e:
                with dve.Fori(0, NC // 2) as i:
                    for s in range(2):
                        add(e, i * 2 + s, 4 + s)


_OUT = (B, P, P)


def kernel(**inputs):
    import numpy as _np
    import concourse.bacc as _bacc
    from concourse import mybir as _mybir
    from concourse.bass_utils import run_bass_kernel_spmd as _run

    nc = _bacc.Bacc("TRN2", target_bir_lowering=False, num_devices=1)
    arrays, aps = {}, {}
    for name, value in inputs.items():
        arr = _np.ascontiguousarray(value)
        arrays[f"in_{name}"] = arr
        aps[name] = nc.dram_tensor(f"in_{name}", arr.shape, _mybir.dt.from_np(arr.dtype), kind="ExternalInput").ap()
    out = nc.dram_tensor("out_x", _OUT, _mybir.dt.float32, kind="ExternalOutput").ap()
    flamingo(nc, aps, out)
    r = _run(nc, [arrays], core_ids=[0])
    return r.results[0]["out_x"]
```

```python
from contextlib import ExitStack

import concourse.bass as bass
from concourse import mybir

F32 = mybir.dt.float32
BF16 = mybir.dt.bfloat16
U32 = mybir.dt.uint32
I32 = mybir.dt.int32
ACT = mybir.ActivationFunctionType
ALU = mybir.AluOpType
AX = mybir.AxisListType.X

P = 128
B = 32
CB = 4
NC = B // CB
W = CB * P
HEADS = 16
D0 = P // HEADS
D3 = 64
VW0 = P + HEADS
VROW = P + HEADS * (VW0 + 1)
QUARTERS = 4
HQ = HEADS // QUARTERS
UNITS = CB * QUARTERS
DRAIN = 9
E0, I0 = 4, 64
R0 = 8
H1 = 512
K1 = H1 // P
E2 = 8
E3, H3, TOP3 = 16, 512, 4
K3 = H3 // P
TOKENS = B * P
REGION = TOKENS + P
ROW3 = P + 1
UNUSED = E3 * REGION
GROUP3 = 4
SLOTS3 = 3 * GROUP3
NT = -(-(TOKENS * TOP3 // P + E3 - 1) // SLOTS3) * SLOTS3
GROUPS3 = NT // SLOTS3
SC = CB * TOP3
NOWHERE = float(1 << 22)
EPS = 1e-5
ROUND = 1.5 * 2.0 ** 23
MASKED = -1e30
ARENA = 31000
CRED = QUARTERS + 1


class Steps:

    def __init__(self, eng, sem):
        self.eng, self.sem, self.base, self.off, self.k, self.at = eng, sem, 0, 0, 0, None

    def loop(self, per):
        self.base, self.off, self.per = self.base + self.k, 0, per
        self.k = 0

    def turn(self, i):
        assert self.k in (0, self.per), self.k
        self.off, self.k = self.per * i, 0

    def end(self, n):
        assert self.k == self.per, self.k
        self.base, self.off, self.k = self.base + self.per * n, 0, 0

    def __call__(self, ins):
        self.k += 1
        ins.then_inc(self.sem, 1)
        self.eng.wait_ge(self.sem, self.off + (self.base + self.k))

    def held(self, ins, mark):
        self(ins)
        self.eng.sem_inc(mark, 1)


def slices_at(u, kA):
    if kA <= 5:
        return [u] if u < kA else []
    return list(range(min(u * kA // (UNITS - 1), kA), min((u + 1) * kA // (UNITS - 1), kA)))


def lagging(c, p, u, lag, first, live):
    if u >= lag:
        return (c, p, u - lag) if live else None
    return None if first else (c - 1, 1 - p, u - lag + UNITS)


def flamingo(nc, a, out):
    ctx = ExitStack()
    with ctx:
        def sb(name, shape, dt=F32):
            return ctx.enter_context(nc.sbuf_tensor(name, shape, dt))

        sems = {}

        def sem(name):
            if name not in sems:
                sems[name] = ctx.enter_context(nc.semaphore(name))
            return sems[name]

        bank = [ctx.enter_context(nc.psum_tensor(f"bank{i}", [P, W], F32)) for i in range(8)]

        def b4(i):
            return bank[i][:, :].rearrange("p (j t) -> p j t", j=CB)

        x = sb("x", [P, B, P])
        ident = sb("ident", [P, P])
        ident16 = sb("ident16", [P, P], BF16)
        ones = sb("ones", [P, P])
        iota8 = sb("iota8", [P, E3])
        round3 = sb("round_constant", [P, 1])
        earlier = sb("earlier", [P, P])
        gates = sb("gates", [P, 9])
        gate3 = sb("gate3", [P, 1])
        graw = sb("graw", [P, 9])

        stats = sb("stats", [P, CB, 6])
        mv = sb("mv", [P, CB, 2])
        ve = sb("ve", [P, CB])
        mhalf = sb("mhalf", [P, CB])
        rstd = sb("rstd", [P, CB])
        xn = sb("xn", [P, CB, P])
        xnT = sb("xnT", [P, W])
        cx = sb("cx", [P, CB, P])
        cxT = sb("cxT", [P, 2, W])
        att = sb("att", [P, 3, 2, CB, P])
        sm, pr, pT = att[:, 0], att[:, 1], att[:, 2]
        nm = sb("nm", [P, 2, CB])
        sums = sb("sums", [P, CB])
        rs = sb("rs", [P, HEADS])
        tmp = sb("tmp", [P, CB, P])
        tmp2 = sb("tmp2", [P, CB, P])

        arena = sb("arena", [P, ARENA])
        used = [0]

        def fresh():
            used[0] = 0

        def ar(shape, dt=F32):
            n = 1
            for s in shape[1:]:
                n *= s
            words = n if dt != BF16 else (n + 1) // 2
            v = arena[0:shape[0], used[0]:used[0] + words]
            used[0] += words
            assert used[0] <= ARENA
            v = v if dt == F32 else v.bitcast(dt)
            if len(shape) == 3:
                v = v.rearrange("p (a b) -> p a b", a=shape[1])
            if len(shape) == 4:
                v = v.rearrange("p (a b c) -> p a b c", a=shape[1], b=shape[2])
            return v

        wq0, wkv0 = sb("wq0", [P, P]), sb("wkv0", [P, 2, 4 * D0])
        wkr0, wvs0 = sb("wkr0", [P, P]), sb("wvs0", [P, D0])
        wo0, bo0 = sb("wo0", [P, P]), sb("bo0", [P, P])
        bq0, bk0g, bk0, bv0g, bv0 = sb("bq0", [P, 1]), sb("bk0g", [P, 4]), sb("bk0", [P, 1]), sb("bv0g", [P, 4 * D0]), sb("bv0", [P, D0])
        headmask = sb("headmask", [P, HEADS])
        wr0, rb0 = sb("wr0", [P, R0]), sb("rb0", [P, R0])
        wg0, wu0 = sb("wg0", [P, E0 * I0]), sb("wu0", [P, E0 * I0])
        wd0 = sb("wd0", [P, 2, 2 * P])
        cw0, cb0 = sb("cw0", [P, 4]), sb("cb0", [P, 1])
        wT1 = sb("wT1", [P, 3, P])
        causal = sb("causal", [P, P])
        w1q, w2q = sb("w1q", [P, H1], BF16), sb("w2q", [P, K1, P], BF16)
        wsc1, wsc2 = sb("wsc1", [P, 1]), sb("wsc2", [P, 1])
        cw1, cb1 = sb("cw1", [P, K1, 3]), sb("cb1", [P, K1])
        wT2 = sb("wT2", [P, 3, P])
        bq2, bk2, bv2 = sb("bq2", [P, 1]), sb("bk2", [P, 1]), sb("bv2", [P, P])
        wg2, bg2 = sb("wg2", [P, P]), sb("bg2", [P, P])
        we2, be2 = sb("we2", [P, E2 * P]), sb("be2", [E2, P])
        gam3, bet3 = sb("gam3", [P, 1]), sb("bet3", [P, 1])
        m3 = sb("m3", [P, HEADS, P])
        wv3, wo3, bo3 = sb("wv3", [P, HEADS * D3]), sb("wo3", [P, 8, P]), sb("bo3", [P, P])
        wr3, rb3 = sb("wr3", [P, E3]), sb("rb3", [P, E3])
        b13 = sb("b13", [P, E3, K3])

        fresh()
        raw1, raw2 = ar([P, 3, P]), ar([P, 3, P])
        w1n, w2n = ar([P, K1, P]), ar([P, H1])
        wabs = ar([P, 2, H1])
        wqkn3 = ar([P, 2, HEADS * D3])
        wqkT3 = ar([P, 2, 8, P])
        kr3 = ar([E3, 2, P])
        keyT = ar([P, 2, E3])
        keysq = ar([P, E3])
        part = ar([P, 2])

        fresh()
        qT0, kT0 = ar([P, 2, W]), ar([P, 2, W])
        v0 = ar([P, 2, CB * D0])
        kbd0 = ar([P, 2, HEADS, P])
        vpad0 = ar([P, 2, VROW])
        on0, oT0 = ar([P, 2, P]), ar([P, 2, P])
        fresh()
        xall0 = ar([P, B, P])
        sg0 = ar([P, 2, W])
        hid0 = ar([P, 2, W])
        conv0, ctap0 = ar([P, CB, P]), ar([P, CB, P])
        lg0, sel0 = ar([P, CB, R0]), ar([P, CB, R0])
        top0, idx0, idf0 = ar([P, CB, 8]), ar([P, CB, 8], U32), ar([P, CB, 8])
        oh0 = ar([P, 2, CB, R0])
        wsel0, wsum0 = ar([P, 2, CB]), ar([P, CB])
        cwt0 = ar([P, CB, R0])
        ccp0 = ar([P, CB])
        fresh()
        qT1, kT1 = ar([P, W]), ar([P, W])
        v1 = ar([P, CB, P])
        fresh()
        am1, sc1 = ar([P, CB]), ar([P, CB])
        xr1 = ar([P, CB, P])
        xq1 = ar([P, CB, P], BF16)
        xqT1 = ar([P, W], BF16)
        iscb1 = ar([P, CB, P])
        sbc1 = ar([P, W])
        hs1, hc1 = ar([P, 2, CB, P]), ar([P, 2, CB, P])
        h1 = ar([P, K1, W])
        am2, sc2, isc2 = ar([P, CB]), ar([P, CB]), ar([P, CB])
        hr1 = ar([P, 2, H1])
        hq1 = ar([P, CB, H1], BF16)
        hqT1 = ar([P, 2, 2 * K1 * P], BF16)
        fresh()
        lg2, top2, idx2, idf2 = ar([P, CB, P]), ar([P, CB, 8]), ar([P, CB, 8], U32), ar([P, CB])
        ex2, pg2, oh2 = ar([P, CB, P]), ar([P, CB]), ar([P, CB, E2])
        ohT2 = ar([E2, W])
        acc2 = ar([P, CB, P])
        fresh()
        g3 = ar([P, 2, HEADS, W])
        v3 = [ar([P, CB, HEADS, D3 + 1]) for _ in range(2)]
        on3 = ar([P, 2, HEADS * D3])
        oT3 = ar([P, 8, P])
        rows3 = ar([P, SC, ROW3])
        rowsu3 = arena[:, used[0] - SC * ROW3:used[0]].bitcast(U32).rearrange("p (q d) -> p q d", q=SC)
        lg3 = ar([P, CB, E3])
        x23, es3 = ar([P, CB]), ar([P, CB])
        top3, idx3, idf3 = ar([P, CB, 8]), ar([P, CB, 8], U32), ar([P, CB, TOP3])
        ex3 = ar([P, CB, TOP3])
        wt3 = ar([P, B * TOP3])
        oh3, dst3 = ar([P, SC, E3]), ar([P, CB, E3])
        ohs3 = ar([P, CB, E3])
        to3, goes3 = ar([P, SC]), ar([P, SC])
        di3 = ar([P, SC], U32)
        run3, first3 = ar([P, E3]), ar([P, E3])
        xr3 = tmp2
        xrT3 = we2[:, 0:W]
        fresh()
        w1T3, w2T3 = ar([P, E3, H3]), ar([P, E3, H3])
        combined = arena[:, 0:2 * TOP3 * W].rearrange("p (s k j d) -> p s k j d", s=2, k=TOP3, j=CB)
        w1n3, w2n3 = ar([P, 2, K3, P]), ar([P, 2, H3])
        w1c3, w2c3, b1c3 = ar([P, 4, H3]), ar([P, 4, H3]), ar([P, 4, K3])
        cum3 = ar([P, 2, E3])
        cnt3, tl3 = ar([P, E3], I32), ar([P, E3])
        tabf3, tab3 = ar([1, 2, NT]), ar([1, 2, NT], I32)
        iota3 = ar([1, NT])
        ends3 = ar([1, E3], I32)
        at = used[0]
        xt3 = ar([P, SLOTS3, ROW3])
        xtu3 = arena[:, at:used[0]].bitcast(U32).rearrange("p (s d) -> p s d", s=SLOTS3)
        yt3 = ar([P, SLOTS3, P])
        until3 = arena[0:1, at:at + NT * E3].rearrange("p (i e) -> p i e", i=NT)
        padf3 = ar([P, ROW3])
        padu3 = arena[:, used[0] - ROW3:used[0]].bitcast(U32)
        b2b3 = att[:, 0:2].rearrange("p a s j t -> p (a s j t)")
        h3 = att[:, 2].rearrange("p s k t -> p s (k t)")
        sent = nc.dram_tensor("dispatched_rows", (UNUSED + P, ROW3), F32, kind="Internal").ap()
        sent_out = nc.dram_tensor("expert_outputs", (TOP3 * TOKENS, P), F32, kind="Internal").ap()

        rows = lambda ap, n=P: ap.rearrange("(a n) -> a n", a=1)[0].partition_broadcast(n)
        col = lambda ap: ap.rearrange("(p a) -> p a", a=1)

        SETUP_LOADS = [
            (x[:, :, :], a["x"].rearrange("b t d -> t b d")),
            (graw[:, 0:4], rows(a["g_xattn"])), (graw[:, 4:8], rows(a["g_ffn"])), (graw[:, 8:9], rows(a["L3_xattn_gate"])),
            (wq0[:, :], a["L0_xattn_Wq"]), (wkv0[:, 0, :], a["L0_xattn_Wk"]), (wkv0[:, 1, :], a["L0_xattn_Wv"]),
            (wo0[:, :], a["L0_xattn_Wo"]), (bo0[:, :], rows(a["L0_xattn_bo"])), (bq0[:, :], col(a["L0_xattn_bq"])),
            (bv0g[:, :], rows(a["L0_xattn_bv"])),
            (wr0[:, :], a["L0_ffn_Wr"]), (rb0[:, :], rows(a["L0_ffn_router_bias"])),
            (wg0[:, :].rearrange("p (e i) -> p e i", e=E0), a["L0_ffn_Wg"].rearrange("e h i -> h e i")),
            (wu0[:, :].rearrange("p (e i) -> p e i", e=E0), a["L0_ffn_Wu"].rearrange("e h i -> h e i")),
            (cw0[:, :], a["L0_ffn_conv_w"].rearrange("k a h -> h (k a)")), (cb0[:, :], col(a["L0_ffn_conv_b"])),
            (raw1[:, 0, :], a["L1_xattn_Wq"]), (raw1[:, 1, :], a["L1_xattn_Wk"]), (raw1[:, 2, :], a["L1_xattn_Wv"]),
            (w1n[:, :, :], a["L1_ffn_w1"].rearrange("(k p) d -> p k d", p=P)), (w2n[:, :], a["L1_ffn_w2"]),
            (cw1[:, :, :], a["L1_ffn_conv_w"].rearrange("(k p) a t -> p k (a t)", p=P)),
            (cb1[:, :], a["L1_ffn_conv_b"].rearrange("(k p) -> p k", p=P)),
            (raw2[:, 0, :], a["L2_xattn_Wq"]), (raw2[:, 1, :], a["L2_xattn_Wk"]), (raw2[:, 2, :], a["L2_xattn_Wv"]),
            (bq2[:, :], col(a["L2_xattn_bq"])), (bk2[:, :], col(a["L2_xattn_bk"])), (bv2[:, :], rows(a["L2_xattn_bv"])),
            (wg2[:, :], a["L2_ffn_Wg"]), (bg2[:, :], rows(a["L2_ffn_bg"])),
            (we2[:, :].rearrange("p (e f) -> p e f", e=E2), a["L2_ffn_We"].rearrange("e d f -> d e f")), (be2[:, :], a["L2_ffn_be"]),
            (gam3[:, :], col(a["L3_xattn_ln_gamma"])), (bet3[:, :], col(a["L3_xattn_ln_beta"])),
            (wqkn3[:, 0, :], a["L3_xattn_w_q"]), (wqkn3[:, 1, :], a["L3_xattn_w_kv"][:, 0:HEADS * D3]),
            (wv3[:, :], a["L3_xattn_w_kv"][:, HEADS * D3:2 * HEADS * D3]),
            (wo3[:, :, :], a["L3_xattn_w_out"].rearrange("(k p) d -> p k d", p=P)), (bo3[:, :], rows(a["L3_xattn_b_out"])),
            (kr3[:, 0, :], a["L3_ffn_keys"]), (kr3[:, 1, :], a["L3_ffn_rw"]), (rb3[:, :], rows(a["L3_ffn_rb"])),
            (b13[:, :, :], a["L3_ffn_b1"].rearrange("e (k p) -> p e k", p=P)),
        ]
        WD = []
        for e in range(E0):
            pair, u = divmod(e, 2)
            WD.append((wd0[I0 * u:I0 * u + I0, pair, P * u:P * u + P], a["L0_ffn_Wd"][e]))

        s_load, s_wd, s_zero = sem("setup_loaded"), sem("wd0_loaded"), sem("wd0_zeroed")
        s_const = sem("constants_ready")
        s_xdone = sem("x_done")
        block = ctx.enter_context(nc.Block())

        def stage_start(eng, s):
            eng.wait_ge(s_xdone, NC * s + 1)

        ATT = ("A0", "A1", "A2", "A3")
        VAR0 = {"A0": 0, "F0": NC, "A1": 2 * NC, "F1": 3 * NC, "A2": 4 * NC, "F2": 5 * NC, "A3": 6 * NC}
        XN0 = {"A0": 0, "F0": NC, "A1": 2 * NC, "A2": 3 * NC, "F2": 4 * NC, "A3": 5 * NC}
        CX0 = {st: i * NC for i, st in enumerate(ATT)}
        s_var, s_rstd, s_xn = sem("variance"), sem("inverse_deviation"), sem("normalised")
        s_cx, s_cT = sem("context_loaded"), sem("context_transposed")
        STAGE = {n: i for i, n in enumerate(("A0", "F0", "A1", "F1", "A2", "F2", "A3", "F3"))}
        n_loads = len(SETUP_LOADS) + HEADS

        @block.sync
        def _(sp):
            with nc.allow_non_contiguous_dma(reason="small vectors laid along the partitions"):
                for dst, src in SETUP_LOADS:
                    sp.dma_start(dst, src).then_inc(s_load, 16)
                for h in range(HEADS):
                    sp.dma_start(bk0g[D0 * h:D0 * h + D0, :], a["L0_xattn_bk"].rearrange("(g d) -> d g", g=4)).then_inc(s_load, 16)
            sp.wait_ge(s_zero, 1)
            for dst, src in WD:
                sp.dma_start(dst, src).then_inc(s_wd, 16)
            cview = a["ctx_1024"].rearrange("b s e -> s b e")
            for st in ATT:
                if STAGE[st]:
                    stage_start(sp, STAGE[st])
                    sp.wait_ge(s_cT, CX0[st])
                sp.dma_start(cx[:, :, :], cview[:, 0:CB, :]).then_inc(s_cx, 16)
                with sp.Fori(1, NC) as c:
                    sp.wait_ge(s_cT, c + CX0[st])
                    sp.dma_start(cx[:, :, :], cview[:, bass.ds(c * CB, CB), :]).then_inc(s_cx, 16)
            stage_start(sp, STAGE["F3"])
            s_w, s_wT = [sem("F3_weights_loaded0"), sem("F3_weights_loaded1")], sem("F3_weights_transposed")

            def load_expert(e, p):
                one = bass.ds(e, 1)
                sp.dma_start(w1n3[:, p, :, :], a["L3_ffn_w1"][one].rearrange("e (k p) d -> p (e k) d", p=P)).then_inc(s_w[p], 16)
                sp.dma_start(w2n3[:, p, :], a["L3_ffn_w2"][one].rearrange("e d f -> d (e f)")).then_inc(s_w[p], 16)

            for p in range(2):
                load_expert(p, p)
            sp.dma_start(b2b3[:, :], rows(a["L3_ffn_b2"].rearrange("e d -> (e d)"))).then_inc(sem("F3_b2_loaded"), 16)
            with sp.Fori(1, E3 // 2) as i:
                for p in range(2):
                    sp.wait_ge(s_wT, 4 * i + (2 * p - 2))
                    load_expert(i * 2 + p, p)
            sp.wait_ge(sem("F3_table"), 1)
            s_pad = sem("F3_padded")
            sp.dma_start(sent[UNUSED:UNUSED + P, :], padf3[:, :]).then_inc(s_pad, 16)
            with sp.Fori(0, E3) as e:
                end = sp.value_load(ends3[0:1, bass.ds(e, 1)], min_val=0, max_val=UNUSED - P)
                sp.dma_start(sent[bass.ds(end, P), :], padf3[:, :]).then_inc(s_pad, 16)
            sp.wait_ge(s_pad, 16 * (E3 + 1))
            sp.wait_ge(sem("F3_dispatched"), 16 * SC * NC)

            def load_tile(i, s):
                at = sp.value_load(tab3[0:1, 1, bass.ds(i, 1)], min_val=0, max_val=UNUSED)
                sp.dma_start(xt3[:, s, :], sent[bass.ds(at, P), :]).then_inc(sem(f"F3_tiles_loaded{s // GROUP3}"), 16)

            for s in range(SLOTS3):
                load_tile(s, s)
            with sp.Fori(1, GROUPS3) as g:
                for s in range(SLOTS3):
                    if s % GROUP3 == 0:
                        sp.wait_ge(sem(f"F3_scattered{s // GROUP3}"), g * (16 * GROUP3))
                    load_tile(g * SLOTS3 + s, s)
            for half in range(SLOTS3 // GROUP3):
                sp.wait_ge(sem(f"F3_scattered{half}"), GROUPS3 * GROUP3 * 16)

            s_out = sem("out_stored")

            def load_outputs(c, p):
                for k in range(TOP3):
                    sp.dma_start(combined[:, p, k, :, :], sent_out[bass.ds(c * W + k * TOKENS, W), :].rearrange("(j t) d -> t j d", t=P))\
                        .then_inc(sem(f"F3_outputs_loaded{p}"), 16)

            def store(c):
                sp.dma_start(out.rearrange("b t d -> t b d")[:, bass.ds(c * CB, CB), :], x[:, bass.ds(c * CB, CB), :]).then_inc(s_out, 16)

            for p in range(2):
                load_outputs(p, p)
            with sp.Fori(0, NC // 2 - 1) as i:
                for p in range(2):
                    sp.wait_ge(s_xdone, i * 2 + (NC * STAGE["F3"] + p + 2))
                    load_outputs(i * 2 + (p + 2), p)
                    store(i * 2 + p)
            for c in (NC - 2, NC - 1):
                sp.wait_ge(s_xdone, NC * STAGE["F3"] + c + 2)
                store(c)
            sp.wait_ge(s_out, 16 * NC)

        @block.gpsimd
        def _(pl):
            step = Steps(pl, sem("pool_steps"))
            s_held = sem("held")
            step(pl.memset(wd0[:, :, :], 0.0))
            pl.memset(rstd[:, :], 0.0).then_inc(s_zero, 1)
            step(pl.memset(ident[:, :], 0.0))
            step(pl.affine_select(out=ident[:, :], in_=ident[:, :], compare_op=ALU.not_equal, fill=1.0, base=0,
                                  pattern=[[-1, P]], channel_multiplier=1))
            pl.tensor_copy(ident16[:, :], ident[:, :])
            pl.memset(ones[:, :], 1.0)
            pl.memset(mhalf[:, :], -0.5)
            pl.memset(round3[:, :], ROUND)
            step(pl.memset(headmask[:, :], 1.0))
            step(pl.affine_select(out=headmask[:, :], in_=headmask[:, :], compare_op=ALU.is_ge, fill=0.0, base=0,
                                  pattern=[[-D0, HEADS]], channel_multiplier=1))
            step(pl.affine_select(out=headmask[:, :], in_=headmask[:, :], compare_op=ALU.is_ge, fill=0.0, base=D0 - 1,
                                  pattern=[[D0, HEADS]], channel_multiplier=-1))
            step(pl.memset(causal[:, :], 0.0))
            step(pl.affine_select(out=causal[:, :], in_=causal[:, :], compare_op=ALU.is_ge, fill=MASKED, base=0,
                                  pattern=[[1, P]], channel_multiplier=-1))
            step(pl.memset(earlier[:, :], 1.0))
            step(pl.affine_select(out=earlier[:, :], in_=earlier[:, :], compare_op=ALU.is_gt, fill=0.0, base=0,
                                  pattern=[[1, P]], channel_multiplier=-1))
            pl.iota(iota8[:, :], pattern=[[1, E3]], base=0, channel_multiplier=0, allow_small_or_imprecise_dtypes=True).then_inc(s_const, 1)

            def power(st, n):
                pl.wait_ge(s_var, n + (1 + VAR0[st]))
                pl.tensor_tensor(rstd[:, :], ve[:, :], mhalf[:, :], ALU.pow).then_inc(s_rstd, 1)

            pl.wait_ge(sem("setup_done"), 1)
            step(pl.memset(vpad0[:, :, :], 0.0))
            for s in range(2):
                pl.memset(vpad0[:, s, P:P + HEADS * (VW0 + 1)].rearrange("p (h r) -> p h r", r=VW0 + 1)[:, :, 0:1], 1.0)
            power("A0", 0)
            power("A0", 1)

            def spread(c, p, more):
                for j in range(CB):
                    s = j % 2
                    if j == 0:
                        pl.wait_ge(sem("A0_kv_ready"), c + 1)
                    pl.wait_ge(sem("A0_pv_done"), (c * UNITS + QUARTERS * j) + (CRED - QUARTERS))
                    pl.tensor_tensor(kbd0[:, s, :, :], kT0[:, p, j * P:j * P + P].unsqueeze(1).to_broadcast([P, HEADS, P]),
                                     headmask[:, :].unsqueeze(2).to_broadcast([P, HEADS, P]), ALU.mult)
                    pl.tensor_tensor(vpad0[:, s, 0:HEADS * (VW0 + D0)].rearrange("p (h r) -> p h r", r=VW0 + D0)[:, :, 0:D0],
                                     v0[:, p, j * D0:j * D0 + D0].unsqueeze(1).to_broadcast([P, HEADS, D0]),
                                     bv0[:, :].unsqueeze(1).to_broadcast([P, HEADS, D0]), ALU.add).then_inc(sem("A0_spread"), 1)
                    if j == 0 and more:
                        power("A0", c + 2)

            with pl.Fori(0, NC // 2 - 1) as i:
                for p in range(2):
                    spread(i * 2 + p, p, True)
            spread(NC - 2, 0, False)
            spread(NC - 1, 1, False)

            stage_start(pl, STAGE["F0"])
            with pl.Fori(0, NC) as c:
                pl.wait_ge(s_var, c + (1 + VAR0["F0"]))
                pl.tensor_tensor(rstd[:, :], ve[:, :], mhalf[:, :], ALU.pow).then_inc(s_rstd, 1)
                pl.wait_ge(s_xn, c + (1 + XN0["F0"]))
                pl.tensor_copy(xall0[:, bass.ds(c * CB, CB), :], xn[:, :, :]).then_inc(sem("F0_xn_kept"), 1)
                pl.wait_ge(sem("F0_xnT"), c + 1)
                pl.wait_ge(sem("F0_convT"), c + 1)
                pl.sem_inc(s_held, 1)
                xv = xnT[:, :].rearrange("p (j t) -> p j t", j=CB)
                pl.tensor_scalar(conv0[:, :, :], xv, cw0[:, 3:4], cb0[:, 0:1], ALU.mult, ALU.add)
                for k in range(3):
                    lag = 3 - k
                    n = P - lag
                    pl.tensor_scalar(ctap0[:, :, 0:n], xv[:, :, 0:n], cw0[:, k:k + 1], None, ALU.mult).then_inc(sem("F0_tap"), 1)
                    pl.wait_ge(sem("F0_tap"), c * 6 + (2 * k + 1))
                    t = pl.tensor_tensor(conv0[:, :, lag:P], conv0[:, :, lag:P], ctap0[:, :, 0:n], ALU.add)
                    t.then_inc(sem("F0_tap") if k < 2 else sem("F0_conv"), 1)
                    if k < 2:
                        pl.wait_ge(sem("F0_tap"), c * 6 + (2 * k + 2))
                        pl.sem_inc(s_held, 1)
                    else:
                        pl.sem_inc(sem("F0_tap"), 1)

            with pl.Fori(0, NC) as c:
                power("A1", c)
            with pl.Fori(0, NC) as c:
                power("F1", c)
                pl.wait_ge(sem("F1_scale1"), c + 1)
                pl.wait_ge(sem("F1_scaleT"), c + 1)
                pl.sem_inc(s_held, 1)
                pl.tensor_copy(iscb1[:, :, :], am1[:, :].unsqueeze(2).to_broadcast([P, CB, P])).then_inc(sem("F1_scale_spread"), 1)
            with pl.Fori(0, NC) as c:
                power("A2", c)
            with pl.Fori(0, NC) as c:
                power("F2", c)
            stage_start(pl, STAGE["A3"])
            pl.iota(goes3[:, :].rearrange("p (j k) -> p j k", j=CB), pattern=[[P, CB], [TOKENS, TOP3]], base=0, channel_multiplier=1,
                    allow_small_or_imprecise_dtypes=True)
            pl.iota(first3[:, :], pattern=[[REGION, E3]], base=0, channel_multiplier=0, allow_small_or_imprecise_dtypes=True)\
                .then_inc(sem("F3_constants"), 1)
            pl.sem_inc(sem("F3_rows_free"), 1)

            def dispatch(c):
                pl.wait_ge(sem("F3_variance"), c + 1)
                pl.tensor_tensor(rstd[:, :], ve[:, :], mhalf[:, :], ALU.pow).then_inc(sem("F3_inverse_deviation"), 1)
                pl.wait_ge(sem("F3_rows_copied"), c + 2)
                pl.wait_ge(sem("F3_rows_ready"), c + 1)
                pl.sem_inc(s_held, 1)
                for q in range(SC):
                    pl.indirect_dma_start(sent, bass.IndirectOffsetOnAxis(di3[:, q:q + 1], 0), rows3[:, q, :], None)\
                        .then_inc(sem("F3_dispatched"), 16)
                pl.wait_ge(sem("F3_dispatched"), c * (16 * SC) + 16 * SC)
                pl.sem_inc(sem("F3_rows_free"), 1)

            for n in range(6):
                power("A3", n)
            with pl.Fori(0, NC - 3) as c:
                power("A3", c * 2 + 6)
                power("A3", c * 2 + 7)
                dispatch(c)
            dispatch(NC - 3)
            dispatch(NC - 2)
            dispatch(NC - 1)

            stage_start(pl, STAGE["F3"])
            pl.iota(iota3[:, :], pattern=[[1, NT]], base=0, channel_multiplier=0, allow_small_or_imprecise_dtypes=True)
            pl.memset(padf3[:, :], 0.0).then_inc(sem("F3_constants"), 1)
            with pl.Fori(0, GROUPS3) as g:
                for s in range(SLOTS3):
                    pl.wait_ge(sem("F3_output"), g * SLOTS3 + (s + 3))
                    pl.sem_inc(s_held, 1)
                    pl.indirect_dma_start(sent_out, bass.IndirectOffsetOnAxis(xtu3[:, s, P:P + 1], 0), yt3[:, s, :], None,
                                          bounds_check=TOP3 * TOKENS - 1, oob_is_err=False).then_inc(sem(f"F3_scattered{s // GROUP3}"), 16)

        @block.tensor
        def _(pe):
            pe.wait_ge(s_const, 1)
            pe.wait_ge(s_load, 16 * n_loads)
            s_bk, s_gone = sem("setup_bank_full"), sem("setup_bank_gone")
            n = [0]

            def group(pairs):
                i = n[0]
                if i >= 8:
                    pe.wait_ge(s_gone, i - 7)
                for q, (src, parts) in enumerate(pairs):
                    last = nc.tensor.transpose(bank[i % 8][:, q * parts:(q + 1) * parts], src, ident[0:parts, 0:parts])
                last.then_inc(s_bk, 1)
                n[0] += 1

            group([(raw1[:, i, :], P) for i in range(3)])
            group([(raw2[:, i, :], P) for i in range(3)])
            for t in range(2):
                for half in range(2):
                    group([(wqkn3[:, t, (4 * half + q) * P:(4 * half + q + 1) * P], P) for q in range(4)])
            group([(kr3[:, t, :], E3) for t in range(2)])
            pe.wait_ge(s_gone, 6)
            for qd in range(4):
                i = n[0]
                if i >= 8:
                    pe.wait_ge(s_gone, i - 7)
                for u in range(HQ):
                    h = 8 * (qd // 2) + 2 * u + qd % 2
                    r = slice(D3 * (h % 2), D3 * (h % 2) + D3)
                    last = nc.tensor.matmul(bank[i % 8][:, u * P:u * P + P], wqkT3[r, 0, h // 2, :], wqkT3[r, 1, h // 2, :], start=True, stop=True)
                last.then_inc(s_bk, 1)
                n[0] += 1
            pe.wait_ge(sem("setup_abs"), 1)
            pe.wait_ge(s_gone, n[0] - 7)
            nc.tensor.matmul(bank[n[0] % 8][:, 0:2], ones[:, :], part[:, :], start=True, stop=True).then_inc(s_bk, 1)
            n[0] += 1
            pe.wait_ge(sem("setup_keysq"), 1)
            pe.wait_ge(s_gone, n[0] - 7)
            nc.tensor.matmul(bank[n[0] % 8][:, 0:E3], ones[:, :], keysq[:, :], start=True, stop=True).then_inc(s_bk, 1)
            n[0] += 1
            pe.wait_ge(sem("setup_ternary"), 1)
            group([(wabs[:, 0, q * P:(q + 1) * P], P) for q in range(4)])
            group([(wabs[:, 1, q * P:(q + 1) * P], P) for q in range(4)])
            pe.wait_ge(sem("setup_done"), 1)

            def transpose_x(st, c):
                pe.wait_ge(s_xn, c + (1 + XN0[st]))
                for j in range(CB):
                    last = nc.tensor.transpose(bank[0][:, j * P:j * P + P], xn[:, j, :], ident[:, :])
                return last

            def routing(c, u):
                if u == 8:
                    pe.wait_ge(sem("F3_normalised"), c + 1)
                    for j in range(CB):
                        last = nc.tensor.transpose(bank[5][:, j * P:j * P + P], xr3[:, j, :], ident[:, :])
                    last.then_inc(sem("F3_xT"), 1)
                if u == 9:
                    pe.wait_ge(sem("F3_xnT"), c + 1)
                    for j in range(CB):
                        last = nc.tensor.matmul(bank[5][:, j * E3:j * E3 + E3], xrT3[:, j * P:j * P + P], wr3[:, :], start=True, stop=True)
                    last.then_inc(sem("F3_lg"), 1)
                if u == 12:
                    pe.wait_ge(sem("F3_chosen"), c + 1)
                    chosen = ohs3[:, :, :].rearrange("p j e -> p (j e)")
                    nc.tensor.matmul(bank[5][:, 0:CB * E3], earlier[:, :], chosen, start=True, stop=True)
                    nc.tensor.matmul(bank[5][:, CB * E3:2 * CB * E3], ones[:, :], chosen, start=True, stop=True).then_inc(sem("F3_counts"), 1)

            def heads(st):
                l0 = st == "A0"
                kA = 5 if l0 else 2 + HEADS + 2 * CB
                A = bank[6]

                def piece(c, p, s):
                    pe.wait_ge(sem(st + "_slice_gone"), c * kA + (s + 1))
                    if s == 0:
                        pe.wait_ge(s_xn, c + (1 + XN0[st]))
                        for j in range(CB):
                            last = nc.tensor.transpose(A[:, j * P:j * P + P], xn[:, j, :], ident[:, :])
                        last.then_inc(sem(st + "_slice"), 1)
                        return
                    if s == 1:
                        pe.wait_ge(s_cx, c * 16 + (16 + 16 * CX0[st]))
                        for j in range(CB):
                            last = nc.tensor.transpose(A[:, j * P:j * P + P], cx[:, j, :], ident[:, :])
                        last.then_inc(sem(st + "_slice"), 1)
                        return
                    pe.wait_ge(sem(st + "_xnT"), c + 1)
                    if l0 and s == 2:
                        last = nc.tensor.matmul(A[:, :], wq0[:, :], xnT[:, :], start=True, stop=True)
                    elif l0 and s == 3:
                        pe.wait_ge(sem(st + "_cxT"), c + 1)
                        last = nc.tensor.matmul(A[:, :], wkr0[:, :], cxT[:, p, :], start=True, stop=True)
                    elif l0:
                        for j in range(CB):
                            last = nc.tensor.matmul(A[:, j * D0:j * D0 + D0], cxT[:, p, j * P:j * P + P], wvs0[:, :], start=True, stop=True)
                    elif s < 2 + HEADS:
                        last = nc.tensor.matmul(A[:, :], m3[:, s - 2, :], xnT[:, :], start=True, stop=True)
                    else:
                        j, half = divmod(s - 2 - HEADS, 2)
                        pe.wait_ge(sem(st + "_cxT"), c + 1)
                        last = nc.tensor.matmul(A[:, :], cxT[:, p, j * P:j * P + P], wv3[:, half * W:half * W + W], start=True, stop=True)
                    last.then_inc(sem(st + "_slice"), 1)

                def body(c, p, more, first=False, live=True):
                    for u in range(UNITS if live else DRAIN):
                        if live:
                            j, qd = divmod(u, QUARTERS)
                            pe.wait_ge(sem(st + "_less_max"), c * UNITS + (u - 1 + CRED))
                            if u == 0:
                                pe.wait_ge(sem(st + "_slices_ready"), c + 1)
                            if l0:
                                if qd == 0:
                                    pe.wait_ge(sem("A0_spread"), c * CB + (j + 1))
                                nc.tensor.matmul(bank[u % 2][:, :], qT0[:, p, j * P:j * P + P], kbd0[:, j % 2, qd * HQ:(qd + 1) * HQ, :],
                                                 start=True, stop=True).then_inc(sem(st + "_scores"), 1)
                            else:
                                for i in range(HQ):
                                    last = nc.tensor.matmul(bank[u % 2][:, i * P:i * P + P], g3[:, p, qd * HQ + i, j * P:j * P + P],
                                                            cxT[:, p, j * P:j * P + P], start=True, stop=True)
                                last.then_inc(sem(st + "_scores"), 1)
                        mine = slices_at(u, kA) if more else []
                        for s in mine[:1]:
                            piece(c + 1, 1 - p, s)
                        unit = lagging(c, p, u, 2, first, live)
                        if unit:
                            cc, pp, v = unit
                            j, qd = divmod(v, QUARTERS)
                            pe.wait_ge(sem(st + "_pT"), cc * UNITS + (v + 1 + CRED))
                            if l0:
                                if qd == 0:
                                    pe.wait_ge(sem("A0_normal"), cc * CB + (j + 1))
                                for i in range(HQ):
                                    h = qd * HQ + i
                                    last = nc.tensor.matmul(bank[4][:, 0:VW0], pT[:, v % 2, i, :], vpad0[:, j % 2, h * VW0:h * VW0 + VW0],
                                                            start=(h == 0), stop=(h == HEADS - 1))
                            else:
                                pe.wait_ge(sem("A3_normal"), cc * UNITS + (v + 1))
                                for i in range(HQ):
                                    last = nc.tensor.matmul(bank[4][:, i * (D3 + 1):(i + 1) * (D3 + 1)], pT[:, v % 2, i, :],
                                                            v3[pp][:, j, qd * HQ + i, :], start=True, stop=True)
                            last.then_inc(sem(st + "_pv_done"), 1)
                        unit = lagging(c, p, u, 1, first, live)
                        if unit:
                            cc, pp, v = unit
                            pe.wait_ge(sem(st + "_exp"), cc * UNITS + (v + 1 + CRED))
                            pe.wait_ge(sem(st + "_pT"), cc * UNITS + (v - 1 + CRED))
                            for i in range(HQ):
                                last = nc.tensor.transpose(bank[2 + v % 2][:, i * P:i * P + P], pr[:, v % 2, i, :], ident[:, :])
                            last.then_inc(sem(st + "_pT_full"), 1)
                        for s in mine[1:]:
                            piece(c + 1, 1 - p, s)
                        if not l0 and not first:
                            if u in (8, 12) and live:
                                pe.wait_ge(sem("A3_oT"), c * (2 * CB) + (3 if u == 8 else 5))
                            if live:
                                routing(c - 1, u)
                            if u == 10 and live:
                                pe.wait_ge(sem("F3_chosen"), c)
                            if u == 14 and live:
                                pe.wait_ge(sem("F3_rows_ready"), c)
                        for part_, lag in enumerate((6,) if l0 else (6, 7)):
                            unit = lagging(c, p, u, lag, first, live)
                            if unit and unit[2] % QUARTERS == 0:
                                cc, j = unit[0], unit[2] // QUARTERS
                                if l0:
                                    pe.wait_ge(sem("A0_normal"), cc * CB + (j + 2))
                                    pe.wait_ge(sem("A0_oT"), cc * CB + (j + 1))
                                    nc.tensor.transpose(bank[5][:, 0:P], on0[:, j % 2, :], ident[:, :]).then_inc(sem("A0_oT_full"), 1)
                                else:
                                    pe.wait_ge(sem("A3_normal"), cc * UNITS + (QUARTERS * (j + 1) + 1))
                                    pe.wait_ge(sem("A3_oT"), cc * (2 * CB) + (2 * j + part_ + 1))
                                    for q in range(4):
                                        k = 4 * part_ + q
                                        last = nc.tensor.transpose(bank[5][:, q * P:q * P + P], on3[:, j % 2, k * P:k * P + P], ident[:, :])
                                    last.then_inc(sem("A3_oT_full"), 1)
                        unit = lagging(c, p, u, 7 if l0 else 8, first, live)
                        if unit and unit[2] % QUARTERS == 0:
                            cc, j = unit[0], unit[2] // QUARTERS
                            if j == 0:
                                pe.wait_ge(s_xdone, cc + (NC * STAGE[st] + 1))
                            if l0:
                                pe.wait_ge(sem("A0_oT"), cc * CB + (j + 2))
                                nc.tensor.matmul(bank[7][:, j * P:j * P + P], oT0[:, j % 2, :], wo0[:, :], start=True, stop=True)\
                                    .then_inc(sem(st + "_y"), 1)
                            else:
                                pe.wait_ge(sem("A3_oT"), cc * (2 * CB) + (2 * j + 3))
                                for k in range(8):
                                    last = nc.tensor.matmul(bank[7][:, j * P:j * P + P], oT3[:, k, :], wo3[:, k, :], start=(k == 0), stop=(k == 7))
                                last.then_inc(sem(st + "_y"), 1)

                for s in range(kA):
                    piece(0, 0, s)
                body(0, 0, True, True)
                with pe.Fori(0, NC // 2 - 2) as i:
                    for p in range(2):
                        body(i * 2 + (p + 1), 1 - p, True)
                body(NC - 3, 1, True)
                body(NC - 2, 0, True)
                body(NC - 1, 1, False)
                body(NC, 0, False, live=False)

            heads("A0")

            stage_start(pe, STAGE["F0"])

            def f0(c):
                transpose_x("F0", c).then_inc(sem("F0_xT"), 1)
                pe.wait_ge(sem("F0_xnT"), c + 1)
                pe.wait_ge(sem("F0_tanh"), c + 1)
                for j in range(CB):
                    last = nc.tensor.matmul(bank[5][:, j * R0:j * R0 + R0], xnT[:, j * P:j * P + P], wr0[:, :], start=True, stop=True)
                last.then_inc(sem("F0_router"), 1)
                for k in range(2):
                    pe.wait_ge(sem("F0_silu"), c * 2 + (k + 1))
                    nc.tensor.matmul(bank[1 + 2 * k][:, :], wg0[:, k * P:k * P + P], xnT[:, :], start=True, stop=True).then_inc(sem("F0_gate"), 1)
                    pe.wait_ge(sem("F0_hid"), c * 2 + (k + 1))
                    nc.tensor.matmul(bank[2 + 2 * k][:, :], wu0[:, k * P:k * P + P], xnT[:, :], start=True, stop=True).then_inc(sem("F0_up"), 1)
                pe.wait_ge(sem("F0_conv"), c + 2)
                for j in range(CB):
                    last = nc.tensor.transpose(bank[0][:, j * P:j * P + P], conv0[:, j, :], ident[:, :])
                last.then_inc(sem("F0_convT"), 1)
                pe.wait_ge(sem("F0_hid"), c * 2 + 4)
                for j in range(CB):
                    pe.wait_ge(sem("F0_down_read"), c * CB + (j + 1))
                    for k in range(2):
                        last = nc.tensor.matmul(bank[6 + j % 2][:, k * 2 * P:(k + 1) * 2 * P], hid0[:, k, j * P:j * P + P], wd0[:, k, :],
                                                start=True, stop=True)
                    last.then_inc(sem("F0_down"), 1)

            pe.wait_ge(s_wd, 64)
            f0(0)
            with pe.Fori(1, NC) as c:
                pe.wait_ge(sem("F0_conv_read"), c)
                f0(c)

            def single(st):
                before = 0 if st == "A1" else NC
                stage_start(pe, STAGE[st])
                wT = wT1 if st == "A1" else wT2

                def front(c, first, back):
                    if not first:
                        pe.wait_ge(sem("A12_xnT"), c + before)
                    transpose_x(st, c).then_inc(sem("A12_xT"), 1)
                    pe.wait_ge(s_cx, c * 16 + (16 + 16 * CX0[st]))
                    if not first:
                        pe.wait_ge(sem("A12_cxT"), c + before)
                    for j in range(CB):
                        last = nc.tensor.transpose(bank[1][:, j * P:j * P + P], cx[:, j, :], ident[:, :])
                    last.then_inc(s_cT, 1)
                    if back and st == "A2":
                        probs_T(c - 1)
                    pe.wait_ge(sem("A12_xnT"), c + 1 + before)
                    if not first:
                        pe.wait_ge(sem("A12_qT"), c + before)
                    nc.tensor.matmul(bank[2][:, :], wT[:, 0, :], xnT[:, :], start=True, stop=True).then_inc(sem("A12_q"), 1)
                    pe.wait_ge(sem("A12_cxT"), c + 1 + before)
                    if not first:
                        pe.wait_ge(sem("A12_kT"), c + before)
                    nc.tensor.matmul(bank[3][:, :], wT[:, 1, :], cxT[:, 0, :], start=True, stop=True).then_inc(sem("A12_k"), 1)
                    if back:
                        pv(c - 1)
                    if not first:
                        pe.wait_ge(sem("A12_v_sb"), c + before)
                    for j in range(CB):
                        last = nc.tensor.matmul(bank[4][:, j * P:j * P + P], cxT[:, 0, j * P:j * P + P], wT[:, 2, :], start=True, stop=True)
                    last.then_inc(sem("A12_v"), 1)
                    pe.wait_ge(sem("A12_qT"), c + 1 + before)
                    pe.wait_ge(sem("A12_kT"), c + 1 + before)
                    if not first:
                        pe.wait_ge(sem(st + "_less_max"), c)
                    for j in range(CB):
                        js = slice(j * P, j * P + P)
                        lhs, rhs = (kT1, qT1) if st == "A1" else (qT1, kT1)
                        last = nc.tensor.matmul(bank[7][:, js], lhs[:, js], rhs[:, js], start=True, stop=True)
                    last.then_inc(sem("A12_scores"), 1)

                def probs_T(c):
                    pe.wait_ge(sem("A12_exp"), c + 1 + before)
                    for j in range(CB):
                        last = nc.tensor.transpose(bank[5][:, j * P:j * P + P], pr[:, 0, j, :], ident[:, :])
                    last.then_inc(sem(st + "_pT_full"), 1)

                def pv(c):
                    pe.wait_ge(sem("A12_v_sb"), c + 1 + before)
                    if st == "A1":
                        pe.wait_ge(sem(st + "_normal"), c + 1)
                        src = pr
                    else:
                        pe.wait_ge(sem(st + "_pT"), c + 1)
                        src = pT
                    for j in range(CB):
                        last = nc.tensor.matmul(bank[6][:, j * P:j * P + P], src[:, 0, j, :], v1[:, j, :], start=True, stop=True)
                    last.then_inc(sem("A12_pv_done"), 1)

                front(0, True, False)
                with pe.Fori(1, NC) as c:
                    front(c, False, True)
                if st == "A2":
                    probs_T(NC - 1)
                pv(NC - 1)

            single("A1")

            stage_start(pe, STAGE["F1"])

            b0h = bank[0][:, :].bitcast(BF16)

            def up1(c, first):
                pe.wait_ge(sem("F1_xq"), c + 1)
                if not first:
                    pe.wait_ge(sem("F1_hqT"), c * 2 - 1)
                for j in range(CB):
                    last = nc.tensor.transpose(b0h[:, j * P:j * P + P], xq1[:, j, :], ident16[:, :])
                last.then_inc(sem("F1_xT"), 1)
                pe.wait_ge(sem("F1_xqT"), c + 1)
                up1_products(c, first, (0, 1))

            def up1_products(c, first, ks):
                for k in ks:
                    if not first:
                        pe.wait_ge(sem("F1_hs"), c * K1 + (k + 1 - K1))
                    nc.tensor.matmul(bank[1 + k][:, :], w1q[:, k * P:k * P + P], xqT1[:, :], start=True, stop=True).then_inc(sem("F1_h"), 1)

            def scales(c):
                pe.wait_ge(sem("F1_scale_spread"), c + 1)
                for j in range(CB):
                    last = nc.tensor.transpose(bank[0][:, j * P:j * P + P], iscb1[:, j, :], ident[:, :])
                last.then_inc(sem("F1_scaleT"), 1)

            def tokens_back(c, j):
                pe.wait_ge(sem("F1_round2"), c * CB + (j + 1))
                for k in range(K1):
                    last = nc.tensor.transpose(bank[6 + j % 2][:, k * P:k * P + P], h1[:, k, j * P:j * P + P], ident[:, :])
                last.then_inc(sem("F1_hT"), 1)

            def f1(c, more):
                pe.wait_ge(sem("F1_silu"), c * K1 + K1)
                tokens_back(c, 0)
                tokens_back(c, 1)
                if more:
                    up1(c + 1, False)
                tokens_back(c, 2)
                tokens_back(c, 3)
                if more:
                    scales(c + 1)
                    up1_products(c + 1, False, (2, 3))
                for q in range(2):
                    pe.wait_ge(sem("F1_hq"), c * CB + (2 * q + 4))
                    if q == 0:
                        pe.wait_ge(sem("F1_sbc"), c + (2 if more else 1))
                    pe.wait_ge(sem("F1_hqT"), c * 2 + (q + 1))
                    for k in range(2 * K1):
                        last = nc.tensor.transpose(b0h[:, k * P:k * P + P], hq1[:, 2 * q + k // K1, k % K1 * P:k % K1 * P + P], ident16[:, :])
                    last.then_inc(sem("F1_hqT_full"), 1)
                    pe.wait_ge(sem("F1_hqT"), c * 2 + (q + 2))
                    if q == 0:
                        pe.wait_ge(s_xdone, c + (NC * STAGE["F1"] + 1))
                    for j in (2 * q, 2 * q + 1):
                        for k in range(K1):
                            kk = j % 2 * K1 + k
                            last = nc.tensor.matmul(bank[5][:, j * P:j * P + P], hqT1[:, q, kk * P:kk * P + P], w2q[:, k, :],
                                                    start=(k == 0), stop=(k == K1 - 1))
                    last.then_inc(sem("F1_y"), 1)

            up1(0, True)
            scales(0)
            up1_products(0, True, (2, 3))
            with pe.Fori(0, NC - 1) as c:
                f1(c, True)
            f1(NC - 1, False)

            single("A2")

            stage_start(pe, STAGE["F2"])

            def f2(c):
                transpose_x("F2", c).then_inc(sem("F2_xT"), 1)
                pe.wait_ge(sem("F2_xnT"), c + 1)
                pe.wait_ge(sem("F2_logits_read"), c + 1)
                for j in range(CB):
                    last = nc.tensor.matmul(bank[1][:, j * P:j * P + P], xnT[:, j * P:j * P + P], wg2[:, :], start=True, stop=True)
                last.then_inc(sem("F2_logits"), 1)
                pe.wait_ge(sem("F2_onehot"), c + 1)
                for j in range(CB):
                    last = nc.tensor.transpose(bank[6][0:E2, j * P:j * P + P], oh2[:, j, :], ident[:, :])
                last.then_inc(sem("F2_ohT_full"), 1)
                pe.wait_ge(sem("F2_ohT"), c + 1)
                for j in range(CB):
                    last = nc.tensor.matmul(bank[7][:, j * P:j * P + P], ohT2[:, j * P:j * P + P], be2[:, :], start=True, stop=True)
                last.then_inc(sem("F2_bias"), 1)
                for j in range(CB):
                    for half in range(2):
                        pe.wait_ge(sem("F2_z_read"), c * (2 * CB) + (2 * j + half + 1))
                        nc.tensor.matmul(bank[2 + (2 * j + half) % 4][:, :], xnT[:, j * P:j * P + P], we2[:, half * W:half * W + W],
                                         start=True, stop=True).then_inc(sem("F2_z"), 1)

            f2(0)
            with pe.Fori(1, NC) as c:
                pe.wait_ge(sem("F2_xnT"), c)
                f2(c)

            stage_start(pe, STAGE["A3"])
            heads("A3")

            stage_start(pe, STAGE["F3"])

            def expert_T(e, p):
                pe.wait_ge(sem(f"F3_weights_loaded{p}"), e * 16 + (32 - 16 * p))
                pe.wait_ge(sem("F3_w_sb"), e * 2 + 1)
                for k in range(K3):
                    last = nc.tensor.transpose(bank[2 * p][:, k * P:k * P + P], w1n3[:, p, k, :], ident[:, :])
                last.then_inc(sem("F3_weights_transposed"), 1)
                pe.wait_ge(sem("F3_w_sb"), e * 2 + 2)
                for k in range(K3):
                    last = nc.tensor.transpose(bank[2 * p + 1][:, k * P:k * P + P], w2n3[:, p, k * P:k * P + P], ident[:, :])
                last.then_inc(sem("F3_weights_transposed"), 1)

            routing(NC - 1, 8)
            for e in range(2):
                expert_T(e, e)
            routing(NC - 1, 9)
            for e in range(2, 4):
                expert_T(e, e % 2)
            routing(NC - 1, 12)
            with pe.Fori(2, E3 // 2) as i:
                for p in range(2):
                    expert_T(i * 2 + p, p)

            def tile_T(turn, s):
                pe.wait_ge(sem(f"F3_tiles_loaded{s % SLOTS3 // GROUP3}"), turn * (16 * GROUP3) + 16 * GROUP3)
                nc.tensor.transpose(bank[6 + s % 2][:, 0:P], xt3[:, s % SLOTS3, 0:P], ident[:, :]).then_inc(sem("F3_tile_T"), 1)

            def up(n, s):
                pe.wait_ge(sem("F3_tile_xT"), n + 1)
                pe.wait_ge(sem("F3_tile_weights"), n + 1)
                for k in range(K3):
                    last = nc.tensor.matmul(bank[s % 2][:, k * P:k * P + P], w1c3[:, s % 4, k * P:k * P + P],
                                            xnT[:, (s % 4) * P:(s % 4) * P + P], start=True, stop=True)
                last.then_inc(sem("F3_up"), 1)

            def down(n, s):
                pe.wait_ge(sem("F3_gelu"), n + 1)
                pe.wait_ge(sem("F3_output"), n + 1)
                for k in range(K3):
                    last = nc.tensor.matmul(bank[2 + s % 2][:, 0:P], h3[:, s % 2, k * P:k * P + P], w2c3[:, s % 4, k * P:k * P + P],
                                            start=(k == 0), stop=(k == K3 - 1))
                last.then_inc(sem("F3_down"), 1)

            pe.wait_ge(sem("F3_w_sb"), 2 * E3 + 4)
            tile_T(0, 0)
            tile_T(0, 1)
            up(0, 0)
            with pe.Fori(0, GROUPS3 - 1) as g:
                for s in range(SLOTS3):
                    tile_T(g + (s + 2) // SLOTS3, s + 2)
                    up(g * SLOTS3 + (s + 1), s + 1)
                    down(g * SLOTS3 + s, s)
            for s in range(SLOTS3):
                n = NT - SLOTS3 + s
                if n + 2 < NT:
                    tile_T(GROUPS3 - 1, s + 2)
                if n + 1 < NT:
                    up(n + 1, s + 1)
                down(n, s)

        @block.scalar
        def _(act):
            copy = lambda o, i: nc.scalar.activation(o, i, ACT.Copy)
            aff = lambda o, i, s, b: nc.scalar.activation(o, i, ACT.Identity, bias=b, scale=s)
            exp = lambda o, i: nc.scalar.activation(o, i, ACT.Exp)
            act.wait_ge(s_load, 16 * n_loads)
            s_bk, s_gone = sem("setup_bank_full"), sem("setup_bank_gone")
            nc.scalar.activation(gates[:, :], graw[:, :], ACT.Tanh).then_inc(sem("setup_gates"), 1)
            n = [0]

            def out_of_bank(dst, cols, scale=1.0):
                act.wait_ge(s_bk, n[0] + 1)
                src = bank[n[0] % 8][:, 0:cols]
                if len(dst.shape) == 3:
                    src = src.rearrange("p (a b) -> p a b", a=dst.shape[1])
                nc.scalar.activation(dst, src, ACT.Copy, scale=scale).then_inc(s_gone, 1)
                n[0] += 1

            out_of_bank(wT1[:, :, :], 3 * P)
            out_of_bank(wT2[:, :, :], 3 * P)
            for t in range(2):
                for half in range(2):
                    out_of_bank(wqkT3[:, t, 4 * half:4 * half + 4, :], W)
            out_of_bank(keyT[:, :, :], 2 * E3)
            for qd in range(4):
                out_of_bank(m3[:, 8 * (qd // 2) + qd % 2:8 * (qd // 2) + 8:2, :], W, scale=float(D3) ** -0.5)
            act.wait_ge(sem("setup_wscale"), 1)
            n[0] += 2
            out_of_bank(w1q[:, :], W)
            out_of_bank(w2q[:, :, :], W)
            act.wait_ge(sem("setup_done"), 1)

            def routing(c, u):
                if u == 8:
                    act.wait_ge(sem("F3_xT"), c + 1)
                    copy(xrT3, b4(5).rearrange("p j t -> p (j t)")).then_inc(sem("F3_xnT"), 1)
                    act.wait_ge(sem("F3_rows_free"), c + 1)
                    copy(rows3[:, :, 0:P].rearrange("p (j k) d -> p j k d", j=CB), xr3[:, :, :].unsqueeze(2).to_broadcast([P, CB, TOP3, P]))\
                        .then_inc(sem("F3_rows_copied"), 1)
                if u == 10:
                    act.wait_ge(sem("F3_less_max"), c + 1)
                    exp(ex3[:, :, :], top3[:, :, 0:TOP3]).then_inc(sem("F3_exp"), 1)

            def heads(st):
                l0 = st == "A0"
                kA = 5 if l0 else 2 + HEADS + 2 * CB
                A = bank[6]

                def piece(c, p, s):
                    act.wait_ge(sem(st + "_slice"), c * kA + (s + 1))
                    gone = sem(st + "_slice_gone")
                    if s == 0:
                        if l0:
                            copy(xnT[:, :], A[:, :]).then_inc(sem(st + "_xnT"), 1)
                        else:
                            aff(xnT[:, :], A[:, :], gam3[:, 0:1], bet3[:, 0:1]).then_inc(sem(st + "_xnT"), 1)
                        act.wait_ge(sem(st + "_xnT"), c + 1)
                        act.sem_inc(gone, 1)
                        return
                    if s == 1:
                        copy(cxT[:, p, :], A[:, :]).then_inc(sem(st + "_cxT"), 1)
                        act.wait_ge(sem(st + "_cxT"), c + 1)
                        act.sem_inc(gone, 1)
                        act.sem_inc(s_cT, 1)
                        return
                    if l0 and s == 2:
                        i = aff(qT0[:, p, :], A[:, :], float(D0) ** -0.5, bq0[:, 0:1])
                    elif l0 and s == 3:
                        i = aff(kT0[:, p, :], A[:, :], 1.0, bk0[:, 0:1])
                    elif l0:
                        i = copy(v0[:, p, :], A[:, 0:CB * D0])
                    elif s < 2 + HEADS:
                        i = copy(g3[:, p, s - 2, :], A[:, :])
                    else:
                        j, half = divmod(s - 2 - HEADS, 2)
                        i = copy(v3[p][:, j, 8 * half:8 * half + 8, 0:D3], A[:, :].rearrange("p (h d) -> p h d", d=D3))
                    i.then_inc(gone, 1)
                    if s == kA - 1:
                        act.wait_ge(gone, c * kA + (kA + 1))
                        act.sem_inc(sem(st + "_slices_ready"), 1)
                        if l0:
                            act.sem_inc(sem("A0_kv_ready"), 1)

                def body(c, p, more, first=False, live=True):
                    for u in range(UNITS if live else DRAIN):
                        mine = slices_at(u, kA) if more else []
                        for s in mine[:1]:
                            piece(c + 1, 1 - p, s)
                        if live:
                            act.wait_ge(sem(st + "_less_max"), c * UNITS + (u + 1 + CRED))
                            if not (first and u < 2):
                                act.wait_ge(sem(st + "_pT_full"), c * UNITS + (u - 1))
                            exp(pr[:, u % 2, :, :], sm[:, u % 2, :, :]).then_inc(sem(st + "_exp"), 1)
                        unit = lagging(c, p, u, 1, first, live)
                        if unit:
                            cc, pp, v = unit
                            act.wait_ge(sem(st + "_pT_full"), cc * UNITS + (v + 1))
                            act.wait_ge(sem(st + "_pv_done"), cc * UNITS + (v - 1 + CRED))
                            copy(pT[:, v % 2, :, :], b4(2 + v % 2)).then_inc(sem(st + "_pT"), 1)
                        for s in mine[1:]:
                            piece(c + 1, 1 - p, s)
                        for part_, lag in enumerate((6,) if l0 else (6, 7)):
                            unit = lagging(c, p, u, lag, first, live)
                            if unit and unit[2] % QUARTERS == 0:
                                cc, j = unit[0], unit[2] // QUARTERS
                                if l0:
                                    act.wait_ge(sem("A0_oT_full"), cc * CB + (j + 1))
                                    copy(oT0[:, j % 2, :], bank[5][:, 0:P]).then_inc(sem("A0_oT"), 1)
                                else:
                                    act.wait_ge(sem("A3_oT_full"), cc * (2 * CB) + (2 * j + part_ + 5))
                                    act.wait_ge(sem("A3_y"), cc * CB + (j + 1))
                                    copy(oT3[:, 4 * part_:4 * part_ + 4, :], b4(5)).then_inc(sem("A3_oT"), 1)
                        if not l0 and not first and live:
                            routing(c - 1, u)

                act.sem_inc(sem(st + "_slice_gone"), 1)
                act.sem_inc(sem(st + "_pT"), CRED)
                act.sem_inc(sem(st + "_exp"), CRED)
                act.sem_inc(sem(st + "_pv_done"), CRED)
                act.sem_inc(sem(st + "_oT"), 1)
                if not l0:
                    act.sem_inc(sem("A3_y"), 1)
                    act.sem_inc(sem("A3_oT_full"), 4)
                    act.sem_inc(sem("F3_rows_copied"), 1)
                for s in range(kA):
                    piece(0, 0, s)
                body(0, 0, True, True)
                with act.Fori(0, NC // 2 - 2) as i:
                    for p in range(2):
                        body(i * 2 + (p + 1), 1 - p, True)
                body(NC - 3, 1, True)
                body(NC - 2, 0, True)
                body(NC - 1, 1, False)
                body(NC, 0, False, live=False)

            heads("A0")

            stage_start(act, STAGE["F0"])
            act.sem_inc(sem("F0_tanh"), 1)
            act.sem_inc(sem("F0_silu"), 2)
            with act.Fori(0, NC) as c:
                act.wait_ge(sem("F0_xT"), c + 1)
                act.wait_ge(sem("F0_up"), c * 2 + 1)
                act.wait_ge(sem("F0_conv"), c + 1)
                copy(xnT[:, :], bank[0][:, :]).then_inc(sem("F0_xnT"), 1)
                act.wait_ge(sem("F0_router"), c + 1)
                act.wait_ge(sem("F0_weights"), c + 1)
                nc.scalar.activation(lg0[:, :, :], bank[5][:, 0:CB * R0].rearrange("p (j r) -> p j r", j=CB), ACT.Tanh, scale=0.5)\
                    .then_inc(sem("F0_tanh"), 1)
                for k in range(2):
                    act.wait_ge(sem("F0_gate"), c * 2 + (k + 1))
                    act.wait_ge(sem("F0_hid"), c * 2 + (k + 1))
                    nc.scalar.activation(sg0[:, k, :], bank[1 + 2 * k][:, :], ACT.Silu).then_inc(sem("F0_silu"), 1)

            def single(st):
                before = 0 if st == "A1" else NC
                stage_start(act, STAGE[st])

                def front(c, first, back):
                    act.wait_ge(sem("A12_xT"), c + 1 + before)
                    if not first:
                        act.wait_ge(sem("A12_q"), c + before)
                    copy(xnT[:, :], bank[0][:, :]).then_inc(sem("A12_xnT"), 1)
                    act.wait_ge(s_cT, c + (1 + CX0[st]))
                    if not first:
                        act.wait_ge(sem("A12_v"), c + before)
                    copy(cxT[:, 0, :], bank[1][:, :]).then_inc(sem("A12_cxT"), 1)
                    if back and st == "A2":
                        probs_T(c - 1)
                    if not first:
                        act.wait_ge(sem("A12_scores"), c + before)
                    act.wait_ge(sem("A12_q"), c + 1 + before)
                    bias = bq2[:, 0:1] if st == "A2" else 0.0
                    aff(qT1[:, :], bank[2][:, :], float(P) ** -0.5, bias).then_inc(sem("A12_qT"), 1)
                    act.wait_ge(sem("A12_k"), c + 1 + before)
                    aff(kT1[:, :], bank[3][:, :], 1.0, bk2[:, 0:1] if st == "A2" else 0.0).then_inc(sem("A12_kT"), 1)
                    act.wait_ge(sem(st + "_less_max"), c + 1)
                    if not first:
                        act.wait_ge(sem("A12_pv_done"), c + before)
                        act.wait_ge(sem("A12_summed"), c + before)
                    exp(pr[:, 0, :, :], sm[:, 0, :, :]).then_inc(sem("A12_exp"), 1)

                def probs_T(c):
                    act.wait_ge(sem(st + "_pT_full"), c + 1)
                    if not isinstance(c, int):
                        act.wait_ge(sem("A12_pv_done"), c + before)
                    copy(pT[:, 0, :, :], b4(5)).then_inc(sem(st + "_pT"), 1)

                front(0, True, False)
                if st == "A2":
                    with act.Fori(1, NC) as c:
                        front(c, False, True)
                    act.wait_ge(sem("A12_pv_done"), NC - 1 + before)
                    probs_T(NC - 1)
                else:
                    with act.Fori(1, NC) as c:
                        front(c, False, True)

            single("A1")

            stage_start(act, STAGE["F1"])
            act.sem_inc(sem("F1_round2"), 2)
            act.sem_inc(sem("F1_hqT"), 1)

            rnd = lambda o, i, sc: nc.scalar.activation(o, i, ACT.Identity, scale=sc, bias=round3[:, 0:1])

            def up1(c, first):
                act.wait_ge(sem("F1_xT"), c + 1)
                if not first:
                    act.wait_ge(sem("F1_h"), c * K1)
                copy(xqT1[:, :], bank[0][:, 0:W // 2].bitcast(BF16)).then_inc(sem("F1_xqT"), 1)

            def scales(c, first):
                act.wait_ge(sem("F1_scaleT"), c + 2)
                if not first:
                    act.wait_ge(sem("F1_hs"), c * K1)
                copy(sbc1[:, :], bank[0][:, :]).then_inc(sem("F1_sbc"), 1)

            def f1(c, more, first):
                def middle(k):
                    act.wait_ge(sem("F1_hs"), c * K1 + (k + 1))
                    if k < 2 and not first:
                        act.wait_ge(sem("F1_silu"), c * K1 + (k - 1))
                    if k >= 2:
                        act.wait_ge(sem("F1_silu"), c * K1 + (k - 1))
                    nc.scalar.activation(hc1[:, k % 2, :, :], hs1[:, k % 2, :, :], ACT.Copy, scale=cw1[:, k, 1:2]).then_inc(sem("F1_middle"), 1)

                def silu(k):
                    act.wait_ge(sem("F1_conv"), c * K1 + (k + 1))
                    if k == 0 and not first:
                        act.wait_ge(sem("F1_hT"), c * CB)
                    nc.scalar.activation(h1[:, k, :].rearrange("p (j t) -> p j t", j=CB), hc1[:, k % 2, :, :], ACT.Silu,
                                         bias=cb1[:, k:k + 1]).then_inc(sem("F1_silu"), 1)

                middle(0)
                for k in range(1, K1):
                    middle(k)
                    if k < 3 and not first:
                        integers_T(c - 1, k - 1)
                    silu(k - 1)
                silu(K1 - 1)
                if more:
                    up1(c + 1, False)
                for j in range(CB):
                    if j == 2 and more:
                        scales(c + 1, False)
                    act.wait_ge(sem("F1_scale2"), c * 2 + (j // 2 + 1))
                    act.wait_ge(sem("F1_hq"), c * CB + (j + 1))
                    rnd(hr1[:, j % 2, :], bank[6 + j % 2][:, :], sc2[:, j:j + 1]).then_inc(sem("F1_round2"), 1)

            def integers_T(c, q):
                act.wait_ge(sem("F1_hqT_full"), c * 2 + (q + 1))
                act.wait_ge(sem("F1_y"), c * 2 + (q + 1))
                copy(hqT1[:, q, :], bank[0][:, :].bitcast(BF16)).then_inc(sem("F1_hqT"), 1)

            up1(0, True)
            scales(0, True)
            f1(0, True, True)
            with act.Fori(1, NC - 1) as c:
                f1(c, True, False)
            f1(NC - 1, False, False)
            for q in range(2):
                integers_T(NC - 1, q)

            single("A2")

            stage_start(act, STAGE["F2"])

            def f2(c, first):
                act.wait_ge(sem("F2_xT"), c + 1)
                if not first:
                    act.wait_ge(sem("F2_z"), c * (2 * CB))
                copy(xnT[:, :], bank[0][:, :]).then_inc(sem("F2_xnT"), 1)
                act.wait_ge(sem("F2_less_max"), c + 1)
                exp(ex2[:, :, :], lg2[:, :, :]).then_inc(sem("F2_exp"), 1)
                act.wait_ge(sem("F2_ohT_full"), c + 1)
                copy(ohT2[:, :], bank[6][0:E2, :]).then_inc(sem("F2_ohT"), 1)
                act.wait_ge(sem("F2_bias"), c + 1)
                if not first:
                    act.wait_ge(s_xdone, c + (NC * STAGE["F2"] + 1))
                copy(acc2[:, :, :], b4(7)).then_inc(sem("F2_acc"), 1)

            f2(0, True)
            with act.Fori(1, NC) as c:
                f2(c, False)

            stage_start(act, STAGE["A3"])
            heads("A3")

            stage_start(act, STAGE["F3"])
            act.sem_inc(sem("F3_w_sb"), 4)

            def expert_T(e, p):
                one = bass.ds(e, 1)
                for w, wT in enumerate((w1T3, w2T3)):
                    act.wait_ge(sem("F3_weights_transposed"), e * 2 + (w + 1))
                    act.sem_inc(sem("held"), 1)
                    copy(wT[:, one, :], bank[2 * p + w][:, :].unsqueeze(1)).then_inc(sem("F3_w_sb"), 1)

            routing(NC - 1, 8)
            for e in range(2):
                expert_T(e, e)
            for e in range(2, 4):
                expert_T(e, e % 2)
            routing(NC - 1, 10)
            with act.Fori(2, E3 // 2) as i:
                for p in range(2):
                    expert_T(i * 2 + p, p)

            def tile_T(n, s):
                act.wait_ge(sem("F3_tile_T"), n + 1)
                copy(xnT[:, (s % 4) * P:(s % 4) * P + P], bank[6 + s % 2][:, 0:P]).then_inc(sem("F3_tile_xT"), 1)

            def up(n, s):
                act.wait_ge(sem("F3_up"), n + 1)
                for k in range(K3):
                    last = nc.scalar.activation(h3[:, s % 2, k * P:k * P + P], bank[s % 2][:, k * P:k * P + P], ACT.Gelu,
                                                bias=b1c3[:, s % 4, k:k + 1])
                last.then_inc(sem("F3_gelu"), 1)

            tile_T(0, 0)
            tile_T(1, 1)
            with act.Fori(0, GROUPS3 - 1) as g:
                for s in range(SLOTS3):
                    up(g * SLOTS3 + s, s)
                    tile_T(g * SLOTS3 + (s + 2), s + 2)
            for s in range(SLOTS3):
                n = NT - SLOTS3 + s
                up(n, s)
                if n + 2 < NT:
                    tile_T(n + 2, s + 2)

        @block.vector
        def _(dve):
            v = nc.vector
            step = Steps(dve, sem("vector_steps"))
            s_held = sem("held")
            dve.sem_inc(s_xdone, 1)
            dve.wait_ge(s_load, 16 * n_loads)
            dve.wait_ge(s_const, 1)
            step(v.tensor_reduce(wkr0[:, 0:D0], wkv0[:, 0, :].rearrange("p (g d) -> p d g", g=4), AX, ALU.add))
            v.tensor_copy(wkr0[:, D0:P].rearrange("p (h d) -> p h d", d=D0), wkr0[:, 0:D0].unsqueeze(1).to_broadcast([P, HEADS - 1, D0]))
            v.tensor_reduce(wvs0[:, :], wkv0[:, 1, :].rearrange("p (g d) -> p d g", g=4), AX, ALU.add)
            v.tensor_reduce(bv0[:, :], bv0g[:, :].rearrange("p (g d) -> p d g", g=4), AX, ALU.add)
            v.tensor_reduce(bk0[:, :], bk0g[:, :], AX, ALU.add)
            step(v.tensor_scalar(bq0[:, :], bq0[:, :], float(D0) ** -0.5, None, ALU.mult))
            step(v.tensor_scalar(bq2[:, :], bq2[:, :], float(P) ** -0.5, None, ALU.mult))
            dve.wait_ge(sem("setup_gates"), 1)
            step(v.tensor_tensor(gate3[:, :], gates[:, 3:4], gates[:, 8:9], ALU.mult))
            v.tensor_reduce(part[:, 0:1], w1n[:, :, :].rearrange("p k d -> p (k d)"), AX, ALU.add, apply_absolute_value=True)
            v.tensor_reduce(part[:, 1:2], w2n[:, :], AX, ALU.add, apply_absolute_value=True).then_inc(sem("setup_abs"), 1)
            s_bk, s_gone = sem("setup_bank_full"), sem("setup_bank_gone")
            dve.wait_ge(s_gone, 7)
            step(v.scalar_tensor_tensor(wr3[:, :], keyT[:, 0, :], 2.0, keyT[:, 1, :], ALU.mult, ALU.add))
            v.tensor_tensor(keysq[:, :], keyT[:, 0, :], keyT[:, 0, :], ALU.mult).then_inc(sem("setup_keysq"), 1)
            dve.wait_ge(s_bk, 12)
            step(v.tensor_scalar(wsc1[:, :], bank[11 % 8][:, 0:1], 1.0 / (H1 * P), EPS, ALU.mult, ALU.max))
            step(v.tensor_scalar(wsc2[:, :], bank[11 % 8][:, 1:2], 1.0 / (H1 * P), EPS, ALU.mult, ALU.max))
            dve.wait_ge(s_bk, 13)
            step(v.tensor_tensor(rb3[:, :], rb3[:, :], bank[12 % 8][:, 0:E3], ALU.subtract))
            dve.wait_ge(s_gone, 11)
            dve.sem_inc(s_gone, 2)
            dve.sem_inc(sem("setup_wscale"), 1)
            for t, (src, wsc) in enumerate(((w1n[:, :, :].rearrange("p k d -> p (k d)"), wsc1), (w2n[:, :], wsc2))):
                step(v.reciprocal(rs[:, t:t + 1], wsc[:, :]))
                step(v.tensor_scalar(wabs[:, t, :], src, rs[:, t:t + 1], ROUND, ALU.mult, ALU.add))
                step(v.tensor_scalar(wabs[:, t, :], wabs[:, t, :], ROUND, 1.0, ALU.subtract, ALU.min))
                step(v.tensor_scalar(wabs[:, t, :], wabs[:, t, :], -1.0, None, ALU.max))
                step(v.tensor_scalar(wsc[:, :], wsc[:, :], 1.0 / 127, None, ALU.mult))
            dve.sem_inc(sem("setup_ternary"), 1)
            dve.wait_ge(s_gone, 15)
            dve.sem_inc(sem("setup_done"), 1)

            def norm_stats(src):
                for j in range(CB):
                    last = v.bn_stats(stats[:, j, :], src[:, j, :])
                step.held(last, s_held)
                for j in range(CB):
                    last = v.bn_aggr(mv[:, j, :], stats[:, j, :])
                step(last)

            def norm_var(st):
                v.tensor_scalar(ve[:, :].unsqueeze(2), mv[:, :, 1:2], EPS, None, ALU.add).then_inc(s_var, 1)

            def norm_apply(st, c, src, n=None, ready=True, free=None):
                dve.wait_ge(s_rstd, (c if n is None else n) + (1 + VAR0[st]))
                if free is not None:
                    dve.wait_ge(*free)
                for j in range(CB):
                    last = v.tensor_scalar(xn[:, j, :], src[:, j, :], mv[:, j, 0:1], rstd[:, j:j + 1], ALU.subtract, ALU.mult)
                if ready:
                    last.then_inc(s_xn, 1)
                else:
                    step(last)

            def xc(c):
                return x[:, bass.ds(c * CB, CB), :]

            def less_max(src, slot, st):
                step(v.tensor_reduce(nm[:, slot, :], src, AX, ALU.max))
                v.tensor_tensor(sm[:, slot, :, :], src, nm[:, slot, :].unsqueeze(2).to_broadcast([P, CB, P]), ALU.subtract)\
                    .then_inc(sem(st + "_less_max"), 1)

            def routing(c, u):
                if u == 6:
                    norm_stats(xc(c))
                    v.tensor_scalar(ve[:, :].unsqueeze(2), mv[:, :, 1:2], EPS, None, ALU.add).then_inc(sem("F3_variance"), 1)
                if u == 7:
                    dve.wait_ge(sem("F3_inverse_deviation"), c + 1)
                    dve.wait_ge(sem("F3_rows_copied"), c + 1)
                    for j in range(CB):
                        last = v.tensor_scalar(xr3[:, j, :], xc(c)[:, j, :], mv[:, j, 0:1], rstd[:, j:j + 1], ALU.subtract, ALU.mult)
                    last.then_inc(sem("F3_normalised"), 1)
                if u == 9:
                    dve.wait_ge(sem("F3_rows_free"), c + 1)
                    step(v.tensor_copy(rowsu3[:, :, P:P + 1], goes3[:, :].unsqueeze(2)))
                    v.tensor_scalar(goes3[:, :], goes3[:, :], float(W), None, ALU.add)
                    step(v.tensor_tensor(tmp[:, :, :], xr3[:, :, :], xr3[:, :, :], ALU.mult))
                    step(v.tensor_reduce(x23[:, :], tmp[:, :, :], AX, ALU.add))
                    dve.wait_ge(sem("F3_lg"), c + 1)
                    lgp = bank[5][:, 0:CB * E3].rearrange("p (j e) -> p j e", j=CB)
                    step(v.tensor_tensor(lg3[:, :, :], lgp, rb3[:, :].unsqueeze(1).to_broadcast([P, CB, E3]), ALU.add))
                    step.held(v.tensor_tensor(lg3[:, :, :], lg3[:, :, :], x23[:, :].unsqueeze(2).to_broadcast([P, CB, E3]), ALU.subtract), s_held)
                    for j in range(CB):
                        last = v.max(top3[:, j, :], lg3[:, j, :])
                    step.held(last, s_held)
                    for j in range(CB):
                        last = v.max_index(idx3[:, j, :], top3[:, j, :], lg3[:, j, :])
                    step(last)
                    v.tensor_copy(idf3[:, :, :], idx3[:, :, 0:TOP3])
                    step(v.tensor_copy(es3[:, :].unsqueeze(2), top3[:, :, 0:1]))
                    v.tensor_tensor(top3[:, :, 0:TOP3], top3[:, :, 0:TOP3], es3[:, :].unsqueeze(2).to_broadcast([P, CB, TOP3]), ALU.subtract)\
                        .then_inc(sem("F3_less_max"), 1)
                    step(v.tensor_tensor(oh3[:, :, :], iota8[:, :].unsqueeze(1).to_broadcast([P, SC, E3]),
                                         idf3[:, :, :].rearrange("p j k -> p (j k)").unsqueeze(2).to_broadcast([P, SC, E3]), ALU.is_equal))
                    v.tensor_reduce(ohs3[:, :, :], oh3[:, :, :].rearrange("p (j k) e -> p j e k", j=CB), AX, ALU.add).then_inc(sem("F3_chosen"), 1)
                if u == 12:
                    dve.wait_ge(sem("F3_exp"), c + 1)
                    step(v.tensor_reduce(es3[:, :], ex3[:, :, :], AX, ALU.add))
                    step(v.reciprocal(es3[:, :], es3[:, :]))
                    step(v.tensor_scalar(es3[:, :], es3[:, :], gates[:, 7:8], None, ALU.mult))
                    step(v.tensor_tensor(wt3[:, bass.ds(c * SC, SC)].rearrange("p (j k) -> p j k", j=CB), ex3[:, :, :],
                                         es3[:, :].unsqueeze(2).to_broadcast([P, CB, TOP3]), ALU.mult))
                    dve.wait_ge(sem("F3_counts"), c + 1)
                    for j in range(CB):
                        step(v.tensor_tensor(dst3[:, j, :], bank[5][:, j * E3:j * E3 + E3], run3[:, :], ALU.add))
                        step(v.tensor_tensor(run3[:, :], bank[5][:, (CB + j) * E3:(CB + j + 1) * E3], run3[:, :], ALU.add))
                    o4 = oh3[:, :, :].rearrange("p (j k) e -> p j k e", j=CB)
                    step(v.tensor_tensor(o4, o4, dst3[:, :, :].unsqueeze(2).to_broadcast([P, CB, TOP3, E3]), ALU.mult))
                    step(v.tensor_reduce(to3[:, :], oh3[:, :, :], AX, ALU.add))
                    v.tensor_copy(di3[:, :], to3[:, :]).then_inc(sem("F3_rows_ready"), 1)

            def heads(st):
                l0 = st == "A0"
                kA = 5 if l0 else 2 + HEADS + 2 * CB
                bias, gate = (bo0, gates[:, 0:1]) if l0 else (bo3, gate3[:, 0:1])

                def softmax(n0, u):
                    dve.wait_ge(sem(st + "_scores"), n0 + (u + 1))
                    dve.wait_ge(sem(st + "_exp"), n0 + (u - 1 + CRED))
                    less_max(b4(u % 2), u % 2, st)

                def normal(c, p, n0, u):
                    j, qd = divmod(u, QUARTERS)
                    if l0:
                        if qd != QUARTERS - 1:
                            return
                        dve.wait_ge(sem(st + "_pv_done"), n0 + (u + 1 + CRED))
                        step(v.reciprocal(rs[:, :], bank[4][:, P:VW0]))
                        v.tensor_tensor(on0[:, j % 2, :].rearrange("p (h d) -> p h d", d=D0), bank[4][:, 0:P].rearrange("p (h d) -> p h d", d=D0),
                                        rs[:, :].unsqueeze(2).to_broadcast([P, HEADS, D0]), ALU.mult).then_inc(sem("A0_normal"), 1)
                        return
                    dve.wait_ge(sem(st + "_pv_done"), n0 + (u + 1 + CRED))
                    if qd == 0:
                        dve.wait_ge(sem("A3_oT_full"), c * (2 * CB) + (2 * j + 2))
                    o = bank[4][:, 0:HQ * (D3 + 1)].rearrange("p (h d) -> p h d", d=D3 + 1)
                    step(v.reciprocal(rs[:, 0:HQ].unsqueeze(2), o[:, :, D3:D3 + 1]))
                    v.tensor_tensor(on3[:, j % 2, qd * HQ * D3:(qd + 1) * HQ * D3].rearrange("p (h d) -> p h d", d=D3), o[:, :, 0:D3],
                                    rs[:, 0:HQ].unsqueeze(2).to_broadcast([P, HQ, D3]), ALU.mult).then_inc(sem("A3_normal"), 1)

                def front(c, k):
                    if l0:
                        if k == 0:
                            norm_stats(xc(c))
                            norm_var(st)
                        if k == 2:
                            norm_apply(st, c, xc(c), free=(sem(st + "_xnT"), c) if not isinstance(c, int) or c else None)
                        return
                    if k == 0:
                        norm_stats(xc(c))
                        norm_var(st)
                    if k == 1:
                        norm_apply(st, c, xc(c), n=c * 2, ready=False, free=(sem(st + "_xnT"), c) if not isinstance(c, int) or c else None)
                    if k == 2:
                        norm_stats(xn)
                        norm_var(st)
                    if k == 3:
                        norm_apply(st, c, xn, n=c * 2 + 1)

                def body(c, p, more, first=False, live=True, ahead=True):
                    for u in range(UNITS if live else DRAIN):
                        if more and ahead and 2 <= u < 6:
                            front(c + 2, u - 2)
                        if live:
                            softmax(c * UNITS, u)
                        unit = lagging(c, p, u, 2, first, live)
                        if unit:
                            normal(unit[0], unit[1], unit[0] * UNITS, unit[2])
                        if u == 4 and not first:
                            dve.wait_ge(sem(st + "_y"), c * CB + (0 if l0 else 1))
                            step(v_add(tmp[:, :, :], b4(7), bias[:, :].unsqueeze(1).to_broadcast([P, CB, P])))
                            v.scalar_tensor_tensor(xc(c - 1), tmp[:, :, :], gate, xc(c - 1), ALU.mult, ALU.add).then_inc(s_xdone, 1)
                        if not l0 and not first and live:
                            routing(c - 1, u)

                v_add = lambda o, x0, x1: v.tensor_tensor(o, x0, x1, ALU.add)
                dve.sem_inc(sem(st + "_less_max"), CRED)
                dve.sem_inc(sem(st + "_normal"), 1)
                if not l0:
                    for s in range(2):
                        v.memset(v3[s][:, :, :, D3:D3 + 1], 1.0)
                    dve.wait_ge(sem("F3_constants"), 1)
                    step(v.tensor_copy(run3[:, :], first3[:, :]))
                for k in range(4):
                    front(0, k)
                for k in range(4):
                    front(1, k)
                body(0, 0, True, True)
                step.loop(2 * (UNITS + CB + 1 + 2) if l0 else 2 * (UNITS + UNITS + 1 + 5 + 25))
                with dve.Fori(0, NC // 2 - 2) as i:
                    step.turn(i)
                    for p in range(2):
                        body(i * 2 + (p + 1), 1 - p, True)
                step.end(NC // 2 - 2)
                body(NC - 3, 1, True)
                body(NC - 2, 0, True, ahead=False)
                body(NC - 1, 1, False)
                body(NC, 0, False, live=False)

            heads("A0")

            stage_start(dve, STAGE["F0"])
            dve.sem_inc(sem("F0_hid"), 2)
            dve.sem_inc(sem("F0_weights"), 1)
            dve.sem_inc(sem("F0_down_read"), 2)
            dve.sem_inc(sem("F0_up"), 1)
            dve.sem_inc(sem("F0_conv"), 1)
            dve.sem_inc(sem("F0_convT"), 1)

            def f0_norm(c, first):
                norm_stats(xc(c))
                norm_var("F0")
                dve.wait_ge(s_rstd, c + (1 + VAR0["F0"]))
                if not first:
                    dve.wait_ge(sem("F0_xT"), c)
                    dve.wait_ge(sem("F0_xn_kept"), c)
                for j in range(CB):
                    last = v.tensor_scalar(xn[:, j, :], xc(c)[:, j, :], mv[:, j, 0:1], rstd[:, j:j + 1], ALU.subtract, ALU.mult)
                last.then_inc(s_xn, 1)

            def f0(c, more):
                dve.wait_ge(sem("F0_tanh"), c + 2)
                step(v.tensor_scalar(lg0[:, :, :], lg0[:, :, :], 0.5, 0.5, ALU.mult, ALU.add))
                step.held(v.tensor_tensor(sel0[:, :, :], lg0[:, :, :], rb0[:, :].unsqueeze(1).to_broadcast([P, CB, R0]), ALU.add), s_held)
                for j in range(CB):
                    last = v.max(top0[:, j, :], sel0[:, j, :])
                step.held(last, s_held)
                for j in range(CB):
                    last = v.max_index(idx0[:, j, :], top0[:, j, :], sel0[:, j, :])
                step(last)
                step(v.tensor_copy(idf0[:, :, :], idx0[:, :, :]))
                for r in range(2):
                    step(v.tensor_tensor(oh0[:, r, :, :], iota8[:, 0:R0].unsqueeze(1).to_broadcast([P, CB, R0]),
                                         idf0[:, :, r:r + 1].to_broadcast([P, CB, R0]), ALU.is_equal))
                step(v.tensor_tensor(oh0[:, 0, :, :], oh0[:, 0, :, :], oh0[:, 1, :, :], ALU.add))
                step(v.tensor_tensor(cwt0[:, :, :], oh0[:, 0, :, :], lg0[:, :, :], ALU.mult))
                step(v.tensor_reduce(wsum0[:, :], cwt0[:, :, :], AX, ALU.add))
                step(v.tensor_scalar(wsum0[:, :], wsum0[:, :], 1e-9, None, ALU.add))
                step(v.reciprocal(wsum0[:, :], wsum0[:, :]))
                step(v.tensor_tensor(cwt0[:, :, :], cwt0[:, :, :], wsum0[:, :].unsqueeze(2).to_broadcast([P, CB, R0]), ALU.mult))
                v.tensor_tensor(ccp0[:, :].unsqueeze(2), cwt0[:, :, E0:E0 + 1], cwt0[:, :, E0 + 2:E0 + 3], ALU.add).then_inc(sem("F0_weights"), 1)
                for k in range(2):
                    dve.wait_ge(sem("F0_up"), c * 2 + (k + 2))
                    dve.wait_ge(sem("F0_silu"), c * 2 + (k + 3))
                    if k == 0:
                        dve.wait_ge(sem("F0_down"), c * CB) if not (isinstance(c, int) and c == 0) else None
                    v.tensor_tensor(hid0[:, k, :], bank[2 + 2 * k][:, :], sg0[:, k, :], ALU.mult).then_inc(sem("F0_hid"), 1)
                if more:
                    f0_norm(c + 1, False)
                dve.wait_ge(sem("F0_weights"), c + 2)
                dve.wait_ge(sem("F0_xn_kept"), c + 1)
                xk = xall0[:, bass.ds(c * CB, CB), :]
                for j in range(CB):
                    last = v.tensor_scalar(tmp2[:, j, :], xk[:, j, :], 0.0, cwt0[:, j, R0 - 1:R0], ALU.max, ALU.mult)
                step(last)
                for j in range(CB):
                    last = v.scalar_tensor_tensor(tmp[:, j, :], xk[:, j, :], ccp0[:, j:j + 1], tmp2[:, j, :], ALU.mult, ALU.add)
                step(last)
                dve.wait_ge(sem("F0_convT"), c + 2)
                v.tensor_tensor(tmp[:, :, :], b4(0), tmp[:, :, :], ALU.add).then_inc(sem("F0_conv_read"), 1)
                dve.wait_ge(sem("F0_conv_read"), c + 1)
                for j in range(CB):
                    dve.wait_ge(sem("F0_down"), c * CB + (j + 1))
                    o = b4(6 + j % 2)
                    for e in range(E0):
                        last = v.scalar_tensor_tensor(tmp[:, j, :], o[:, e, :], cwt0[:, j, e:e + 1], tmp[:, j, :], ALU.mult, ALU.add)
                        if e < E0 - 1:
                            step(last)
                    last.then_inc(sem("F0_down_read"), 1)
                dve.wait_ge(sem("F0_down_read"), c * CB + (CB + 2))
                v.scalar_tensor_tensor(xc(c), tmp[:, :, :], gates[:, 4:5], xc(c), ALU.mult, ALU.add).then_inc(s_xdone, 1)

            f0_norm(0, True)
            f0(0, True)
            step.loop(13 + 2 + 2 + CB * (E0 - 1))
            with dve.Fori(1, NC - 1) as c:
                step.turn(c - 1)
                f0(c, True)
            step.end(NC - 2)
            f0(NC - 1, False)

            def single(st):
                before = 0 if st == "A1" else NC
                stage_start(dve, STAGE[st])
                gate = gates[:, 1:2] if st == "A1" else gates[:, 2:3]

                def ln(c, first):
                    norm_stats(xc(c))
                    norm_var(st)
                    norm_apply(st, c, xc(c), free=None if first else (sem("A12_xT"), c + before))

                def summed(c):
                    dve.wait_ge(sem("A12_exp"), c + 1 + before)
                    step(v.tensor_reduce(sums[:, :], pr[:, 0, :, :], AX, ALU.add))
                    step(v.reciprocal(sums[:, :], sums[:, :]))
                    dve.sem_inc(sem("A12_summed"), 1)
                    if st == "A1":
                        v.tensor_tensor(pr[:, 0, :, :], pr[:, 0, :, :], sums[:, :].unsqueeze(2).to_broadcast([P, CB, P]), ALU.mult)\
                            .then_inc(sem(st + "_normal"), 1)

                def residual(c):
                    dve.wait_ge(sem("A12_pv_done"), c + 1 + before)
                    if st == "A1":
                        v.scalar_tensor_tensor(xc(c), b4(6), gate, xc(c), ALU.mult, ALU.add).then_inc(s_xdone, 1)
                    else:
                        step(v.tensor_tensor(tmp[:, :, :], b4(6), sums[:, :].unsqueeze(2).to_broadcast([P, CB, P]), ALU.mult))
                        v.scalar_tensor_tensor(xc(c), tmp[:, :, :], gate, xc(c), ALU.mult, ALU.add).then_inc(s_xdone, 1)

                def scores(c, first):
                    dve.wait_ge(sem("A12_v"), c + 1 + before)
                    if st == "A1":
                        v.tensor_copy(v1[:, :, :], b4(4)).then_inc(sem("A12_v_sb"), 1)
                    else:
                        v.tensor_tensor(v1[:, :, :], b4(4), bv2[:, :].unsqueeze(1).to_broadcast([P, CB, P]), ALU.add).then_inc(sem("A12_v_sb"), 1)
                    dve.wait_ge(sem("A12_scores"), c + 1 + before)
                    if not first:
                        dve.wait_ge(sem("A12_exp"), c + before)
                    if st == "A1":
                        step(v.tensor_tensor(sm[:, 0, :, :], b4(7), causal[:, :].unsqueeze(1).to_broadcast([P, CB, P]), ALU.add))
                        less_max(sm[:, 0, :, :], 0, st)
                    else:
                        less_max(b4(7), 0, st)

                per = 2 + 2 + 1 + 1
                ln(0, True)
                ln(1, False)
                scores(0, True)
                step.loop(per)
                with dve.Fori(1, NC - 1) as c:
                    step.turn(c - 1)
                    summed(c - 1)
                    ln(c + 1, False)
                    residual(c - 1)
                    scores(c, False)
                step.end(NC - 2)
                summed(NC - 2)
                residual(NC - 2)
                scores(NC - 1, False)
                summed(NC - 1)
                residual(NC - 1)

            single("A1")

            stage_start(dve, STAGE["F1"])
            dve.sem_inc(sem("F1_hq"), 2)
            dve.sem_inc(sem("F1_scaleT"), 1)
            dve.sem_inc(sem("F1_y"), 2)

            def f1_norm(c, first):
                norm_apply("F1", c, xc(c), ready=False)
                if not first:
                    dve.wait_ge(sem("F1_scale_spread"), c)
                step(v.tensor_reduce(am1[:, :], xn[:, :, :], AX, ALU.max, apply_absolute_value=True))
                step(v.tensor_scalar(am1[:, :], am1[:, :], EPS, None, ALU.max))
                step(v.reciprocal(sc1[:, :], am1[:, :]))
                v.tensor_scalar(sc1[:, :], sc1[:, :], 127.0, None, ALU.mult).then_inc(sem("F1_scale1"), 1)
                dve.wait_ge(sem("F1_scale1"), c + 1)
                for j in range(CB):
                    last = v.tensor_scalar(xr1[:, j, :], xn[:, j, :], sc1[:, j:j + 1], ROUND, ALU.mult, ALU.add)
                step(last)
                if not first:
                    dve.wait_ge(sem("F1_xT"), c)
                v.tensor_scalar(xq1[:, :, :], xr1[:, :, :], ROUND, 127.0, ALU.subtract, ALU.min).then_inc(sem("F1_xq"), 1)

            def f1(c, more, first):
                def scaled(k):
                    dve.wait_ge(sem("F1_h"), c * K1 + (k + 1))
                    if k >= 2:
                        dve.wait_ge(sem("F1_middle"), c * K1 + (k - 1))
                    v.scalar_tensor_tensor(hs1[:, k % 2, :, :], b4(1 + k), wsc1[:, 0:1], sbc1[:, :].rearrange("p (j t) -> p j t", j=CB),
                                           ALU.mult, ALU.mult).then_inc(sem("F1_hs"), 1)

                def taps(k):
                    dve.wait_ge(sem("F1_middle"), c * K1 + (k + 1))
                    h, o = hs1[:, k % 2, :, :], hc1[:, k % 2, :, :]
                    step(v.scalar_tensor_tensor(o[:, :, 1:P], h[:, :, 0:P - 1], cw1[:, k, 0:1], o[:, :, 1:P], ALU.mult, ALU.add))
                    v.scalar_tensor_tensor(o[:, :, 0:P - 1], h[:, :, 1:P], cw1[:, k, 2:3], o[:, :, 0:P - 1], ALU.mult, ALU.add)\
                        .then_inc(sem("F1_conv"), 1)
                    dve.wait_ge(sem("F1_conv"), c * K1 + (k + 1))

                dve.wait_ge(sem("F1_sbc"), c + 1)
                scaled(0)
                for k in range(1, K1):
                    scaled(k)
                    taps(k - 1)
                taps(K1 - 1)
                if more:
                    norm_stats(xc(c + 1))
                    norm_var("F1")
                if not first:
                    residual1(c - 1)
                if more:
                    f1_norm(c + 1, False)
                for q in range(2):
                    dve.wait_ge(sem("F1_hT"), c * CB + (2 * q + 2))
                    pair = slice(2 * q, 2 * q + 2)
                    for j in (2 * q, 2 * q + 1):
                        last = v.tensor_reduce(am2[:, j:j + 1], bank[6 + j % 2][:, :], AX, ALU.max, apply_absolute_value=True)
                    step(last)
                    step(v.tensor_scalar(am2[:, pair], am2[:, pair], EPS, None, ALU.max))
                    step(v.reciprocal(sc2[:, pair], am2[:, pair]))
                    v.tensor_scalar(sc2[:, pair], sc2[:, pair], 127.0, None, ALU.mult).then_inc(sem("F1_scale2"), 1)
                    hq(c, 2 * q)
                    hq(c, 2 * q + 1)
                step(v.tensor_scalar(isc2[:, :], am2[:, :], wsc2[:, 0:1], gates[:, 5:6], ALU.mult, ALU.mult))

            def residual1(c):
                dve.wait_ge(sem("F1_y"), c * 2 + 4)
                for j in range(CB):
                    last = v.scalar_tensor_tensor(xc(c)[:, j, :], bank[5][:, j * P:j * P + P], isc2[:, j:j + 1], xc(c)[:, j, :], ALU.mult, ALU.add)
                last.then_inc(s_xdone, 1)

            def hq(c, j):
                dve.wait_ge(sem("F1_round2"), c * CB + (j + 3))
                v.tensor_scalar(hq1[:, j, :], hr1[:, j % 2, :], ROUND, 127.0, ALU.subtract, ALU.min).then_inc(sem("F1_hq"), 1)

            norm_stats(xc(0))
            norm_var("F1")
            f1_norm(0, True)
            f1(0, True, True)
            step.loop(2 + 1 + 3 + 1 + K1 + 2 * 3 + 1)
            with dve.Fori(1, NC - 1) as c:
                step.turn(c - 1)
                f1(c, True, False)
            step.end(NC - 2)
            f1(NC - 1, False, False)
            residual1(NC - 1)

            single("A2")

            stage_start(dve, STAGE["F2"])
            dve.sem_inc(sem("F2_z_read"), 4)
            dve.sem_inc(sem("F2_logits_read"), 1)

            def f2(c, more, first):
                dve.wait_ge(sem("F2_logits"), c + 1)
                v.tensor_tensor(lg2[:, :, :], b4(1), bg2[:, :].unsqueeze(1).to_broadcast([P, CB, P]), ALU.add).then_inc(sem("F2_logits_read"), 1)
                dve.wait_ge(sem("F2_logits_read"), c + 2)
                dve.sem_inc(s_held, 1)
                for j in range(CB):
                    last = v.max(top2[:, j, :], lg2[:, j, :])
                step.held(last, s_held)
                for j in range(CB):
                    last = v.max_index(idx2[:, j, :], top2[:, j, :], lg2[:, j, :])
                step(last)
                v.tensor_tensor(lg2[:, :, :], lg2[:, :, :], top2[:, :, 0:1].to_broadcast([P, CB, P]), ALU.subtract).then_inc(sem("F2_less_max"), 1)
                step(v.tensor_single_scalar(idx2[:, :, 0:1], idx2[:, :, 0:1], E2 - 1, ALU.bitwise_and))
                step(v.tensor_copy(idf2[:, :].unsqueeze(2), idx2[:, :, 0:1]))
                if not first:
                    dve.wait_ge(sem("F2_ohT_full"), c)
                v.tensor_tensor(oh2[:, :, :], iota8[:, 0:E2].unsqueeze(1).to_broadcast([P, CB, E2]),
                                idf2[:, :].unsqueeze(2).to_broadcast([P, CB, E2]), ALU.is_equal).then_inc(sem("F2_onehot"), 1)
                dve.wait_ge(sem("F2_exp"), c + 1)
                step(v.tensor_reduce(pg2[:, :], ex2[:, :, :], AX, ALU.add))
                step(v.reciprocal(pg2[:, :], pg2[:, :]))
                step(v.tensor_scalar(pg2[:, :], pg2[:, :], gates[:, 6:7], None, ALU.mult))
                if more:
                    norm_stats(xc(c + 1))
                    norm_var("F2")
                    norm_apply("F2", c + 1, xc(c + 1), free=(sem("F2_xT"), c + 1))
                dve.wait_ge(sem("F2_acc"), c + 1)
                for j in range(CB):
                    for half in range(2):
                        dve.wait_ge(sem("F2_z"), c * (2 * CB) + (2 * j + half + 1))
                        z = b4(2 + (2 * j + half) % 4)
                        for q in range(4):
                            e = 4 * half + q
                            last = v.scalar_tensor_tensor(acc2[:, j, :], z[:, q, :], oh2[:, j, e:e + 1], acc2[:, j, :], ALU.mult, ALU.add)
                            if q < 3:
                                step(last)
                        last.then_inc(sem("F2_z_read"), 1)
                        dve.wait_ge(sem("F2_z_read"), c * (2 * CB) + (2 * j + half + 5))
                step(v.tensor_scalar(acc2[:, :, :], acc2[:, :, :], 0.0, None, ALU.max))
                for j in range(CB):
                    last = v.scalar_tensor_tensor(xc(c)[:, j, :], acc2[:, j, :], pg2[:, j:j + 1], xc(c)[:, j, :], ALU.mult, ALU.add)
                last.then_inc(s_xdone, 1)

            norm_stats(xc(0))
            norm_var("F2")
            norm_apply("F2", 0, xc(0))
            f2(0, True, True)
            step.loop(2 + 2 + 3 + 2 + 2 * CB * 3 + 1)
            with dve.Fori(1, NC - 1) as c:
                step.turn(c - 1)
                f2(c, True, False)
            step.end(NC - 2)
            f2(NC - 1, False, False)

            stage_start(dve, STAGE["A3"])
            heads("A3")

            stage_start(dve, STAGE["F3"])
            for u in (6, 7, 9, 12):
                routing(NC - 1, u)
            dve.wait_ge(sem("F3_constants"), 2)
            v.memset(padu3[:, P:P + 1], int(NOWHERE))

            step(v.tensor_tensor(cum3[:, 0, :], run3[:, :], first3[:, :], ALU.subtract))
            step(v.tensor_scalar(cnt3[:, :], cum3[:, 0, :], float(P - 1), None, ALU.add))
            step(v.tensor_single_scalar(cnt3[:, :], cnt3[:, :], P.bit_length() - 1, ALU.arith_shift_right))
            step(v.tensor_copy(tl3[:, :], cnt3[:, :]))
            step(v.tensor_copy(cum3[:, 0, :], tl3[:, :]))
            n, lag = 0, 1
            while lag < E3:
                v.tensor_copy(cum3[:, 1 - n, 0:lag], cum3[:, n, 0:lag])
                step(v.tensor_tensor(cum3[:, 1 - n, lag:E3], cum3[:, n, lag:E3], cum3[:, n, 0:E3 - lag], ALU.add))
                n, lag = 1 - n, 2 * lag
            step(v.tensor_tensor(until3[:, :, :], cum3[0:1, n, :].unsqueeze(1).to_broadcast([1, NT, E3]),
                                 iota3[:, :].unsqueeze(2).to_broadcast([1, NT, E3]), ALU.is_le))
            step(v.tensor_reduce(tabf3[:, 0, :], until3[:, :, :], AX, ALU.add))
            step(v.tensor_scalar(tabf3[:, 0, :], tabf3[:, 0, :], float(E3 - 1), None, ALU.min))
            step(v.tensor_scalar(tl3[:, :], tl3[:, :], -float(P), float(REGION), ALU.mult, ALU.add))
            step(v.tensor_tensor(until3[:, :, :], until3[:, :, :], tl3[0:1, :].unsqueeze(1).to_broadcast([1, NT, E3]), ALU.mult))
            step(v.tensor_reduce(tabf3[:, 1, :], until3[:, :, :], AX, ALU.add))
            step(v.scalar_tensor_tensor(tabf3[:, 1, :], iota3[:, :], float(P), tabf3[:, 1, :], ALU.mult, ALU.add))
            step(v.tensor_scalar(tabf3[:, 1, :], tabf3[:, 1, :], float(UNUSED), None, ALU.min))
            v.tensor_copy(ends3[:, :], run3[0:1, :])
            v.tensor_copy(tab3[:, :, :], tabf3[:, :, :]).then_inc(sem("F3_table"), 1)
            dve.wait_ge(sem("F3_table"), 1)

            dve.wait_ge(sem("F3_w_sb"), 2 * E3 + 4)
            dve.wait_ge(sem("F3_b2_loaded"), 16)
            dve.sem_inc(sem("F3_down"), 3)
            dve.sem_inc(sem("F3_output"), 2)

            def weights(n, s):
                e = dve.value_load(tab3[0:1, 0, bass.ds(n, 1)], min_val=0, max_val=E3 - 1)
                if not isinstance(n, int) or n >= 4:
                    dve.wait_ge(sem("F3_down"), n)
                v.tensor_copy(w1c3[:, s % 4, :], w1T3[:, :, :].rearrange("p e f -> p (e f)")[:, bass.ds(e * H3, H3)])
                v.tensor_copy(b1c3[:, s % 4, :], b13[:, :, :].rearrange("p e k -> p (e k)")[:, bass.ds(e * K3, K3)])
                v.tensor_copy(w2c3[:, s % 4, :], w2T3[:, :, :].rearrange("p e f -> p (e f)")[:, bass.ds(e * H3, H3)])\
                    .then_inc(sem("F3_tile_weights"), 1)

            def output(n, s, g):
                e = dve.value_load(tab3[0:1, 0, bass.ds(n, 1)], min_val=0, max_val=E3 - 1)
                dve.wait_ge(sem("F3_down"), n + 4)
                if g is not None:
                    dve.wait_ge(sem(f"F3_scattered{s // GROUP3}"), g * (16 * GROUP3))
                v.tensor_tensor(yt3[:, s, :], bank[2 + s % 2][:, 0:P], b2b3[:, bass.ds(e * P, P)], ALU.add).then_inc(sem("F3_output"), 1)

            for n in range(3):
                weights(n, n)
            for s in range(SLOTS3):
                weights(s + 3, s + 3)
                output(s, s, None)
            with dve.Fori(1, GROUPS3 - 1) as g:
                for s in range(SLOTS3):
                    weights(g * SLOTS3 + (s + 3), s + 3)
                    output(g * SLOTS3 + s, s, g)
            for s in range(SLOTS3):
                n = NT - SLOTS3 + s
                if n + 3 < NT:
                    weights(n + 3, s + 3)
                output(n, s, GROUPS3 - 1)

            def combine(c, p, i):
                dve.wait_ge(sem(f"F3_outputs_loaded{p}"), i * (16 * TOP3) + 16 * TOP3)
                for k in range(TOP3):
                    for j in range(CB):
                        last = v.scalar_tensor_tensor(xc(c)[:, j, :], combined[:, p, k, j, :], wt3[:, bass.ds(c * SC + (j * TOP3 + k), 1)],
                                                      xc(c)[:, j, :], ALU.mult, ALU.add)
                    if k < TOP3 - 1:
                        step(last)
                last.then_inc(s_xdone, 1)

            step.loop(2 * (TOP3 - 1))
            with dve.Fori(0, NC // 2) as i:
                step.turn(i)
                for p in range(2):
                    combine(i * 2 + p, p, i)
            step.end(NC // 2)


_OUT = (B, P, P)


def kernel(**inputs):
    import numpy as _np
    import concourse.bacc as _bacc
    from concourse import mybir as _mybir
    from concourse.bass_utils import run_bass_kernel_spmd as _run

    nc = _bacc.Bacc("TRN2", target_bir_lowering=False, num_devices=1)
    arrays, aps = {}, {}
    for name, value in inputs.items():
        arr = _np.ascontiguousarray(value)
        arrays[f"in_{name}"] = arr
        aps[name] = nc.dram_tensor(f"in_{name}", arr.shape, _mybir.dt.from_np(arr.dtype), kind="ExternalInput").ap()
    out = nc.dram_tensor("out_x", _OUT, _mybir.dt.float32, kind="ExternalOutput").ap()
    flamingo(nc, aps, out)
    r = _run(nc, [arrays], core_ids=[0])
    return r.results[0]["out_x"]
```

```python
from contextlib import ExitStack

import concourse.bass as bass
from concourse import mybir

F32 = mybir.dt.float32
BF16 = mybir.dt.bfloat16
U32 = mybir.dt.uint32
I32 = mybir.dt.int32
ACT = mybir.ActivationFunctionType
ALU = mybir.AluOpType
AX = mybir.AxisListType.X

P = 128
B = 32
CB = 4
NC = B // CB
W = CB * P
HEADS = 16
D0 = P // HEADS
D3 = 64
QUARTERS = 4
KV0 = 2 * D0
ROWS0 = P // QUARTERS
VW0 = 2 * P - ROWS0
PARTS0 = P // (2 * D0)
QT0W = HEADS // 2 * P
HQ = HEADS // QUARTERS
UNITS = CB * QUARTERS
DRAIN0, DRAIN3 = 8, 6
DOWN0 = (6, 7, 3, 4)
E0, I0 = 4, 64
MIDDLE1 = (1, 3)
TAPS0 = 4
R0 = 8
H1 = 512
K1 = H1 // P
E2 = 8
E3, H3, TOP3 = 16, 512, 4
K3 = H3 // P
TOKENS = B * P
REGION = TOKENS + P
ROW3 = P + 1
UNUSED = E3 * REGION
GROUP3 = 4
SLOTS3 = 3 * GROUP3
NT = -(-(TOKENS * TOP3 // P + E3 - 1) // SLOTS3) * SLOTS3
GROUPS3 = NT // SLOTS3
PADDED_BY_POOL = 12
SC = CB * TOP3
NOWHERE = float(1 << 22)
EPS = 1e-5
ROUND = 1.5 * 2.0 ** 23
MASKED = -1e30
ARENA = 31000
AHEAD0 = 4
SLICES0 = (0, 1, 3, 4, 8, 11, 12, 13, 14)
CRED = QUARTERS + 1


class Steps:

    def __init__(self, eng, sem):
        self.eng, self.sem, self.base, self.off, self.k, self.at = eng, sem, 0, 0, 0, None

    def loop(self, per):
        self.base, self.off, self.per = self.base + self.k, 0, per
        self.k = 0

    def turn(self, i):
        assert self.k in (0, self.per), self.k
        self.off, self.k = self.per * i, 0

    def end(self, n):
        assert self.k == self.per, self.k
        self.base, self.off, self.k = self.base + self.per * n, 0, 0

    def __call__(self, ins):
        self.k += 1
        ins.then_inc(self.sem, 1)
        self.eng.wait_ge(self.sem, self.off + (self.base + self.k))

    def issue(self, ins):
        self.k += 1
        ins.then_inc(self.sem, 1)
        return self.k

    def until(self, k):
        self.eng.wait_ge(self.sem, self.off + (self.base + k))

    def held(self, ins, mark):
        self(ins)
        self.eng.sem_inc(mark, 1)


def slices_at(u, kA):
    if kA == len(SLICES0):
        return [SLICES0.index(u)] if u in SLICES0 else []
    return list(range(min(u * kA // (UNITS - 1), kA), min((u + 1) * kA // (UNITS - 1), kA)))


def head3(qd, i):
    return qd // 2 * 2 * HQ + 2 * i + qd % 2


def lagging(c, p, u, lag, first, live):
    if u >= lag:
        return (c, p, u - lag) if live else None
    return None if first else (c - 1, 1 - p, u - lag + UNITS)


def flamingo(nc, a, out):
    ctx = ExitStack()
    with ctx:
        def sb(name, shape, dt=F32):
            return ctx.enter_context(nc.sbuf_tensor(name, shape, dt))

        sems = {}

        def sem(name):
            if name not in sems:
                sems[name] = ctx.enter_context(nc.semaphore(name))
            return sems[name]

        bank = [ctx.enter_context(nc.psum_tensor(f"bank{i}", [P, W], F32)) for i in range(8)]

        def b4(i):
            return bank[i][:, :].rearrange("p (j t) -> p j t", j=CB)

        def slice_bank(s, first):
            return bank[(6 - s) % 8] if first else bank[6]

        x = sb("x", [P, B, P])
        ident = sb("ident", [P, P])
        ident16 = sb("ident16", [P, P], BF16)
        ones = sb("ones", [P, P])
        iota8 = sb("iota8", [P, E3])
        round3 = sb("round_constant", [P, 1])
        earlier = sb("earlier", [P, P])
        gates = sb("gates", [P, 9])
        gate3 = sb("gate3", [P, 1])
        graw = sb("graw", [P, 9])

        stats = sb("stats", [P, CB, 6])
        mv = sb("mv", [P, CB, 2])
        ve = sb("ve", [P, CB])
        mhalf = sb("mhalf", [P, CB])
        rstd = sb("rstd", [P, CB])
        xn = sb("xn", [P, CB, P])
        xnT = sb("xnT", [P, W])
        cx = sb("cx", [P, CB, P])
        cxT = sb("cxT", [P, 2, W])
        att = sb("att", [P, 3, 2, CB, P])
        sm, pr, pT = att[:, 0], att[:, 1], att[:, 2]
        ex = att[:, 0:2].rearrange("p a s j t -> p (a s) j t")
        nm = sb("nm", [P, 2, CB])
        sums = sb("sums", [P, CB])
        rs = sb("rs", [P, HEADS])
        tmp = sb("tmp", [P, CB, P])
        tmp2 = sb("tmp2", [P, CB, P])

        arena = sb("arena", [P, ARENA])
        used = [0]

        def fresh():
            used[0] = 0

        def ar(shape, dt=F32):
            n = 1
            for s in shape[1:]:
                n *= s
            words = n if dt != BF16 else (n + 1) // 2
            v = arena[0:shape[0], used[0]:used[0] + words]
            used[0] += words
            assert used[0] <= ARENA
            v = v if dt == F32 else v.bitcast(dt)
            if len(shape) == 3:
                v = v.rearrange("p (a b) -> p a b", a=shape[1])
            if len(shape) == 4:
                v = v.rearrange("p (a b c) -> p a b c", a=shape[1], b=shape[2])
            return v

        wq0, wkv0 = sb("wq0", [P, P]), sb("wkv0", [P, 2, 4 * D0])
        wkvs0 = sb("wkvs0", [P, KV0])
        wo0, bo0 = sb("wo0", [P, P]), sb("bo0", [P, P])
        bq0row, bq0 = sb("bq0row", [P, P]), sb("bq0", [P, CB * HEADS, D0])
        bk0g, bv0g, bkv0 = sb("bk0g", [P, 4 * D0]), sb("bv0g", [P, 4 * D0]), sb("bkv0", [P, KV0])
        wr0, rb0 = sb("wr0", [P, R0]), sb("rb0", [P, R0])
        wg0, wu0 = sb("wg0", [P, E0 * I0]), sb("wu0", [P, E0 * I0])
        wd0 = sb("wd0", [P, 2, 2 * P])
        cw0, cb0 = sb("cw0", [P, TAPS0]), sb("cb0", [1, P])
        wT1 = sb("wT1", [P, 3, P])
        causal = sb("causal", [P, P])
        w1q, w2q = sb("w1q", [P, H1], BF16), sb("w2q", [P, K1, P], BF16)
        wsc1, wsc2 = sb("wsc1", [P, 1]), sb("wsc2", [P, 1])
        cw1, cb1 = sb("cw1", [P, K1, 3]), sb("cb1", [P, K1])
        wT2 = sb("wT2", [P, 3, P])
        bq2, bk2, bv2 = sb("bq2", [P, 1]), sb("bk2", [P, 1]), sb("bv2", [P, P])
        wg2, bg2 = sb("wg2", [P, P]), sb("bg2", [P, P])
        we2, be2 = sb("we2", [P, E2 * P]), sb("be2", [E2, P])
        gam3, bet3 = sb("gam3", [P, 1]), sb("bet3", [P, 1])
        wqk3 = sb("wqk3", [P, 2, HEADS * D3])
        wv3, wo3, bo3 = sb("wv3", [P, HEADS * D3]), sb("wo3", [P, 8, P]), sb("bo3", [P, P])
        wr3, rb3 = sb("wr3", [P, E3]), sb("rb3", [P, E3])
        b13 = sb("b13", [P, E3, K3])

        fresh()
        qraw0, kvraw0 = ar([P, CB * HEADS, D0]), ar([P, CB, KV0])
        q0, qrest0 = ar([P, CB * HEADS, D0]), ar([P, CB * HEADS, D0])
        k0, krest0 = ar([P, CB, D0]), ar([P, CB, D0])
        qs0 = ar([P, CB * HEADS, PARTS0, D0], BF16)
        ks0 = ar([P, CB, 2 * PARTS0, D0], BF16)
        qT0 = ar([P, 2, CB, QT0W], BF16)
        kT0 = ar([P, 2, CB, 2 * P], BF16)
        v0 = ar([P, 2, CB, VW0])
        outT0 = ar([P, W])
        on0, oT0 = ar([P, 2, P]), ar([P, 2, P])
        raw1, raw2 = ar([P, 3, P]), ar([P, 3, P])
        w1n, w2n = ar([P, K1, P]), ar([P, H1])
        wabs = ar([P, 2, H1])
        kr3 = ar([E3, 2, P])
        keyT = ar([P, 2, E3])
        keysq = ar([P, E3])
        part = ar([P, 2])
        fresh()
        xall0 = ar([P, B, P])
        sg0 = ar([P, 2, W])
        up0 = ar([P, 2, W])
        hid0 = ar([P, 2, W])
        cin0 = ar([P, CB, TAPS0 - 1 + P])
        taps0 = ar([P, TAPS0, P])
        lg0, sel0 = ar([P, CB, R0]), ar([P, CB, R0])
        top0, idx0, idf0 = ar([P, CB, 8]), ar([P, CB, 8], U32), ar([P, CB, 8])
        oh0 = ar([P, 2, CB, R0])
        wsum0 = ar([P, CB])
        cwt0 = ar([P, CB, R0])
        ccp0 = ar([P, CB])
        fresh()
        qT1, kT1 = ar([P, W]), ar([P, W])
        v1 = [ar([P, CB, P]) for _ in range(2)]
        fresh()
        am1, sc1 = ar([P, CB]), ar([P, CB])
        xr1 = ar([P, CB, P])
        xq1 = ar([P, CB, P], BF16)
        xqT1 = ar([P, W], BF16)
        iscb1 = ar([P, CB, P])
        sbc1 = ar([P, W])
        hs1, hc1 = ar([P, 2, CB, P]), ar([P, 2, CB, P])
        h1 = ar([P, K1, W])
        am2, sc2, isc2 = ar([P, CB]), ar([P, CB]), ar([P, CB])
        hr1 = ar([P, CB, H1])
        hq1 = ar([P, CB, H1], BF16)
        hqT1 = ar([P, 2, 2 * K1 * P], BF16)
        fresh()
        lg2, top2, idx2, idf2 = ar([P, CB, P]), ar([P, CB, 8]), ar([P, CB, 8], U32), ar([P, CB])
        ex2, ps2, pg2 = ar([P, CB, P]), ar([P, CB]), ar([P, CB])
        oh2 = [ar([P, CB, E2]) for _ in range(2)]
        ohT2 = ar([E2, W])
        acc2 = ar([P, CB, P])
        fresh()
        qk3 = ar([P, 2, HEADS, W])
        v3 = [ar([P, CB, HEADS, D3 + 1]) for _ in range(2)]
        on3 = ar([P, 2, HEADS * D3])
        oT3 = ar([P, 8, P])
        rows3 = ar([P, SC, ROW3])
        rowsu3 = arena[:, used[0] - SC * ROW3:used[0]].bitcast(U32).rearrange("p (q d) -> p q d", q=SC)
        lg3 = ar([P, CB, E3])
        x23, es3 = ar([P, CB]), ar([P, CB])
        top3, idx3, idf3 = ar([P, CB, 8]), ar([P, CB, 8], U32), ar([P, CB, TOP3])
        ex3 = ar([P, CB, TOP3])
        wt3 = ar([P, B * TOP3])
        oh3, dst3 = ar([P, SC, E3]), ar([P, CB, E3])
        ohs3 = ar([P, CB, E3])
        to3, goes3 = ar([P, SC]), ar([P, SC])
        di3 = ar([P, SC], U32)
        run3, first3 = ar([P, E3]), ar([P, E3])
        xr3 = tmp2
        xrT3 = we2[:, 0:W]
        fresh()
        w1T3, w2T3 = ar([P, E3, H3]), ar([P, E3, H3])
        combined = arena[:, 0:2 * TOP3 * W].rearrange("p (s k j d) -> p s k j d", s=2, k=TOP3, j=CB)
        w1n3, w2n3 = ar([P, 2, K3, P]), ar([P, 2, H3])
        w1c3, w2c3, b1c3 = ar([P, 4, H3]), ar([P, 4, H3]), ar([P, 4, K3])
        cum3 = ar([P, 2, E3])
        cnt3, tl3 = ar([P, E3], I32), ar([P, E3])
        tabf3, tab3 = ar([1, 2, NT]), ar([1, 2, NT], I32)
        iota3 = ar([1, NT])
        ends3 = ar([1, E3], I32)
        at = used[0]
        xt3 = ar([P, SLOTS3, ROW3])
        xtu3 = arena[:, at:used[0]].bitcast(U32).rearrange("p (s d) -> p s d", s=SLOTS3)
        yt3 = ar([P, SLOTS3, P])
        until3 = arena[0:1, at:at + NT * E3].rearrange("p (i e) -> p i e", i=NT)
        padf3 = ar([P, ROW3])
        padu3 = arena[:, used[0] - ROW3:used[0]].bitcast(U32)
        b2c3 = tmp
        b2b3 = att[:, 0:2].rearrange("p a s j t -> p (a s j t)")
        h3 = att[:, 2].rearrange("p s k t -> p s (k t)")
        HT1 = (bank[6], bank[7], bank[3], bank[4])
        sent = nc.dram_tensor("dispatched_rows", (UNUSED + P, ROW3), F32, kind="Internal").ap()
        sent_out = nc.dram_tensor("expert_outputs", (TOP3 * TOKENS, P), F32, kind="Internal").ap()

        rows = lambda ap, n=P: ap.rearrange("(a n) -> a n", a=1)[0].partition_broadcast(n)
        col = lambda ap: ap.rearrange("(p a) -> p a", a=1)

        FIRST_LOADS = [
            (x[:, 0:CB, :], a["x"][0:CB].rearrange("b t d -> t b d")), (cx[:, :, :], a["ctx_1024"][0:CB].rearrange("b s e -> s b e")),
            (wkv0[:, 0, :], a["L0_xattn_Wk"]), (wkv0[:, 1, :], a["L0_xattn_Wv"]),
            (bk0g[:, :], rows(a["L0_xattn_bk"])), (bv0g[:, :], rows(a["L0_xattn_bv"])), (bq0row[:, :], rows(a["L0_xattn_bq"])),
            (wq0[:, :], a["L0_xattn_Wq"]), (x[:, CB:2 * CB, :], a["x"][CB:2 * CB].rearrange("b t d -> t b d")),
        ]
        SETUP_LOADS = [
            (x[:, 2 * CB:B, :], a["x"][2 * CB:B].rearrange("b t d -> t b d")),
            (graw[:, 0:4], rows(a["g_xattn"])), (graw[:, 4:8], rows(a["g_ffn"])), (graw[:, 8:9], rows(a["L3_xattn_gate"])),
            (wo0[:, :], a["L0_xattn_Wo"]), (bo0[:, :], rows(a["L0_xattn_bo"])),
            (wr0[:, :], a["L0_ffn_Wr"]), (rb0[:, :], rows(a["L0_ffn_router_bias"])),
            (wg0[:, :].rearrange("p (e i) -> p e i", e=E0), a["L0_ffn_Wg"].rearrange("e h i -> h e i")),
            (wu0[:, :].rearrange("p (e i) -> p e i", e=E0), a["L0_ffn_Wu"].rearrange("e h i -> h e i")),
            (cw0[:, :], a["L0_ffn_conv_w"].rearrange("k a h -> h (k a)")), (cb0[:, :], a["L0_ffn_conv_b"].rearrange("(a d) -> a d", a=1)),
            (raw1[:, 0, :], a["L1_xattn_Wq"]), (raw1[:, 1, :], a["L1_xattn_Wk"]), (raw1[:, 2, :], a["L1_xattn_Wv"]),
            (w1n[:, :, :], a["L1_ffn_w1"].rearrange("(k p) d -> p k d", p=P)), (w2n[:, :], a["L1_ffn_w2"]),
            (cw1[:, :, :], a["L1_ffn_conv_w"].rearrange("(k p) a t -> p k (a t)", p=P)),
            (cb1[:, :], a["L1_ffn_conv_b"].rearrange("(k p) -> p k", p=P)),
            (raw2[:, 0, :], a["L2_xattn_Wq"]), (raw2[:, 1, :], a["L2_xattn_Wk"]), (raw2[:, 2, :], a["L2_xattn_Wv"]),
            (bq2[:, :], col(a["L2_xattn_bq"])), (bk2[:, :], col(a["L2_xattn_bk"])), (bv2[:, :], rows(a["L2_xattn_bv"])),
            (wg2[:, :], a["L2_ffn_Wg"]), (bg2[:, :], rows(a["L2_ffn_bg"])),
            (we2[:, :].rearrange("p (e f) -> p e f", e=E2), a["L2_ffn_We"].rearrange("e d f -> d e f")), (be2[:, :], a["L2_ffn_be"]),
            (gam3[:, :], col(a["L3_xattn_ln_gamma"])), (bet3[:, :], col(a["L3_xattn_ln_beta"])),
            (wqk3[:, 0, :], a["L3_xattn_w_q"]), (wqk3[:, 1, :], a["L3_xattn_w_kv"][:, 0:HEADS * D3]),
            (wv3[:, :], a["L3_xattn_w_kv"][:, HEADS * D3:2 * HEADS * D3]),
            (wo3[:, :, :], a["L3_xattn_w_out"].rearrange("(k p) d -> p k d", p=P)), (bo3[:, :], rows(a["L3_xattn_b_out"])),
            (kr3[:, 0, :], a["L3_ffn_keys"]), (kr3[:, 1, :], a["L3_ffn_rw"]), (rb3[:, :], rows(a["L3_ffn_rb"])),
            (b13[:, :, :], a["L3_ffn_b1"].rearrange("e (k p) -> p e k", p=P)),
        ]
        WD = []
        for e in range(E0):
            pair, u = divmod(e, 2)
            WD.append((wd0[I0 * u:I0 * u + I0, pair, P * u:P * u + P], a["L0_ffn_Wd"][e]))

        s_first, s_load, s_wd, s_zero = sem("first_loaded"), sem("setup_loaded"), sem("wd0_loaded"), sem("wd0_zeroed")
        s_const = sem("constants_ready")
        s_xdone = sem("x_done")
        block = ctx.enter_context(nc.Block())

        def stage_start(eng, s):
            eng.wait_ge(s_xdone, NC * s + 1)

        ATT = ("A0", "A1", "A2", "A3")
        VAR0 = {"A0": 0, "F0": NC, "A1": 2 * NC, "F1": 3 * NC, "A2": 4 * NC, "F2": 5 * NC, "A3": 6 * NC}
        XN0 = {"A0": 0, "F0": NC, "A1": 2 * NC, "A2": 3 * NC, "F2": 4 * NC, "A3": 5 * NC}
        CX0 = {st: i * NC for i, st in enumerate(ATT)}
        s_var, s_rstd, s_xn = sem("variance"), sem("inverse_deviation"), sem("normalised")
        s_cx, s_cT = sem("context_loaded"), sem("context_transposed")
        STAGE = {n: i for i, n in enumerate(("A0", "F0", "A1", "F1", "A2", "F2", "A3", "F3"))}
        n_loads, n_first = len(SETUP_LOADS), len(FIRST_LOADS)

        @block.sync
        def _(sp):
            with nc.allow_non_contiguous_dma(reason="small vectors laid along the partitions"):
                for dst, src in FIRST_LOADS:
                    sp.dma_start(dst, src).then_inc(s_first, 16)
                for dst, src in SETUP_LOADS:
                    sp.dma_start(dst, src).then_inc(s_load, 16)
            sp.wait_ge(s_zero, 1)
            for dst, src in WD:
                sp.dma_start(dst, src).then_inc(s_wd, 16)
            cview = a["ctx_1024"].rearrange("b s e -> s b e")
            for st in ATT:
                if STAGE[st]:
                    stage_start(sp, STAGE[st])
                    sp.wait_ge(s_cT, CX0[st])
                    sp.dma_start(cx[:, :, :], cview[:, 0:CB, :]).then_inc(s_cx, 16)
                else:
                    sp.sem_inc(s_cx, 16)
                with sp.Fori(1, NC) as c:
                    sp.wait_ge(s_cT, c + CX0[st])
                    sp.dma_start(cx[:, :, :], cview[:, bass.ds(c * CB, CB), :]).then_inc(s_cx, 16)
            stage_start(sp, STAGE["F3"])
            s_w, s_wT = [sem("F3_weights_loaded0"), sem("F3_weights_loaded1")], sem("F3_weights_transposed")

            def load_expert(e, p):
                one = bass.ds(e, 1)
                sp.dma_start(w1n3[:, p, :, :], a["L3_ffn_w1"][one].rearrange("e (k p) d -> p (e k) d", p=P)).then_inc(s_w[p], 16)
                sp.dma_start(w2n3[:, p, :], a["L3_ffn_w2"][one].rearrange("e d f -> d (e f)")).then_inc(s_w[p], 16)

            for p in range(2):
                load_expert(p, p)
            sp.dma_start(b2b3[:, :], rows(a["L3_ffn_b2"].rearrange("e d -> (e d)"))).then_inc(sem("F3_b2_loaded"), 16)
            with sp.Fori(1, E3 // 2) as i:
                for p in range(2):
                    sp.wait_ge(s_wT, 4 * i + (2 * p - 2))
                    load_expert(i * 2 + p, p)
            sp.wait_ge(sem("F3_table"), 1)
            with sp.Fori(PADDED_BY_POOL, E3) as e:
                end = sp.value_load(ends3[0:1, bass.ds(e, 1)], min_val=0, max_val=UNUSED - P)
                sp.dma_start(sent[bass.ds(end, P), :], padf3[:, :]).then_inc(sem("F3_last_padded"), 16)
            sp.wait_ge(sem("F3_padded"), 16 * (PADDED_BY_POOL + 1))
            sp.wait_ge(sem("F3_last_padded"), 16 * (E3 - PADDED_BY_POOL))
            sp.wait_ge(sem("F3_dispatched"), 16 * SC * NC)

            def load_tile(i, s):
                at = sp.value_load(tab3[0:1, 1, bass.ds(i, 1)], min_val=0, max_val=UNUSED)
                sp.dma_start(xt3[:, s, :], sent[bass.ds(at, P), :]).then_inc(sem(f"F3_tiles_loaded{s // GROUP3}"), 16)

            for s in range(SLOTS3):
                load_tile(s, s)
            with sp.Fori(1, GROUPS3) as g:
                for s in range(SLOTS3):
                    if s % GROUP3 == 0:
                        sp.wait_ge(sem(f"F3_scattered{s // GROUP3}"), g * (16 * GROUP3))
                    load_tile(g * SLOTS3 + s, s)
            for half in range(SLOTS3 // GROUP3):
                sp.wait_ge(sem(f"F3_scattered{half}"), GROUPS3 * GROUP3 * 16)

            s_out = sem("out_stored")

            def load_outputs(c, p):
                for k in range(TOP3):
                    sp.dma_start(combined[:, p, k, :, :], sent_out[bass.ds(c * W + k * TOKENS, W), :].rearrange("(j t) d -> t j d", t=P))\
                        .then_inc(sem(f"F3_outputs_loaded{p}"), 16)

            def store(c):
                sp.dma_start(out.rearrange("b t d -> t b d")[:, bass.ds(c * CB, CB), :], x[:, bass.ds(c * CB, CB), :]).then_inc(s_out, 16)

            for p in range(2):
                load_outputs(p, p)
            with sp.Fori(0, NC // 2 - 1) as i:
                for p in range(2):
                    sp.wait_ge(s_xdone, i * 2 + (NC * STAGE["F3"] + p + 2))
                    load_outputs(i * 2 + (p + 2), p)
                    store(i * 2 + p)
            for c in (NC - 2, NC - 1):
                sp.wait_ge(s_xdone, NC * STAGE["F3"] + c + 2)
                store(c)
            sp.wait_ge(s_out, 16 * NC)

        @block.gpsimd
        def _(pl):
            step = Steps(pl, sem("pool_steps"))
            s_held = sem("held")
            step(pl.memset(wd0[:, :, :], 0.0))
            pl.memset(rstd[:, :], 0.0).then_inc(s_zero, 1)
            step(pl.memset(ident[:, :], 0.0))
            step(pl.affine_select(out=ident[:, :], in_=ident[:, :], compare_op=ALU.not_equal, fill=1.0, base=0,
                                  pattern=[[-1, P]], channel_multiplier=1))
            pl.tensor_copy(ident16[:, :], ident[:, :])
            pl.memset(ones[:, :], 1.0)
            pl.memset(mhalf[:, :], -0.5)
            pl.memset(round3[:, :], ROUND)
            step(pl.memset(causal[:, :], 0.0))
            step(pl.affine_select(out=causal[:, :], in_=causal[:, :], compare_op=ALU.is_ge, fill=MASKED, base=0,
                                  pattern=[[1, P]], channel_multiplier=-1))
            step(pl.memset(earlier[:, :], 1.0))
            step(pl.affine_select(out=earlier[:, :], in_=earlier[:, :], compare_op=ALU.is_gt, fill=0.0, base=0,
                                  pattern=[[1, P]], channel_multiplier=-1))
            pl.iota(iota8[:, :], pattern=[[1, E3]], base=0, channel_multiplier=0, allow_small_or_imprecise_dtypes=True).then_inc(s_const, 1)

            def power(st, n):
                pl.wait_ge(s_var, n + (1 + VAR0[st]))
                pl.tensor_tensor(rstd[:, :], ve[:, :], mhalf[:, :], ALU.pow).then_inc(s_rstd, 1)

            for s in range(2):
                step(pl.memset(kT0[0:P // 2, s, :, P:2 * P], 0.0))
                step(pl.memset(kT0[P // 2:P, s, :, 0:P], 0.0))
                step(pl.memset(v0[:, s, :, :], 0.0))
                step(pl.memset(v0[:, s, :, P - ROWS0 + D0:P - ROWS0 + D0 + 1], 1.0))
            power("A0", 0)
            power("A0", 1)

            def split(c, p, more):
                pl.wait_ge(sem("A0_raw"), c * 2 + 1)
                pl.tensor_tensor(v0[:, p, :, P - ROWS0:P - ROWS0 + D0], kvraw0[:, :, D0:KV0], bkv0[:, D0:KV0].unsqueeze(1).to_broadcast([P, CB, D0]), ALU.add)
                step.held(pl.tensor_tensor(k0[:, :, :], kvraw0[:, :, 0:D0], bkv0[:, 0:D0].unsqueeze(1).to_broadcast([P, CB, D0]), ALU.add), s_held)
                first, second, third = ks0[:, :, 0:PARTS0:3, :], ks0[:, :, 1:PARTS0:3, :], ks0[:, :, 2:PARTS0:3, :]
                of = lambda t, like: t.unsqueeze(2).to_broadcast(list(like.shape))
                step(pl.tensor_copy(first, of(k0[:, :, :], first)))
                pl.tensor_tensor(krest0[:, :, :], k0[:, :, :], ks0[:, :, 0, :], ALU.subtract)
                step(pl.tensor_tensor(second, of(k0[:, :, :], second), first, ALU.subtract))
                step.held(pl.tensor_tensor(third, of(krest0[:, :, :], third), second[:, :, 0:2, :], ALU.subtract), s_held)
                pl.tensor_copy(ks0[:, :, PARTS0:2 * PARTS0, :], ks0[:, :, 0:PARTS0, :]).then_inc(sem("A0_split"), 1)
                pl.wait_ge(sem("A0_raw"), c * 2 + 2)
                first, second, third = qs0[:, :, 0:3, :], qs0[:, :, 3:6, :], qs0[:, :, 6:8, :]
                pl.tensor_tensor(q0[:, :, :], qraw0[:, :, :], bq0[:, :, :], ALU.add)
                step(pl.tensor_tensor(first, of(qraw0[:, :, :], first), of(bq0[:, :, :], first), ALU.add))
                pl.tensor_tensor(qrest0[:, :, :], q0[:, :, :], qs0[:, :, 0, :], ALU.subtract)
                step(pl.tensor_tensor(second, of(q0[:, :, :], second), first, ALU.subtract))
                pl.tensor_tensor(third, of(qrest0[:, :, :], third), second[:, :, 0:2, :], ALU.subtract).then_inc(sem("A0_split"), 1)
                if more:
                    power("A0", c + 1)

            split(0, 0, False)
            step.loop(2 * 6)
            with pl.Fori(0, NC // 2 - 1) as i:
                step.turn(i)
                for p in range(2):
                    split(i * 2 + (p + 1), 1 - p, True)
            step.end(NC // 2 - 1)
            split(NC - 1, 1, False)

            stage_start(pl, STAGE["F0"])
            power("F0", 0)
            for k in range(TAPS0):
                pl.tensor_scalar(taps0[:, k, :], ident[:, :], cw0[:, k:k + 1], None, ALU.mult)
            pl.memset(cin0[:, :, 0:TAPS0 - 1], 0.0).then_inc(sem("F0_constants"), 1)
            power("F0", 1)

            def hidden(c, first):
                for k in range(2):
                    pl.wait_ge(sem("F0_silu"), c * 2 + (k + 3))
                    if k == 0 and not first:
                        pl.wait_ge(sem("F0_down"), c * CB)
                    pl.tensor_tensor(hid0[:, k, :], up0[:, k, :], sg0[:, k, :], ALU.mult).then_inc(sem("F0_hid"), 1)

            hidden(0, True)
            power("F0", 2)
            with pl.Fori(1, NC - 2) as c:
                hidden(c, False)
                power("F0", c + 2)
            hidden(NC - 2, False)
            hidden(NC - 1, False)

            with pl.Fori(0, NC) as c:
                power("A1", c)
            with pl.Fori(0, NC) as c:
                power("F1", c)
                pl.wait_ge(sem("F1_scale1"), c + 1)
                pl.wait_ge(sem("F1_scaleT"), c + 1)
                pl.sem_inc(s_held, 1)
                pl.tensor_copy(iscb1[:, :, :], am1[:, :].unsqueeze(2).to_broadcast([P, CB, P])).then_inc(sem("F1_scale_spread"), 1)
            with pl.Fori(0, NC) as c:
                power("A2", c)
            with pl.Fori(0, NC) as c:
                power("F2", c)
            stage_start(pl, STAGE["A3"])
            pl.iota(goes3[:, :].rearrange("p (j k) -> p j k", j=CB), pattern=[[P, CB], [TOKENS, TOP3]], base=0, channel_multiplier=1,
                    allow_small_or_imprecise_dtypes=True)
            pl.iota(first3[:, :], pattern=[[REGION, E3]], base=0, channel_multiplier=0, allow_small_or_imprecise_dtypes=True)\
                .then_inc(sem("F3_constants"), 1)
            pl.sem_inc(sem("F3_rows_free"), 1)

            def dispatch(c):
                pl.wait_ge(sem("F3_variance"), c + 1)
                pl.tensor_tensor(rstd[:, :], ve[:, :], mhalf[:, :], ALU.pow).then_inc(sem("F3_inverse_deviation"), 1)
                pl.wait_ge(sem("F3_rows_copied"), c + 2)
                pl.wait_ge(sem("F3_rows_ready"), c + 1)
                pl.sem_inc(s_held, 1)
                for q in range(SC):
                    pl.indirect_dma_start(sent, bass.IndirectOffsetOnAxis(di3[:, q:q + 1], 0), rows3[:, q, :], None)\
                        .then_inc(sem("F3_dispatched"), 16)
                pl.wait_ge(sem("F3_dispatched"), c * (16 * SC) + 16 * SC)
                pl.sem_inc(sem("F3_rows_free"), 1)

            for n in range(6):
                power("A3", n)
            with pl.Fori(0, NC - 3) as c:
                power("A3", c * 2 + 6)
                power("A3", c * 2 + 7)
                dispatch(c)
            dispatch(NC - 3)
            dispatch(NC - 2)

            stage_start(pl, STAGE["F3"])
            pl.iota(iota3[:, :], pattern=[[1, NT]], base=0, channel_multiplier=0, allow_small_or_imprecise_dtypes=True)
            pl.memset(padf3[:, :], 0.0).then_inc(sem("F3_constants"), 1)
            dispatch(NC - 1)
            pl.wait_ge(sem("F3_table"), 1)
            s_pad = sem("F3_padded")
            pl.dma_start(sent[UNUSED:UNUSED + P, :], padf3[:, :]).then_inc(s_pad, 16)
            with pl.Fori(0, PADDED_BY_POOL) as e:
                end = pl.value_load(ends3[0:1, bass.ds(e, 1)], min_val=0, max_val=UNUSED - P)
                pl.dma_start(sent[bass.ds(end, P), :], padf3[:, :]).then_inc(s_pad, 16)
            with pl.Fori(0, GROUPS3) as g:
                for s in range(SLOTS3):
                    pl.wait_ge(sem("F3_output"), g * SLOTS3 + (s + 3))
                    pl.sem_inc(s_held, 1)
                    pl.indirect_dma_start(sent_out, bass.IndirectOffsetOnAxis(xtu3[:, s, P:P + 1], 0), yt3[:, s, :], None,
                                          bounds_check=TOP3 * TOKENS - 1, oob_is_err=False).then_inc(sem(f"F3_scattered{s // GROUP3}"), 16)

        @block.tensor
        def _(pe):
            pe.wait_ge(s_const, 1)
            pe.wait_ge(s_first, 16 * n_first)

            def setup():
                pe.wait_ge(s_load, 16 * n_loads)
                s_bk, s_gone = sem("setup_bank_full"), sem("setup_bank_gone")
                n = [0]

                def group(pairs):
                    i = n[0]
                    for q, (src, parts) in enumerate(pairs):
                        last = nc.tensor.transpose(bank[i][:, q * parts:(q + 1) * parts], src, ident[0:parts, 0:parts])
                    last.then_inc(s_bk, 1)
                    n[0] += 1

                group([(raw1[:, i, :], P) for i in range(3)])
                group([(raw2[:, i, :], P) for i in range(3)])
                group([(kr3[:, t, :], E3) for t in range(2)])
                pe.wait_ge(sem("setup_vector"), 1)
                nc.tensor.matmul(bank[n[0]][:, 0:2], ones[:, :], part[:, :], start=True, stop=True).then_inc(s_bk, 1)
                n[0] += 1
                pe.wait_ge(sem("setup_vector"), 2)
                nc.tensor.matmul(bank[n[0]][:, 0:E3], ones[:, :], keysq[:, :], start=True, stop=True).then_inc(s_bk, 1)
                n[0] += 1
                pe.wait_ge(sem("setup_vector"), 4)
                group([(wabs[:, 0, q * P:(q + 1) * P], P) for q in range(4)])
                group([(wabs[:, 1, q * P:(q + 1) * P], P) for q in range(4)])
                pe.wait_ge(sem("setup_done"), 1)

            def transpose_x(st, c):
                pe.wait_ge(s_xn, c + (1 + XN0[st]))
                for j in range(CB):
                    last = nc.tensor.transpose(bank[0][:, j * P:j * P + P], xn[:, j, :], ident[:, :])
                return last

            def routing(c, u):
                if u == 8:
                    pe.wait_ge(sem("F3_normalised"), c + 1)
                    for j in range(CB):
                        last = nc.tensor.transpose(bank[5][:, j * P:j * P + P], xr3[:, j, :], ident[:, :])
                    last.then_inc(sem("F3_xT"), 1)
                if u == 9:
                    pe.wait_ge(sem("F3_xnT"), c + 1)
                    for j in range(CB):
                        last = nc.tensor.matmul(bank[5][:, j * E3:j * E3 + E3], xrT3[:, j * P:j * P + P], wr3[:, :], start=True, stop=True)
                    last.then_inc(sem("F3_lg"), 1)
                if u == 12:
                    pe.wait_ge(sem("F3_chosen"), c + 1)
                    chosen = ohs3[:, :, :].rearrange("p j e -> p (j e)")
                    nc.tensor.matmul(bank[5][:, 0:CB * E3], earlier[:, :], chosen, start=True, stop=True)
                    nc.tensor.matmul(bank[5][:, CB * E3:2 * CB * E3], ones[:, :], chosen, start=True, stop=True).then_inc(sem("F3_counts"), 1)

            def heads(st):
                l0 = st == "A0"
                kA = len(SLICES0) if l0 else 2 + HEADS + 2 * CB

                def piece(c, p, s, first=False):
                    A = slice_bank(s, first)
                    A16 = A[:, :].bitcast(BF16)
                    if not first:
                        pe.wait_ge(sem(st + "_slice_gone"), c * kA + (s + 1))
                    elif s >= 8:
                        pe.wait_ge(sem(st + "_slice_gone"), s - 6)
                    if s == 0:
                        pe.wait_ge(s_xn, c + (1 + XN0[st]))
                        for j in range(CB):
                            last = nc.tensor.transpose(A[:, j * P:j * P + P], xn[:, j, :], ident[:, :])
                        last.then_inc(sem(st + "_slice"), 1)
                        return
                    if s == 1:
                        pe.wait_ge(s_cx, c * 16 + (16 + 16 * CX0[st]))
                        for j in range(CB):
                            last = nc.tensor.transpose(A[:, j * P:j * P + P], cx[:, j, :], ident[:, :])
                        last.then_inc(sem(st + "_slice"), 1)
                        return
                    if l0 and s == 2:
                        pe.wait_ge(sem(st + "_cxT"), c + 1)
                        for j in range(CB):
                            last = nc.tensor.matmul(A[:, j * KV0:j * KV0 + KV0], cxT[:, p, j * P:j * P + P], wkvs0[:, :], start=True, stop=True)
                    elif l0 and s == 3:
                        pe.wait_ge(sem(st + "_xnT"), c + 1)
                        for j in range(CB):
                            last = nc.tensor.matmul(A[:, j * P:j * P + P], xnT[:, j * P:j * P + P], wq0[:, :], start=True, stop=True)
                    elif l0 and s == 4:
                        pe.wait_ge(sem("A0_split"), c * 2 + 1)
                        for j in range(CB):
                            last = nc.tensor.transpose(A16[:, j * P:j * P + P], ks0[:, j, :, :].rearrange("p a d -> p (a d)"), ident16[:, :])
                    elif l0:
                        j = s - 5
                        pe.wait_ge(sem("A0_split"), c * 2 + 2)
                        for i in range(HEADS // 2):
                            h = j * HEADS + 2 * i
                            last = nc.tensor.transpose(A16[:, i * P:i * P + P], qs0[:, h:h + 2, :, :].rearrange("p h a d -> p (h a d)"), ident16[:, :])
                    elif s < 2 + HEADS:
                        t, pair = divmod(s - 2, HEADS // 2)
                        pe.wait_ge(sem(st + ("_cxT" if t else "_xnT")), c + 1)
                        last = nc.tensor.matmul(A[:, :], wqk3[:, t, pair * P:pair * P + P], cxT[:, p, :] if t else xnT[:, :], start=True, stop=True)
                    else:
                        j, half = divmod(s - 2 - HEADS, 2)
                        pe.wait_ge(sem(st + "_cxT"), c + 1)
                        last = nc.tensor.matmul(A[:, :], cxT[:, p, j * P:j * P + P], wv3[:, half * W:half * W + W], start=True, stop=True)
                    last.then_inc(sem(st + "_slice"), 1)

                def body(c, p, more, first=False, live=True):
                    for u in range(UNITS if live else (DRAIN0 if l0 else DRAIN3)):
                        if live:
                            j, qd = divmod(u, QUARTERS)
                            pe.wait_ge(sem(st + "_less_max"), c * UNITS + (u - 1 + CRED))
                            if u == 0:
                                pe.wait_ge(sem(st + "_slices_ready"), c + 1)
                            if l0:
                                for i in range(HQ // 2):
                                    pair = qd * (HQ // 2) + i
                                    last = nc.tensor.matmul(bank[u % 2][:, 2 * i * P:2 * i * P + 2 * P], qT0[:, p, j, pair * P:pair * P + P],
                                                            kT0[:, p, j, :], start=True, stop=True)
                            else:
                                r = slice(D3 * (qd % 2), D3 * (qd % 2) + D3)
                                for i in range(HQ):
                                    q, k = (qk3[r, p, t + qd // 2 * HQ + i, j * P:j * P + P] for t in (0, HEADS // 2))
                                    last = nc.tensor.matmul(bank[u % 2][:, i * P:i * P + P], q, k, start=True, stop=True)
                            last.then_inc(sem(st + "_scores"), 1)
                        unit = lagging(c, p, u, 2, first, live)
                        if unit:
                            cc, pp, v = unit
                            pe.wait_ge(sem(st + "_exp"), cc * UNITS + (v + 1 + CRED))
                            pe.wait_ge(sem(st + "_pT"), cc * UNITS + (v - 1 + CRED))
                            for i in range(HQ):
                                last = nc.tensor.transpose(bank[2 + v % 2][:, i * P:i * P + P], ex[:, v % 4, i, :], ident[:, :])
                            last.then_inc(sem(st + "_pT_full"), 1)
                        mine = slices_at(u, kA) if more else []
                        for s in mine[:1]:
                            piece(c + 1, 1 - p, s)
                        unit = lagging(c, p, u, 3, first, live)
                        if unit:
                            cc, pp, v = unit
                            j, qd = divmod(v, QUARTERS)
                            pe.wait_ge(sem(st + "_pT"), cc * UNITS + (v + 1 + CRED))
                            if l0:
                                if qd == 0:
                                    pe.wait_ge(sem("A0_oT"), cc * (2 * CB) + (2 * j + 1))
                                at = P - ROWS0 * (qd + 1)
                                last = nc.tensor.matmul(bank[4 + j % 2][:, :], v0[:, pp, j, at:at + P], pT[:, v % 2, :, :].rearrange("p i t -> p (i t)"),
                                                        start=(qd == 0), stop=(qd == QUARTERS - 1))
                            else:
                                pe.wait_ge(sem("A3_normal"), cc * UNITS + (v + 1))
                                for i in range(HQ):
                                    last = nc.tensor.matmul(bank[4][:, i * (D3 + 1):(i + 1) * (D3 + 1)], pT[:, v % 2, i, :],
                                                            v3[pp][:, j, head3(qd, i), :], start=True, stop=True)
                            last.then_inc(sem(st + "_pv_done"), 1)
                        for s in mine[1:]:
                            piece(c + 1, 1 - p, s)
                        if not l0 and not first:
                            if u in (9, 13) and live:
                                pe.wait_ge(sem("A3_oT"), c * (2 * CB) + (3 if u == 9 else 5))
                            if live:
                                routing(c - 1, u - 1)
                            if u == 11 and live:
                                pe.wait_ge(sem("F3_chosen"), c)
                            if u == 15 and live:
                                pe.wait_ge(sem("F3_rows_ready"), c)
                        for part_, lag in enumerate((7, 9) if l0 else (7, 8)):
                            unit = lagging(c, p, u, lag, first, live)
                            if unit and unit[2] % QUARTERS == 0:
                                cc, j = unit[0], unit[2] // QUARTERS
                                if l0 and part_ == 0:
                                    pe.wait_ge(sem("A0_oT"), cc * (2 * CB) + (2 * j + 4))
                                    for i in range(HQ):
                                        last = nc.tensor.transpose(bank[4 + j % 2][:, i * P:i * P + P], outT0[:, i * P:i * P + P], ident[:, :])
                                    last.then_inc(sem("A0_oT_full"), 1)
                                elif l0:
                                    pe.wait_ge(sem("A0_normal"), cc * CB + (j + 1))
                                    nc.tensor.transpose(bank[4 + j % 2][:, 0:P], on0[:, j % 2, :], ident[:, :]).then_inc(sem("A0_oT_full"), 1)
                                else:
                                    pe.wait_ge(sem("A3_normal"), cc * UNITS + (QUARTERS * (j + 1) + 1))
                                    pe.wait_ge(sem("A3_oT"), cc * (2 * CB) + (2 * j + part_ + 1))
                                    for q in range(4):
                                        k = 4 * part_ + q
                                        last = nc.tensor.transpose(bank[5][:, q * P:q * P + P], on3[:, j % 2, k * P:k * P + P], ident[:, :])
                                    last.then_inc(sem("A3_oT_full"), 1)
                        unit = lagging(c, p, u, 10 if l0 else 9, first, live)
                        if unit and unit[2] % QUARTERS == 0:
                            cc, j = unit[0], unit[2] // QUARTERS
                            if j == 0:
                                pe.wait_ge(s_xdone, cc + (NC * STAGE[st] + 1))
                            if l0:
                                pe.wait_ge(sem("A0_oT"), cc * (2 * CB) + (2 * j + 5))
                                nc.tensor.matmul(bank[7][:, j * P:j * P + P], oT0[:, j % 2, :], wo0[:, :], start=True, stop=True)\
                                    .then_inc(sem(st + "_y"), 1)
                            else:
                                pe.wait_ge(sem("A3_oT"), cc * (2 * CB) + (2 * j + 3))
                                for k in range(8):
                                    last = nc.tensor.matmul(bank[7][:, j * P:j * P + P], oT3[:, k, :], wo3[:, k, :], start=(k == 0), stop=(k == 7))
                                last.then_inc(sem(st + "_y"), 1)

                for s in range(kA):
                    if l0 and s == AHEAD0:
                        pe.wait_ge(sem("A0_slice_gone"), AHEAD0 + 1)
                        setup()
                    piece(0, 0, s, first=True)
                body(0, 0, True, True)
                with pe.Fori(0, NC // 2 - 2) as i:
                    for p in range(2):
                        body(i * 2 + (p + 1), 1 - p, True)
                body(NC - 3, 1, True)
                body(NC - 2, 0, True)
                body(NC - 1, 1, False)
                body(NC, 0, False, live=False)

            heads("A0")

            stage_start(pe, STAGE["F0"])

            def router(c):
                pe.wait_ge(sem("F0_xnT"), c + 1)
                pe.wait_ge(sem("F0_conv_in"), c + 1)
                for j in range(CB):
                    last = nc.tensor.matmul(bank[0][:, j * R0:j * R0 + R0], xnT[:, j * P:j * P + P], wr0[:, :], start=True, stop=True)
                last.then_inc(sem("F0_router"), 1)

            def gate_up(c, k):
                pe.wait_ge(sem("F0_silu"), c * 2 + (k + 1))
                nc.tensor.matmul(bank[1 + 2 * k][:, :], wg0[:, k * P:k * P + P], xnT[:, :], start=True, stop=True).then_inc(sem("F0_gate"), 1)
                nc.tensor.matmul(bank[2 + 2 * k][:, :], wu0[:, k * P:k * P + P], xnT[:, :], start=True, stop=True).then_inc(sem("F0_up"), 1)

            def conv(c):
                pe.wait_ge(sem("F0_conv_in"), c + 1)
                pe.wait_ge(s_xdone, c + (NC * STAGE["F0"] + 1))
                for j in range(CB):
                    for k in range(TAPS0):
                        nc.tensor.matmul(bank[5][:, j * P:j * P + P], cin0[:, j, k:k + P], taps0[:, k, :], start=(k == 0), stop=False)
                    last = nc.tensor.matmul(bank[5][:, j * P:j * P + P], ones[0:1, :], cb0[:, :], start=False, stop=True)
                last.then_inc(sem("F0_conv"), 1)

            def f0(c, more):
                conv(c)
                pe.wait_ge(sem("F0_hid"), c * 2 + 4)
                for j in range(CB):
                    if j == 2 and more:
                        pe.wait_ge(sem("F0_tanh"), c + 2)
                        transpose_x("F0", c + 1).then_inc(sem("F0_xT"), 1)
                    for k in range(2):
                        last = nc.tensor.matmul(bank[DOWN0[j]][:, k * 2 * P:(k + 1) * 2 * P], hid0[:, k, j * P:j * P + P], wd0[:, k, :],
                                                start=True, stop=True)
                    last.then_inc(sem("F0_down"), 1)
                if more:
                    router(c + 1)
                    gate_up(c + 1, 0)
                if more:
                    pe.wait_ge(sem("F0_down_read"), c * CB + CB)
                    gate_up(c + 1, 1)

            pe.wait_ge(s_wd, 64)
            pe.wait_ge(sem("F0_constants"), 1)
            transpose_x("F0", 0).then_inc(sem("F0_xT"), 1)
            router(0)
            for k in range(2):
                gate_up(0, k)
            with pe.Fori(0, NC - 1) as c:
                f0(c, True)
            f0(NC - 1, False)

            def single(st):
                before = 0 if st == "A1" else NC
                stage_start(pe, STAGE[st])
                wT = wT1 if st == "A1" else wT2

                def front(c, p, first, back):
                    if not first:
                        pe.wait_ge(sem("A12_xnT"), c + before)
                    transpose_x(st, c).then_inc(sem("A12_xT"), 1)
                    pe.wait_ge(s_cx, c * 16 + (16 + 16 * CX0[st]))
                    if not first:
                        pe.wait_ge(sem("A12_cxT"), c + before)
                    for j in range(CB):
                        last = nc.tensor.transpose(bank[1][:, j * P:j * P + P], cx[:, j, :], ident[:, :])
                    last.then_inc(s_cT, 1)
                    pe.wait_ge(sem("A12_xnT"), c + 1 + before)
                    if not first:
                        pe.wait_ge(sem("A12_qT"), c + before)
                    nc.tensor.matmul(bank[2][:, :], wT[:, 0, :], xnT[:, :], start=True, stop=True).then_inc(sem("A12_q"), 1)
                    pe.wait_ge(sem("A12_cxT"), c + 1 + before)
                    if not first:
                        pe.wait_ge(sem("A12_kT"), c + before)
                    nc.tensor.matmul(bank[3][:, :], wT[:, 1, :], cxT[:, 0, :], start=True, stop=True).then_inc(sem("A12_k"), 1)
                    if back and st == "A2":
                        probs_T(c - 1)
                    if not first:
                        pe.wait_ge(sem("A12_v_sb"), c + before)
                    for j in range(CB):
                        last = nc.tensor.matmul(bank[4][:, j * P:j * P + P], cxT[:, 0, j * P:j * P + P], wT[:, 2, :], start=True, stop=True)
                    last.then_inc(sem("A12_v"), 1)
                    pe.wait_ge(sem("A12_qT"), c + 1 + before)
                    pe.wait_ge(sem("A12_kT"), c + 1 + before)
                    if not first:
                        pe.wait_ge(sem(st + "_less_max"), c)
                    for j in range(CB):
                        js = slice(j * P, j * P + P)
                        lhs, rhs = (kT1, qT1) if st == "A1" else (qT1, kT1)
                        last = nc.tensor.matmul(bank[7][:, js], lhs[:, js], rhs[:, js], start=True, stop=True)
                    last.then_inc(sem("A12_scores"), 1)
                    if back:
                        pv(c - 1, 1 - p)

                def probs_T(c):
                    pe.wait_ge(sem("A12_exp"), c + 1 + before)
                    for j in range(CB):
                        last = nc.tensor.transpose(bank[5][:, j * P:j * P + P], pr[:, 0, j, :], ident[:, :])
                    last.then_inc(sem(st + "_pT_full"), 1)

                def pv(c, p):
                    pe.wait_ge(sem("A12_v_sb"), c + 1 + before)
                    pe.wait_ge(s_xdone, c + (NC * STAGE[st] + 1))
                    if st == "A1":
                        pe.wait_ge(sem(st + "_normal"), c + 1)
                        src = pr
                    else:
                        pe.wait_ge(sem(st + "_pT"), c + 1)
                        src = pT
                    for j in range(CB):
                        last = nc.tensor.matmul(bank[6][:, j * P:j * P + P], src[:, 0, j, :], v1[p][:, j, :], start=True, stop=True)
                    last.then_inc(sem("A12_pv_done"), 1)

                front(0, 0, True, False)
                with pe.Fori(0, NC // 2 - 1) as i:
                    for p in range(2):
                        front(i * 2 + (p + 1), 1 - p, False, True)
                front(NC - 1, 1, False, True)
                if st == "A2":
                    probs_T(NC - 1)
                pv(NC - 1, 1)

            single("A1")

            stage_start(pe, STAGE["F1"])

            b0h = bank[0][:, :].bitcast(BF16)

            def up1(c, first):
                pe.wait_ge(sem("F1_xq"), c + 1)
                if not first:
                    pe.wait_ge(sem("F1_hqT"), c * 2 - 1)
                for j in range(CB):
                    last = nc.tensor.transpose(b0h[:, j * P:j * P + P], xq1[:, j, :], ident16[:, :])
                last.then_inc(sem("F1_xT"), 1)
                pe.wait_ge(sem("F1_xqT"), c + 1)
                up1_products(c, first, (0, 1))

            def up1_products(c, first, ks):
                for k in ks:
                    if not first:
                        pe.wait_ge(sem("F1_hs"), c * K1 + (k + 1 - K1))
                    nc.tensor.matmul(bank[1 + k][:, :], w1q[:, k * P:k * P + P], xqT1[:, :], start=True, stop=True).then_inc(sem("F1_h"), 1)

            def scales(c):
                pe.wait_ge(sem("F1_scale_spread"), c + 1)
                for j in range(CB):
                    last = nc.tensor.transpose(bank[0][:, j * P:j * P + P], iscb1[:, j, :], ident[:, :])
                last.then_inc(sem("F1_scaleT"), 1)

            def tokens_back(c, j):
                for k in range(K1):
                    last = nc.tensor.transpose(HT1[j][:, k * P:k * P + P], h1[:, k, j * P:j * P + P], ident[:, :])
                last.then_inc(sem("F1_hT"), 1)

            def f1(c, more):
                pe.wait_ge(sem("F1_silu"), c * K1 + K1)
                for j in range(CB):
                    tokens_back(c, j)
                if more:
                    up1(c + 1, False)
                    scales(c + 1)
                    pe.wait_ge(sem("F1_round2"), c * CB + CB)
                    up1_products(c + 1, False, (2, 3))
                for q in range(2):
                    pe.wait_ge(sem("F1_hq"), c * CB + (2 * q + 2))
                    if q == 0:
                        pe.wait_ge(sem("F1_sbc"), c + (2 if more else 1))
                    pe.wait_ge(sem("F1_hqT"), c * 2 + (q + 1))
                    for k in range(2 * K1):
                        last = nc.tensor.transpose(b0h[:, k * P:k * P + P], hq1[:, 2 * q + k // K1, k % K1 * P:k % K1 * P + P], ident16[:, :])
                    last.then_inc(sem("F1_hqT_full"), 1)
                    pe.wait_ge(sem("F1_hqT"), c * 2 + (q + 2))
                    if q == 0:
                        pe.wait_ge(s_xdone, c + (NC * STAGE["F1"] + 1))
                    for j in (2 * q, 2 * q + 1):
                        for k in range(K1):
                            kk = j % 2 * K1 + k
                            last = nc.tensor.matmul(bank[5][:, j * P:j * P + P], hqT1[:, q, kk * P:kk * P + P], w2q[:, k, :],
                                                    start=(k == 0), stop=(k == K1 - 1))
                    last.then_inc(sem("F1_y"), 1)

            up1(0, True)
            scales(0)
            up1_products(0, True, (2, 3))
            with pe.Fori(0, NC - 1) as c:
                f1(c, True)
            f1(NC - 1, False)

            single("A2")

            stage_start(pe, STAGE["F2"])

            xT2 = [xnT, cx[:, :, :].rearrange("p j d -> p (j d)")]

            def logits(c, p):
                pe.wait_ge(sem("F2_xnT"), c + 1)
                pe.wait_ge(sem("F2_logits_read"), c + 1)
                for j in range(CB):
                    last = nc.tensor.matmul(bank[1][:, j * P:j * P + P], xT2[p][:, j * P:j * P + P], wg2[:, :], start=True, stop=True)
                last.then_inc(sem("F2_logits"), 1)

            def experts(c, p, units):
                for u in units:
                    j, half = u // 4 * 2 + u % 2, u // 2 % 2
                    pe.wait_ge(sem("F2_z_read"), c * (2 * CB) + (u + 1))
                    nc.tensor.matmul(bank[2 + u % 4][:, :], xT2[p][:, j * P:j * P + P], we2[:, half * W:half * W + W],
                                     start=True, stop=True).then_inc(sem("F2_z"), 1)

            def chosen(c, p):
                pe.wait_ge(sem("F2_onehot"), c + 1)
                for j in range(CB):
                    last = nc.tensor.transpose(bank[6][0:E2, j * P:j * P + P], oh2[p][:, j, :], ident[:, :])
                last.then_inc(sem("F2_ohT_full"), 1)

            def bias(c):
                pe.wait_ge(sem("F2_ohT"), c + 1)
                pe.wait_ge(s_xdone, c + (NC * STAGE["F2"] + 1))
                for j in range(CB):
                    last = nc.tensor.matmul(bank[7][:, j * P:j * P + P], ohT2[:, j * P:j * P + P], be2[:, :], start=True, stop=True)
                last.then_inc(sem("F2_bias"), 1)

            def f2(c, p, next1, next2):
                if next1:
                    logits(c + 1, 1 - p)
                experts(c, p, range(4, 8))
                if next1:
                    chosen(c + 1, 1 - p)
                    experts(c + 1, 1 - p, range(4))
                    bias(c + 1)
                if next2:
                    transpose_x("F2", c + 2).then_inc(sem("F2_xT"), 1)

            transpose_x("F2", 0).then_inc(sem("F2_xT"), 1)
            logits(0, 0)
            transpose_x("F2", 1).then_inc(sem("F2_xT"), 1)
            chosen(0, 0)
            experts(0, 0, range(4))
            bias(0)
            with pe.Fori(0, NC // 2 - 1) as i:
                for p in range(2):
                    f2(i * 2 + p, p, True, True)
            f2(NC - 2, 0, True, False)
            f2(NC - 1, 1, False, False)

            stage_start(pe, STAGE["A3"])
            heads("A3")

            stage_start(pe, STAGE["F3"])

            def expert_T(e, p):
                pe.wait_ge(sem(f"F3_weights_loaded{p}"), e * 16 + (32 - 16 * p))
                pe.wait_ge(sem("F3_w_sb"), e * 2 + 1)
                for k in range(K3):
                    last = nc.tensor.transpose(bank[2 * p][:, k * P:k * P + P], w1n3[:, p, k, :], ident[:, :])
                last.then_inc(sem("F3_weights_transposed"), 1)
                pe.wait_ge(sem("F3_w_sb"), e * 2 + 2)
                for k in range(K3):
                    last = nc.tensor.transpose(bank[2 * p + 1][:, k * P:k * P + P], w2n3[:, p, k * P:k * P + P], ident[:, :])
                last.then_inc(sem("F3_weights_transposed"), 1)

            routing(NC - 1, 8)
            for e in range(2):
                expert_T(e, e)
            routing(NC - 1, 9)
            for e in range(2, 4):
                expert_T(e, e % 2)
            routing(NC - 1, 12)
            with pe.Fori(2, E3 // 2) as i:
                for p in range(2):
                    expert_T(i * 2 + p, p)

            def tile_T(turn, s):
                pe.wait_ge(sem(f"F3_tiles_loaded{s % SLOTS3 // GROUP3}"), turn * (16 * GROUP3) + 16 * GROUP3)
                nc.tensor.transpose(bank[6 + s % 2][:, 0:P], xt3[:, s % SLOTS3, 0:P], ident[:, :]).then_inc(sem("F3_tile_T"), 1)

            def up(n, s):
                pe.wait_ge(sem("F3_tile_xT"), n + 1)
                pe.wait_ge(sem("F3_tile_weights"), n + 1)
                for k in range(K3):
                    last = nc.tensor.matmul(bank[s % 2][:, k * P:k * P + P], w1c3[:, s % 4, k * P:k * P + P],
                                            xnT[:, (s % 4) * P:(s % 4) * P + P], start=True, stop=True)
                last.then_inc(sem("F3_up"), 1)

            def down(n, s):
                pe.wait_ge(sem("F3_gelu"), n + 1)
                pe.wait_ge(sem("F3_output"), n + 1)
                for k in range(K3):
                    last = nc.tensor.matmul(bank[2 + s % 2][:, 0:P], h3[:, s % 2, k * P:k * P + P], w2c3[:, s % 4, k * P:k * P + P],
                                            start=(k == 0), stop=(k == K3 - 1))
                last.then_inc(sem("F3_down"), 1)

            pe.wait_ge(sem("F3_w_sb"), 2 * E3 + 4)
            tile_T(0, 0)
            tile_T(0, 1)
            up(0, 0)
            with pe.Fori(0, GROUPS3 - 1) as g:
                for s in range(SLOTS3):
                    tile_T(g + (s + 2) // SLOTS3, s + 2)
                    up(g * SLOTS3 + (s + 1), s + 1)
                    down(g * SLOTS3 + s, s)
            for s in range(SLOTS3):
                n = NT - SLOTS3 + s
                if n + 2 < NT:
                    tile_T(GROUPS3 - 1, s + 2)
                if n + 1 < NT:
                    up(n + 1, s + 1)
                down(n, s)

        @block.scalar
        def _(act):
            copy = lambda o, i: nc.scalar.activation(o, i, ACT.Copy)
            aff = lambda o, i, s, b: nc.scalar.activation(o, i, ACT.Identity, bias=b, scale=s)
            exp = lambda o, i: nc.scalar.activation(o, i, ACT.Exp)
            s_held = sem("held")

            def setup():
                act.wait_ge(s_load, 16 * n_loads)
                s_bk, s_gone = sem("setup_bank_full"), sem("setup_bank_gone")
                nc.scalar.activation(gates[:, :], graw[:, :], ACT.Tanh).then_inc(sem("setup_gates"), 1)
                n = [0]

                def out_of_bank(dst, cols):
                    act.wait_ge(s_bk, n[0] + 1)
                    src = bank[n[0]][:, 0:cols]
                    if len(dst.shape) == 3:
                        src = src.rearrange("p (a b) -> p a b", a=dst.shape[1])
                    copy(dst, src).then_inc(s_gone, 1)
                    n[0] += 1

                out_of_bank(wT1[:, :, :], 3 * P)
                out_of_bank(wT2[:, :, :], 3 * P)
                out_of_bank(keyT[:, :, :], 2 * E3)
                act.wait_ge(sem("setup_vector"), 3)
                n[0] += 2
                out_of_bank(w1q[:, :], W)
                out_of_bank(w2q[:, :, :], W)
                act.wait_ge(sem("setup_done"), 1)

            def routing(c, u):
                if u == 8:
                    act.wait_ge(sem("F3_xT"), c + 1)
                    copy(xrT3, b4(5).rearrange("p j t -> p (j t)")).then_inc(sem("F3_xnT"), 1)
                    act.wait_ge(sem("F3_rows_free"), c + 1)
                    copy(rows3[:, :, 0:P].rearrange("p (j k) d -> p j k d", j=CB), xr3[:, :, :].unsqueeze(2).to_broadcast([P, CB, TOP3, P]))\
                        .then_inc(sem("F3_rows_copied"), 1)
                if u == 10:
                    act.wait_ge(sem("F3_less_max"), c + 1)
                    exp(ex3[:, :, :], top3[:, :, 0:TOP3]).then_inc(sem("F3_exp"), 1)

            def heads(st):
                l0 = st == "A0"
                kA = len(SLICES0) if l0 else 2 + HEADS + 2 * CB

                def piece(c, p, s, first=False):
                    A = slice_bank(s, first)
                    A16 = A[:, :].bitcast(BF16)
                    act.wait_ge(sem(st + "_slice"), c * kA + (s + 1))
                    gone = sem(st + "_slice_gone")
                    if s == 0:
                        if l0:
                            copy(xnT[:, :], A[:, :]).then_inc(sem(st + "_xnT"), 1)
                        else:
                            aff(xnT[:, :], A[:, :], gam3[:, 0:1], bet3[:, 0:1]).then_inc(sem(st + "_xnT"), 1)
                        act.wait_ge(sem(st + "_xnT"), c + 1)
                        act.sem_inc(gone, 1)
                        return
                    if s == 1:
                        copy(cxT[:, p, :], A[:, :]).then_inc(sem(st + "_cxT"), 1)
                        act.wait_ge(sem(st + "_cxT"), c + 1)
                        act.sem_inc(gone, 1)
                        act.sem_inc(s_cT, 1)
                        return
                    if l0 and s < 4:
                        if s == 2:
                            copy(kvraw0[:, :, :], A[:, 0:CB * KV0].rearrange("p (j d) -> p j d", j=CB)).then_inc(sem("A0_raw"), 1)
                        else:
                            nc.scalar.activation(qraw0[:, :, :], A[:, :].rearrange("p (h d) -> p h d", d=D0), ACT.Copy, scale=float(D0) ** -0.5)\
                                .then_inc(sem("A0_raw"), 1)
                        act.wait_ge(sem("A0_raw"), c * 2 + (s - 1))
                        act.sem_inc(gone, 1)
                        return
                    if l0 and s == 4:
                        for q in range(2):
                            half = slice(q * (P // 2), (q + 1) * (P // 2))
                            i = copy(kT0[half, p, :, q * P:q * P + P], A16[half, 0:W].rearrange("p (j t) -> p j t", j=CB))
                    elif l0:
                        i = copy(qT0[:, p, s - 5, :], A16[:, :])
                    elif s < 2 + HEADS:
                        i = nc.scalar.activation(qk3[:, p, s - 2, :], A[:, :], ACT.Copy, scale=float(D3) ** -0.5 if s - 2 < HEADS // 2 else 1.0)
                    else:
                        j, half = divmod(s - 2 - HEADS, 2)
                        i = copy(v3[p][:, j, 8 * half:8 * half + 8, 0:D3], A[:, :].rearrange("p (h d) -> p h d", d=D3))
                    i.then_inc(gone, 1)
                    if s == kA - 1:
                        act.wait_ge(gone, c * kA + (kA + 1))
                        act.sem_inc(sem(st + "_slices_ready"), 1)

                def body(c, p, more, first=False, live=True):
                    for u in range(UNITS if live else (DRAIN0 if l0 else DRAIN3)):
                        unit = lagging(c, p, u, 7, first, live)
                        if l0 and unit and unit[2] % QUARTERS == 0:
                            act.wait_ge(sem("A0_pv_done"), unit[0] * UNITS + (unit[2] + QUARTERS + CRED))
                            copy(outT0[:, :], bank[4 + unit[2] // QUARTERS % 2][:, :]).then_inc(sem("A0_oT"), 1)
                        unit = lagging(c, p, u, 2, first, live)
                        if unit:
                            cc, pp, v = unit
                            act.wait_ge(sem(st + "_pT_full"), cc * UNITS + (v + 1))
                            act.wait_ge(sem(st + "_pv_done"), cc * UNITS + (v - 1 + CRED))
                            copy(pT[:, v % 2, :, :], b4(2 + v % 2)).then_inc(sem(st + "_pT"), 1)
                        mine = slices_at(u, kA) if more else []
                        for s in mine[:1]:
                            piece(c + 1, 1 - p, s)
                        if live:
                            act.wait_ge(sem(st + "_less_max"), c * UNITS + (u + 1 + CRED))
                            exp(ex[:, u % 4, :, :], ex[:, u % 4, :, :]).then_inc(sem(st + "_exp"), 1)
                        for s in mine[1:]:
                            piece(c + 1, 1 - p, s)
                        for part_, lag in enumerate((9,) if l0 else (7, 8)):
                            unit = lagging(c, p, u, lag, first, live)
                            if unit and unit[2] % QUARTERS == 0:
                                cc, j = unit[0], unit[2] // QUARTERS
                                if l0:
                                    act.wait_ge(sem("A0_oT_full"), cc * (2 * CB) + (2 * j + 2))
                                    copy(oT0[:, j % 2, :], bank[4 + j % 2][:, 0:P]).then_inc(sem("A0_oT"), 1)
                                else:
                                    act.wait_ge(sem("A3_oT_full"), cc * (2 * CB) + (2 * j + part_ + 5))
                                    act.wait_ge(sem("A3_y"), cc * CB + (j + 1))
                                    copy(oT3[:, 4 * part_:4 * part_ + 4, :], b4(5)).then_inc(sem("A3_oT"), 1)
                        if not l0 and not first and live:
                            routing(c - 1, u - 1)

                act.sem_inc(sem(st + "_slice_gone"), 1)
                act.sem_inc(sem(st + "_pT"), CRED)
                act.sem_inc(sem(st + "_exp"), CRED)
                act.sem_inc(sem(st + "_pv_done"), CRED)
                act.sem_inc(sem(st + "_oT"), 3 if l0 else 1)
                if not l0:
                    act.sem_inc(sem("A3_y"), 1)
                    act.sem_inc(sem("A3_oT_full"), 4)
                    act.sem_inc(sem("F3_rows_copied"), 1)
                for s in range(kA):
                    if l0 and s == AHEAD0:
                        setup()
                    piece(0, 0, s, first=True)
                body(0, 0, True, True)
                with act.Fori(0, NC // 2 - 2) as i:
                    for p in range(2):
                        body(i * 2 + (p + 1), 1 - p, True)
                body(NC - 3, 1, True)
                body(NC - 2, 0, True)
                body(NC - 1, 1, False)
                body(NC, 0, False, live=False)

            heads("A0")

            stage_start(act, STAGE["F0"])
            act.sem_inc(sem("F0_tanh"), 1)
            act.sem_inc(sem("F0_silu"), 2)

            def f0(c):
                act.wait_ge(sem("F0_xT"), c + 1)
                copy(xnT[:, :], bank[0][:, :]).then_inc(sem("F0_xnT"), 1)
                copy(cin0[:, :, TAPS0 - 1:TAPS0 - 1 + P], b4(0)).then_inc(sem("F0_conv_in"), 1)
                act.wait_ge(s_xn, c + (1 + XN0["F0"]))
                act.sem_inc(s_held, 1)
                copy(xall0[:, bass.ds(c * CB, CB), :], xn[:, :, :]).then_inc(sem("F0_xn_kept"), 1)
                act.wait_ge(sem("F0_router"), c + 1)
                act.wait_ge(sem("F0_weights"), c + 1)
                nc.scalar.activation(lg0[:, :, :], bank[0][:, 0:CB * R0].rearrange("p (j r) -> p j r", j=CB), ACT.Tanh, scale=0.5)\
                    .then_inc(sem("F0_tanh"), 1)
                for k in range(2):
                    act.wait_ge(sem("F0_gate"), c * 2 + (k + 1))
                    act.wait_ge(sem("F0_hid"), c * 2 + (k + 1))
                    nc.scalar.activation(sg0[:, k, :], bank[1 + 2 * k][:, :], ACT.Silu)
                    act.wait_ge(sem("F0_up"), c * 2 + (k + 1))
                    copy(up0[:, k, :], bank[2 + 2 * k][:, :]).then_inc(sem("F0_silu"), 1)

            with act.Fori(0, NC) as c:
                f0(c)

            def single(st):
                before = 0 if st == "A1" else NC
                stage_start(act, STAGE[st])

                def front(c, first, back):
                    act.wait_ge(sem("A12_xT"), c + 1 + before)
                    if not first:
                        act.wait_ge(sem("A12_q"), c + before)
                    copy(xnT[:, :], bank[0][:, :]).then_inc(sem("A12_xnT"), 1)
                    act.wait_ge(s_cT, c + (1 + CX0[st]))
                    if not first:
                        act.wait_ge(sem("A12_v"), c + before)
                    copy(cxT[:, 0, :], bank[1][:, :]).then_inc(sem("A12_cxT"), 1)
                    if back:
                        exponentials(c - 1)
                    if not first:
                        act.wait_ge(sem("A12_scores"), c + before)
                    act.wait_ge(sem("A12_q"), c + 1 + before)
                    bias = bq2[:, 0:1] if st == "A2" else 0.0
                    aff(qT1[:, :], bank[2][:, :], float(P) ** -0.5, bias).then_inc(sem("A12_qT"), 1)
                    act.wait_ge(sem("A12_k"), c + 1 + before)
                    aff(kT1[:, :], bank[3][:, :], 1.0, bk2[:, 0:1] if st == "A2" else 0.0).then_inc(sem("A12_kT"), 1)
                    if back and st == "A2":
                        probs_T(c - 1)

                def exponentials(c):
                    act.wait_ge(sem(st + "_less_max"), c + 1)
                    act.wait_ge(sem("A12_pv_done"), c + before)
                    act.wait_ge(sem("A12_summed"), c + before)
                    exp(pr[:, 0, :, :], sm[:, 0, :, :]).then_inc(sem("A12_exp"), 1)

                def probs_T(c):
                    act.wait_ge(sem(st + "_pT_full"), c + 1)
                    act.wait_ge(sem("A12_pv_done"), c + before)
                    copy(pT[:, 0, :, :], b4(5)).then_inc(sem(st + "_pT"), 1)

                front(0, True, False)
                with act.Fori(0, NC // 2 - 1) as i:
                    for p in range(2):
                        front(i * 2 + (p + 1), False, True)
                front(NC - 1, False, True)
                exponentials(NC - 1)
                if st == "A2":
                    probs_T(NC - 1)

            single("A1")

            stage_start(act, STAGE["F1"])
            act.sem_inc(sem("F1_hqT"), 1)

            rnd = lambda o, i, sc: nc.scalar.activation(o, i, ACT.Identity, scale=sc, bias=round3[:, 0:1])

            def up1(c, first):
                act.wait_ge(sem("F1_xT"), c + 1)
                if not first:
                    act.wait_ge(sem("F1_h"), c * K1)
                copy(xqT1[:, :], bank[0][:, 0:W // 2].bitcast(BF16)).then_inc(sem("F1_xqT"), 1)

            def scales(c, first):
                act.wait_ge(sem("F1_scaleT"), c + 2)
                if not first:
                    act.wait_ge(sem("F1_hs"), c * K1)
                copy(sbc1[:, :], bank[0][:, :]).then_inc(sem("F1_sbc"), 1)

            def f1(c, more, first):
                def middle(c, k):
                    act.wait_ge(sem("F1_hs"), c * K1 + (k + 1))
                    if k >= 2 or not isinstance(c, int) or c:
                        act.wait_ge(sem("F1_silu"), c * K1 + (k - 1))
                    nc.scalar.activation(hc1[:, k % 2, :, :], hs1[:, k % 2, :, :], ACT.Copy, scale=cw1[:, k, 1:2]).then_inc(sem("F1_middle"), 1)

                def silu(k):
                    act.wait_ge(sem("F1_conv"), c * K1 + (k + 1))
                    if k == 0 and not first:
                        act.wait_ge(sem("F1_hT"), c * CB)
                    nc.scalar.activation(h1[:, k, :].rearrange("p (j t) -> p j t", j=CB), hc1[:, k % 2, :, :], ACT.Silu,
                                         bias=cb1[:, k:k + 1]).then_inc(sem("F1_silu"), 1)

                if first:
                    middle(c, 0)
                for k in range(1, K1):
                    if k >= 2 or first:
                        middle(c, k)
                    if k >= 2 and not first:
                        integers_T(c - 1, k - 2)
                    silu(k - 1)
                silu(K1 - 1)
                if more:
                    up1(c + 1, False)
                    scales(c + 1, False)
                act.wait_ge(sem("F1_scale2"), c + 1)
                for j in range(CB):
                    rnd(hr1[:, j, :], HT1[j][:, :], sc2[:, j:j + 1]).then_inc(sem("F1_round2"), 1)
                    if more and j in MIDDLE1:
                        middle(c + 1, MIDDLE1.index(j))

            def integers_T(c, q):
                act.wait_ge(sem("F1_hqT_full"), c * 2 + (q + 1))
                act.wait_ge(sem("F1_y"), c * 2 + (q + 1))
                copy(hqT1[:, q, :], bank[0][:, :].bitcast(BF16)).then_inc(sem("F1_hqT"), 1)

            up1(0, True)
            scales(0, True)
            f1(0, True, True)
            with act.Fori(1, NC - 1) as c:
                f1(c, True, False)
            f1(NC - 1, False, False)
            for q in range(2):
                integers_T(NC - 1, q)

            single("A2")

            stage_start(act, STAGE["F2"])

            xT2 = [xnT, cx[:, :, :].rearrange("p j d -> p (j d)")]

            def chunk_T(c, p):
                act.wait_ge(sem("F2_xT"), c + 1)
                copy(xT2[p][:, :], bank[0][:, :]).then_inc(sem("F2_xnT"), 1)

            def choice(c):
                act.wait_ge(sem("F2_less_max"), c + 1)
                exp(ex2[:, :, :], lg2[:, :, :]).then_inc(sem("F2_exp"), 1)
                act.wait_ge(sem("F2_ohT_full"), c + 1)
                copy(ohT2[:, :], bank[6][0:E2, :]).then_inc(sem("F2_ohT"), 1)

            chunk_T(0, 0)
            chunk_T(1, 1)
            choice(0)
            with act.Fori(0, NC // 2 - 1) as i:
                for p in range(2):
                    choice(i * 2 + (p + 1))
                    chunk_T(i * 2 + (p + 2), p)
            choice(NC - 1)

            stage_start(act, STAGE["A3"])
            heads("A3")

            stage_start(act, STAGE["F3"])
            act.sem_inc(sem("F3_w_sb"), 4)

            def expert_T(e, p):
                one = bass.ds(e, 1)
                for w, wT in enumerate((w1T3, w2T3)):
                    act.wait_ge(sem("F3_weights_transposed"), e * 2 + (w + 1))
                    act.sem_inc(sem("held"), 1)
                    copy(wT[:, one, :], bank[2 * p + w][:, :].unsqueeze(1)).then_inc(sem("F3_w_sb"), 1)

            routing(NC - 1, 8)
            for e in range(2):
                expert_T(e, e)
            for e in range(2, 4):
                expert_T(e, e % 2)
            routing(NC - 1, 10)
            with act.Fori(2, E3 // 2) as i:
                for p in range(2):
                    expert_T(i * 2 + p, p)

            def tile_T(n, s):
                act.wait_ge(sem("F3_tile_T"), n + 1)
                copy(xnT[:, (s % 4) * P:(s % 4) * P + P], bank[6 + s % 2][:, 0:P]).then_inc(sem("F3_tile_xT"), 1)

            def up(n, s):
                act.wait_ge(sem("F3_up"), n + 1)
                for k in range(K3):
                    last = nc.scalar.activation(h3[:, s % 2, k * P:k * P + P], bank[s % 2][:, k * P:k * P + P], ACT.Gelu,
                                                bias=b1c3[:, s % 4, k:k + 1])
                last.then_inc(sem("F3_gelu"), 1)

            tile_T(0, 0)
            tile_T(1, 1)
            with act.Fori(0, GROUPS3 - 1) as g:
                for s in range(SLOTS3):
                    up(g * SLOTS3 + s, s)
                    tile_T(g * SLOTS3 + (s + 2), s + 2)
            for s in range(SLOTS3):
                n = NT - SLOTS3 + s
                up(n, s)
                if n + 2 < NT:
                    tile_T(n + 2, s + 2)

        @block.vector
        def _(dve):
            v = nc.vector
            step = Steps(dve, sem("vector_steps"))
            s_held = sem("held")
            dve.sem_inc(s_xdone, 1)
            dve.wait_ge(s_first, 16 * n_first)
            dve.wait_ge(s_const, 1)
            for t, b in enumerate((bk0g, bv0g)):
                v.tensor_reduce(wkvs0[:, t * D0:t * D0 + D0], wkv0[:, t, :].rearrange("p (g d) -> p d g", g=4), AX, ALU.add)
                v.tensor_reduce(bkv0[:, t * D0:t * D0 + D0], b[:, :].rearrange("p (g d) -> p d g", g=4), AX, ALU.add)
            step(v.tensor_scalar(bq0[:, :, :].rearrange("p (j h) d -> p j (h d)", j=CB), bq0row[:, :].unsqueeze(1).to_broadcast([P, CB, P]),
                                 float(D0) ** -0.5, None, ALU.mult))
            def setup():
                dve.wait_ge(s_load, 16 * n_loads)
                step(v.tensor_scalar(bq2[:, :], bq2[:, :], float(P) ** -0.5, None, ALU.mult))
                dve.wait_ge(sem("setup_gates"), 1)
                step(v.tensor_tensor(gate3[:, :], gates[:, 3:4], gates[:, 8:9], ALU.mult))
                v.tensor_reduce(part[:, 0:1], w1n[:, :, :].rearrange("p k d -> p (k d)"), AX, ALU.add, apply_absolute_value=True)
                v.tensor_reduce(part[:, 1:2], w2n[:, :], AX, ALU.add, apply_absolute_value=True).then_inc(sem("setup_vector"), 1)
                s_bk, s_gone = sem("setup_bank_full"), sem("setup_bank_gone")
                dve.wait_ge(s_gone, 3)
                step(v.scalar_tensor_tensor(wr3[:, :], keyT[:, 0, :], 2.0, keyT[:, 1, :], ALU.mult, ALU.add))
                v.tensor_tensor(keysq[:, :], keyT[:, 0, :], keyT[:, 0, :], ALU.mult).then_inc(sem("setup_vector"), 1)
                dve.wait_ge(s_bk, 4)
                step(v.tensor_scalar(wsc1[:, :], bank[3][:, 0:1], 1.0 / (H1 * P), EPS, ALU.mult, ALU.max))
                step(v.tensor_scalar(wsc2[:, :], bank[3][:, 1:2], 1.0 / (H1 * P), EPS, ALU.mult, ALU.max))
                dve.wait_ge(s_bk, 5)
                step(v.tensor_tensor(rb3[:, :], rb3[:, :], bank[4][:, 0:E3], ALU.subtract))
                dve.sem_inc(s_gone, 2)
                dve.sem_inc(sem("setup_vector"), 1)
                for t, (src, wsc) in enumerate(((w1n[:, :, :].rearrange("p k d -> p (k d)"), wsc1), (w2n[:, :], wsc2))):
                    step(v.reciprocal(rs[:, t:t + 1], wsc[:, :]))
                    step(v.tensor_scalar(wabs[:, t, :], src, rs[:, t:t + 1], ROUND, ALU.mult, ALU.add))
                    step(v.tensor_scalar(wabs[:, t, :], wabs[:, t, :], ROUND, 1.0, ALU.subtract, ALU.min))
                    step(v.tensor_scalar(wabs[:, t, :], wabs[:, t, :], -1.0, None, ALU.max))
                    step(v.tensor_scalar(wsc[:, :], wsc[:, :], 1.0 / 127, None, ALU.mult))
                dve.sem_inc(sem("setup_vector"), 1)
                dve.wait_ge(s_gone, 7)
                dve.sem_inc(sem("setup_done"), 1)

            def norm_stats(src):
                for j in range(CB):
                    last = v.bn_stats(stats[:, j, :], src[:, j, :])
                step.held(last, s_held)
                for j in range(CB):
                    last = v.bn_aggr(mv[:, j, :], stats[:, j, :])
                step(last)

            def norm_var(st):
                v.tensor_scalar(ve[:, :].unsqueeze(2), mv[:, :, 1:2], EPS, None, ALU.add).then_inc(s_var, 1)

            def norm_apply(st, c, src, n=None, ready=True, free=None):
                dve.wait_ge(s_rstd, (c if n is None else n) + (1 + VAR0[st]))
                if free is not None:
                    dve.wait_ge(*free)
                for j in range(CB):
                    last = v.tensor_scalar(xn[:, j, :], src[:, j, :], mv[:, j, 0:1], rstd[:, j:j + 1], ALU.subtract, ALU.mult)
                if ready:
                    last.then_inc(s_xn, 1)
                else:
                    step(last)

            def xc(c):
                return x[:, bass.ds(c * CB, CB), :]

            def less_max(src, dst, slot, st):
                step(v.tensor_reduce(nm[:, slot, :], src, AX, ALU.max))
                v.tensor_tensor(dst, src, nm[:, slot, :].unsqueeze(2).to_broadcast([P, CB, P]), ALU.subtract)\
                    .then_inc(sem(st + "_less_max"), 1)

            def routing(c, u):
                if u == 6:
                    norm_stats(xc(c))
                    v.tensor_scalar(ve[:, :].unsqueeze(2), mv[:, :, 1:2], EPS, None, ALU.add).then_inc(sem("F3_variance"), 1)
                if u == 7:
                    dve.wait_ge(sem("F3_inverse_deviation"), c + 1)
                    dve.wait_ge(sem("F3_rows_copied"), c + 1)
                    for j in range(CB):
                        last = v.tensor_scalar(xr3[:, j, :], xc(c)[:, j, :], mv[:, j, 0:1], rstd[:, j:j + 1], ALU.subtract, ALU.mult)
                    last.then_inc(sem("F3_normalised"), 1)
                if u == 9:
                    dve.wait_ge(sem("F3_rows_free"), c + 1)
                    step(v.tensor_copy(rowsu3[:, :, P:P + 1], goes3[:, :].unsqueeze(2)))
                    v.tensor_scalar(goes3[:, :], goes3[:, :], float(W), None, ALU.add)
                    step(v.tensor_tensor(tmp[:, :, :], xr3[:, :, :], xr3[:, :, :], ALU.mult))
                    step(v.tensor_reduce(x23[:, :], tmp[:, :, :], AX, ALU.add))
                    dve.wait_ge(sem("F3_lg"), c + 1)
                    lgp = bank[5][:, 0:CB * E3].rearrange("p (j e) -> p j e", j=CB)
                    step(v.tensor_tensor(lg3[:, :, :], lgp, rb3[:, :].unsqueeze(1).to_broadcast([P, CB, E3]), ALU.add))
                    step.held(v.tensor_tensor(lg3[:, :, :], lg3[:, :, :], x23[:, :].unsqueeze(2).to_broadcast([P, CB, E3]), ALU.subtract), s_held)
                    for j in range(CB):
                        last = v.max(top3[:, j, :], lg3[:, j, :])
                    step.held(last, s_held)
                    for j in range(CB):
                        last = v.max_index(idx3[:, j, :], top3[:, j, :], lg3[:, j, :])
                    step(last)
                    v.tensor_copy(idf3[:, :, :], idx3[:, :, 0:TOP3])
                    step(v.tensor_copy(es3[:, :].unsqueeze(2), top3[:, :, 0:1]))
                    v.tensor_tensor(top3[:, :, 0:TOP3], top3[:, :, 0:TOP3], es3[:, :].unsqueeze(2).to_broadcast([P, CB, TOP3]), ALU.subtract)\
                        .then_inc(sem("F3_less_max"), 1)
                    step(v.tensor_tensor(oh3[:, :, :], iota8[:, :].unsqueeze(1).to_broadcast([P, SC, E3]),
                                         idf3[:, :, :].rearrange("p j k -> p (j k)").unsqueeze(2).to_broadcast([P, SC, E3]), ALU.is_equal))
                    v.tensor_reduce(ohs3[:, :, :], oh3[:, :, :].rearrange("p (j k) e -> p j e k", j=CB), AX, ALU.add).then_inc(sem("F3_chosen"), 1)
                if u == 12:
                    dve.wait_ge(sem("F3_exp"), c + 1)
                    step(v.tensor_reduce(es3[:, :], ex3[:, :, :], AX, ALU.add))
                    step(v.reciprocal(es3[:, :], es3[:, :]))
                    step(v.tensor_scalar(es3[:, :], es3[:, :], gates[:, 7:8], None, ALU.mult))
                    step(v.tensor_tensor(wt3[:, bass.ds(c * SC, SC)].rearrange("p (j k) -> p j k", j=CB), ex3[:, :, :],
                                         es3[:, :].unsqueeze(2).to_broadcast([P, CB, TOP3]), ALU.mult))
                    dve.wait_ge(sem("F3_counts"), c + 1)
                    for j in range(CB):
                        step(v.tensor_tensor(dst3[:, j, :], bank[5][:, j * E3:j * E3 + E3], run3[:, :], ALU.add))
                        step(v.tensor_tensor(run3[:, :], bank[5][:, (CB + j) * E3:(CB + j + 1) * E3], run3[:, :], ALU.add))
                    o4 = oh3[:, :, :].rearrange("p (j k) e -> p j k e", j=CB)
                    step(v.tensor_tensor(o4, o4, dst3[:, :, :].unsqueeze(2).to_broadcast([P, CB, TOP3, E3]), ALU.mult))
                    step(v.tensor_reduce(to3[:, :], oh3[:, :, :], AX, ALU.add))
                    v.tensor_copy(di3[:, :], to3[:, :]).then_inc(sem("F3_rows_ready"), 1)

            def heads(st):
                l0 = st == "A0"
                kA = len(SLICES0) if l0 else 2 + HEADS + 2 * CB
                bias, gate = (bo0, gates[:, 0:1]) if l0 else (bo3, gate3[:, 0:1])
                parts = (3, 5, 8, 12, 14) if l0 else (2, 3, 4, 5)

                def softmax(n0, u, first):
                    dve.wait_ge(sem(st + "_scores"), n0 + (u + 1))
                    if not (first and u < 4):
                        dve.wait_ge(sem(st + "_pT_full"), n0 + (u - 3))
                    less_max(b4(u % 2), ex[:, u % 4, :, :], u % 2, st)

                def normal(c, p, n0, u):
                    j, qd = divmod(u, QUARTERS)
                    if l0:
                        if qd != 0:
                            return
                        dve.wait_ge(sem("A0_oT_full"), c * (2 * CB) + (2 * j + 1))
                        o = bank[4 + j % 2][:, :].rearrange("p (i q r) -> p q i r", i=HQ, r=ROWS0)
                        sums0 = rs[:, :].rearrange("p (q i a) -> p q i a", q=QUARTERS, a=1)
                        step(v.reciprocal(sums0, o[:, :, :, D0:D0 + 1]))
                        v.tensor_tensor(on0[:, j % 2, :].rearrange("p (q i d) -> p q i d", q=QUARTERS, d=D0), o[:, :, :, 0:D0],
                                        sums0.to_broadcast([P, QUARTERS, HQ, D0]), ALU.mult).then_inc(sem("A0_normal"), 1)
                        return
                    dve.wait_ge(sem(st + "_pv_done"), n0 + (u + 1 + CRED))
                    if qd == 0:
                        dve.wait_ge(sem("A3_oT_full"), c * (2 * CB) + (2 * j + 2))
                    o = bank[4][:, 0:HQ * (D3 + 1)].rearrange("p (h d) -> p h d", d=D3 + 1)
                    step(v.reciprocal(rs[:, 0:HQ].unsqueeze(2), o[:, :, D3:D3 + 1]))
                    of_unit = slice(head3(qd, 0), head3(qd, HQ - 1) + 1, 2)
                    v.tensor_tensor(on3[:, j % 2, :].rearrange("p (h d) -> p h d", d=D3)[:, of_unit, :], o[:, :, 0:D3],
                                    rs[:, 0:HQ].unsqueeze(2).to_broadcast([P, HQ, D3]), ALU.mult).then_inc(sem("A3_normal"), 1)

                def front(c, k):
                    if l0:
                        if k < 2:
                            for j in (2 * k, 2 * k + 1):
                                last = v.bn_stats(stats[:, j, :], xc(c)[:, j, :])
                            if k:
                                step.held(last, s_held)
                        if k == 2:
                            for j in range(CB):
                                last = v.bn_aggr(mv[:, j, :], stats[:, j, :])
                            step(last)
                            norm_var(st)
                        if k == 3:
                            dve.wait_ge(s_rstd, c + (1 + VAR0[st]))
                            if not isinstance(c, int) or c:
                                dve.wait_ge(sem(st + "_xnT"), c)
                        if k >= 3:
                            for j in (2 * k - 6, 2 * k - 5):
                                last = v.tensor_scalar(xn[:, j, :], xc(c)[:, j, :], mv[:, j, 0:1], rstd[:, j:j + 1], ALU.subtract, ALU.mult)
                            if k == 4:
                                last.then_inc(s_xn, 1)
                        return
                    if k == 0:
                        norm_stats(xc(c))
                        norm_var(st)
                    if k == 1:
                        norm_apply(st, c, xc(c), n=c * 2, ready=False, free=(sem(st + "_xnT"), c) if not isinstance(c, int) or c else None)
                    if k == 2:
                        norm_stats(xn)
                        norm_var(st)
                    if k == 3:
                        norm_apply(st, c, xn, n=c * 2 + 1)

                def body(c, p, more, first=False, live=True, ahead=True):
                    for u in range(UNITS if live else (DRAIN0 if l0 else DRAIN3)):
                        if more and ahead and u in parts:
                            front(c + 2, parts.index(u))
                        if live:
                            softmax(c * UNITS, u, first)
                        unit = lagging(c, p, u, 8 if l0 else 3, first, live)
                        if unit:
                            normal(unit[0], unit[1], unit[0] * UNITS, unit[2])
                        if u == (7 if l0 else 5) and not first:
                            dve.wait_ge(sem(st + "_y"), c * CB + (0 if l0 else 1))
                            step(v.tensor_tensor(tmp[:, :, :], b4(7), bias[:, :].unsqueeze(1).to_broadcast([P, CB, P]), ALU.add))
                            v.scalar_tensor_tensor(xc(c - 1), tmp[:, :, :], gate, xc(c - 1), ALU.mult, ALU.add).then_inc(s_xdone, 1)
                        if not l0 and not first and live:
                            routing(c - 1, u - 1)

                dve.sem_inc(sem(st + "_less_max"), CRED)
                if not l0:
                    dve.sem_inc(sem(st + "_normal"), 1)
                    for s in range(2):
                        v.memset(v3[s][:, :, :, D3:D3 + 1], 1.0)
                    dve.wait_ge(sem("F3_constants"), 1)
                    step(v.tensor_copy(run3[:, :], first3[:, :]))
                for c in range(2):
                    for k in range(len(parts)):
                        front(c, k)
                if l0:
                    setup()
                body(0, 0, True, True)
                step.loop(2 * (UNITS + CB + 1 + 2) if l0 else 2 * (UNITS + UNITS + 1 + 5 + 25))
                with dve.Fori(0, NC // 2 - 2) as i:
                    step.turn(i)
                    for p in range(2):
                        body(i * 2 + (p + 1), 1 - p, True)
                step.end(NC // 2 - 2)
                body(NC - 3, 1, True)
                body(NC - 2, 0, True, ahead=False)
                body(NC - 1, 1, False)
                body(NC, 0, False, live=False)

            heads("A0")

            stage_start(dve, STAGE["F0"])
            dve.sem_inc(sem("F0_hid"), 2)
            dve.sem_inc(sem("F0_weights"), 1)

            def f0_stats(c):
                norm_stats(xc(c))
                norm_var("F0")

            def f0_norm(c, first):
                dve.wait_ge(s_rstd, c + (1 + VAR0["F0"]))
                if not first:
                    dve.wait_ge(sem("F0_xT"), c)
                    dve.wait_ge(sem("F0_xn_kept"), c)
                for j in range(CB):
                    last = v.tensor_scalar(xn[:, j, :], xc(c)[:, j, :], mv[:, j, 0:1], rstd[:, j:j + 1], ALU.subtract, ALU.mult)
                last.then_inc(s_xn, 1)

            def router(c):
                dve.wait_ge(sem("F0_tanh"), c + 2)
                step(v.tensor_scalar(lg0[:, :, :], lg0[:, :, :], 0.5, 0.5, ALU.mult, ALU.add))
                step.held(v.tensor_tensor(sel0[:, :, :], lg0[:, :, :], rb0[:, :].unsqueeze(1).to_broadcast([P, CB, R0]), ALU.add), s_held)
                for j in range(CB):
                    last = v.max(top0[:, j, :], sel0[:, j, :])
                step.held(last, s_held)
                for j in range(CB):
                    last = v.max_index(idx0[:, j, :], top0[:, j, :], sel0[:, j, :])
                step(last)
                step(v.tensor_copy(idf0[:, :, :], idx0[:, :, :]))
                for r in range(2):
                    step(v.tensor_tensor(oh0[:, r, :, :], iota8[:, 0:R0].unsqueeze(1).to_broadcast([P, CB, R0]),
                                         idf0[:, :, r:r + 1].to_broadcast([P, CB, R0]), ALU.is_equal))
                step(v.tensor_tensor(oh0[:, 0, :, :], oh0[:, 0, :, :], oh0[:, 1, :, :], ALU.add))
                step(v.tensor_tensor(cwt0[:, :, :], oh0[:, 0, :, :], lg0[:, :, :], ALU.mult))
                step(v.tensor_reduce(wsum0[:, :], cwt0[:, :, :], AX, ALU.add))
                step(v.tensor_scalar(wsum0[:, :], wsum0[:, :], 1e-9, None, ALU.add))
                step(v.reciprocal(wsum0[:, :], wsum0[:, :]))
                step(v.tensor_tensor(cwt0[:, :, :], cwt0[:, :, :], wsum0[:, :].unsqueeze(2).to_broadcast([P, CB, R0]), ALU.mult))
                v.tensor_tensor(ccp0[:, :].unsqueeze(2), cwt0[:, :, E0:E0 + 1], cwt0[:, :, E0 + 2:E0 + 3], ALU.add).then_inc(sem("F0_weights"), 1)

            def f0(c, more, ahead):
                if more:
                    f0_norm(c + 1, False)
                dve.wait_ge(sem("F0_weights"), c + 2)
                dve.wait_ge(sem("F0_xn_kept"), c + 1)
                xk = xall0[:, bass.ds(c * CB, CB), :]
                for j in range(CB):
                    last = v.tensor_scalar(tmp2[:, j, :], xk[:, j, :], 0.0, cwt0[:, j, R0 - 1:R0], ALU.max, ALU.mult)
                step(last)
                for j in range(CB):
                    last = v.scalar_tensor_tensor(tmp[:, j, :], xk[:, j, :], ccp0[:, j:j + 1], tmp2[:, j, :], ALU.mult, ALU.add)
                step(last)
                for j0 in (0, 2):
                    dve.wait_ge(sem("F0_down"), c * CB + (j0 + 2))
                    before = [None, None]
                    for e in range(E0):
                        for q in range(2):
                            j = j0 + q
                            if e:
                                step.until(before[q])
                            before[q] = step.issue(v.scalar_tensor_tensor(tmp[:, j, :], b4(DOWN0[j])[:, e, :], cwt0[:, j, e:e + 1], tmp[:, j, :],
                                                                          ALU.mult, ALU.add))
                    step.until(before[1])
                    dve.sem_inc(sem("F0_down_read"), 2)
                dve.wait_ge(sem("F0_conv"), c + 1)
                step(v.tensor_tensor(tmp[:, :, :], b4(5), tmp[:, :, :], ALU.add))
                v.scalar_tensor_tensor(xc(c), tmp[:, :, :], gates[:, 4:5], xc(c), ALU.mult, ALU.add).then_inc(s_xdone, 1)
                if ahead:
                    f0_stats(c + 2)
                if more:
                    router(c + 1)

            f0_stats(0)
            f0_norm(0, True)
            f0_stats(1)
            router(0)
            f0(0, True, True)
            step.loop(13 + 2 + 2 + CB * E0 + 1)
            with dve.Fori(1, NC - 2) as c:
                step.turn(c - 1)
                f0(c, True, True)
            step.end(NC - 3)
            f0(NC - 2, True, False)
            f0(NC - 1, False, False)

            def single(st):
                before = 0 if st == "A1" else NC
                stage_start(dve, STAGE[st])
                gate = gates[:, 1:2] if st == "A1" else gates[:, 2:3]

                def ln(c, first):
                    norm_stats(xc(c))
                    norm_var(st)
                    norm_apply(st, c, xc(c), free=None if first else (sem("A12_xT"), c + before))

                def summed(c):
                    dve.wait_ge(sem("A12_exp"), c + 1 + before)
                    step(v.tensor_reduce(sums[:, :], pr[:, 0, :, :], AX, ALU.add))
                    step(v.reciprocal(sums[:, :], sums[:, :]))
                    dve.sem_inc(sem("A12_summed"), 1)
                    if st == "A1":
                        v.tensor_tensor(pr[:, 0, :, :], pr[:, 0, :, :], sums[:, :].unsqueeze(2).to_broadcast([P, CB, P]), ALU.mult)\
                            .then_inc(sem(st + "_normal"), 1)

                def residual(c):
                    dve.wait_ge(sem("A12_pv_done"), c + 1 + before)
                    if st == "A1":
                        v.scalar_tensor_tensor(xc(c), b4(6), gate, xc(c), ALU.mult, ALU.add).then_inc(s_xdone, 1)
                    else:
                        step(v.tensor_tensor(tmp[:, :, :], b4(6), sums[:, :].unsqueeze(2).to_broadcast([P, CB, P]), ALU.mult))
                        v.scalar_tensor_tensor(xc(c), tmp[:, :, :], gate, xc(c), ALU.mult, ALU.add).then_inc(s_xdone, 1)

                def scores(c, p, first):
                    dve.wait_ge(sem("A12_v"), c + 1 + before)
                    if st == "A1":
                        v.tensor_copy(v1[p][:, :, :], b4(4)).then_inc(sem("A12_v_sb"), 1)
                    else:
                        v.tensor_tensor(v1[p][:, :, :], b4(4), bv2[:, :].unsqueeze(1).to_broadcast([P, CB, P]), ALU.add).then_inc(sem("A12_v_sb"), 1)
                    dve.wait_ge(sem("A12_scores"), c + 1 + before)
                    if not first:
                        dve.wait_ge(sem("A12_exp"), c + before)
                    if st == "A1":
                        step(v.tensor_tensor(sm[:, 0, :, :], b4(7), causal[:, :].unsqueeze(1).to_broadcast([P, CB, P]), ALU.add))
                        less_max(sm[:, 0, :, :], sm[:, 0, :, :], 0, st)
                    else:
                        less_max(b4(7), sm[:, 0, :, :], 0, st)

                per = 2 + 2 + 1 + 1
                ln(0, True)
                ln(1, False)
                scores(0, 0, True)
                step.loop(2 * per)
                with dve.Fori(0, NC // 2 - 1) as i:
                    step.turn(i)
                    for p in range(2):
                        c = i * 2 + (p + 1)
                        norm_stats(xc(c + 1))
                        norm_var(st)
                        summed(c - 1)
                        norm_apply(st, c + 1, xc(c + 1), free=(sem("A12_xT"), c + 1 + before))
                        scores(c, 1 - p, False)
                        residual(c - 1)
                step.end(NC // 2 - 1)
                summed(NC - 2)
                scores(NC - 1, 1, False)
                residual(NC - 2)
                summed(NC - 1)
                residual(NC - 1)

            single("A1")

            stage_start(dve, STAGE["F1"])
            dve.sem_inc(sem("F1_scaleT"), 1)
            dve.sem_inc(sem("F1_y"), 2)

            def f1_norm(c, first):
                norm_apply("F1", c, xc(c), ready=False)
                if not first:
                    dve.wait_ge(sem("F1_scale_spread"), c)
                step(v.tensor_reduce(am1[:, :], xn[:, :, :], AX, ALU.max, apply_absolute_value=True))
                step(v.tensor_scalar(am1[:, :], am1[:, :], EPS, None, ALU.max))
                step(v.reciprocal(sc1[:, :], am1[:, :]))
                v.tensor_scalar(sc1[:, :], sc1[:, :], 127.0, None, ALU.mult).then_inc(sem("F1_scale1"), 1)
                dve.wait_ge(sem("F1_scale1"), c + 1)
                for j in range(CB):
                    last = v.tensor_scalar(xr1[:, j, :], xn[:, j, :], sc1[:, j:j + 1], ROUND, ALU.mult, ALU.add)
                step(last)
                if not first:
                    dve.wait_ge(sem("F1_xT"), c)
                v.tensor_scalar(xq1[:, :, :], xr1[:, :, :], ROUND, 127.0, ALU.subtract, ALU.min).then_inc(sem("F1_xq"), 1)

            def f1(c, more, first):
                def scaled(k):
                    dve.wait_ge(sem("F1_h"), c * K1 + (k + 1))
                    if k >= 2:
                        dve.wait_ge(sem("F1_middle"), c * K1 + (k - 1))
                    v.scalar_tensor_tensor(hs1[:, k % 2, :, :], b4(1 + k), wsc1[:, 0:1], sbc1[:, :].rearrange("p (j t) -> p j t", j=CB),
                                           ALU.mult, ALU.mult).then_inc(sem("F1_hs"), 1)

                def taps(k, between=lambda: None):
                    dve.wait_ge(sem("F1_middle"), c * K1 + (k + 1))
                    h, o = hs1[:, k % 2, :, :], hc1[:, k % 2, :, :]
                    one = step.issue(v.scalar_tensor_tensor(o[:, :, 1:P], h[:, :, 0:P - 1], cw1[:, k, 0:1], o[:, :, 1:P], ALU.mult, ALU.add))
                    between()
                    step.until(one)
                    v.scalar_tensor_tensor(o[:, :, 0:P - 1], h[:, :, 1:P], cw1[:, k, 2:3], o[:, :, 0:P - 1], ALU.mult, ALU.add)\
                        .then_inc(sem("F1_conv"), 1)
                    dve.wait_ge(sem("F1_conv"), c * K1 + (k + 1))

                back = (lambda j: None) if first else (lambda j: hq(c - 1, j))
                dve.wait_ge(sem("F1_sbc"), c + 1)
                scaled(0)
                back(0)
                scaled(1)
                back(1)
                taps(0, lambda: back(2))
                scaled(2)
                taps(1, lambda: back(3))
                scaled(3)
                taps(2)
                taps(3)
                if more:
                    norm_stats(xc(c + 1))
                    norm_var("F1")
                if not first:
                    residual1(c - 1)
                if more:
                    f1_norm(c + 1, False)
                for j in range(CB):
                    dve.wait_ge(sem("F1_hT"), c * CB + (j + 1))
                    last = v.tensor_reduce(am2[:, j:j + 1], HT1[j][:, :], AX, ALU.max, apply_absolute_value=True)
                step(last)
                step(v.tensor_scalar(am2[:, :], am2[:, :], EPS, None, ALU.max))
                step(v.reciprocal(sc2[:, :], am2[:, :]))
                v.tensor_scalar(sc2[:, :], sc2[:, :], 127.0, None, ALU.mult).then_inc(sem("F1_scale2"), 1)
                step(v.tensor_scalar(isc2[:, :], am2[:, :], wsc2[:, 0:1], gates[:, 5:6], ALU.mult, ALU.mult))

            def residual1(c):
                dve.wait_ge(sem("F1_y"), c * 2 + 4)
                for j in range(CB):
                    last = v.scalar_tensor_tensor(xc(c)[:, j, :], bank[5][:, j * P:j * P + P], isc2[:, j:j + 1], xc(c)[:, j, :], ALU.mult, ALU.add)
                last.then_inc(s_xdone, 1)

            def hq(c, j):
                dve.wait_ge(sem("F1_round2"), c * CB + (j + 1))
                v.tensor_scalar(hq1[:, j, :], hr1[:, j, :], ROUND, 127.0, ALU.subtract, ALU.min).then_inc(sem("F1_hq"), 1)

            norm_stats(xc(0))
            norm_var("F1")
            f1_norm(0, True)
            f1(0, True, True)
            step.loop(2 + 1 + 3 + 1 + K1 + 3 + 1)
            with dve.Fori(1, NC - 1) as c:
                step.turn(c - 1)
                f1(c, True, False)
            step.end(NC - 2)
            f1(NC - 1, False, False)
            for j in range(CB):
                hq(NC - 1, j)
            residual1(NC - 1)

            single("A2")

            stage_start(dve, STAGE["F2"])
            dve.sem_inc(sem("F2_z_read"), 4)
            dve.sem_inc(sem("F2_logits_read"), 1)

            def choose(c, p, ahead):
                dve.wait_ge(sem("F2_logits"), c + 1)
                v.tensor_tensor(lg2[:, :, :], b4(1), bg2[:, :].unsqueeze(1).to_broadcast([P, CB, P]), ALU.add).then_inc(sem("F2_logits_read"), 1)
                if ahead:
                    for j in range(CB):
                        v.bn_stats(stats[:, j, :], xc(c + 1)[:, j, :])
                dve.wait_ge(sem("F2_logits_read"), c + 2)
                dve.sem_inc(s_held, 1)
                for j in range(CB):
                    last = v.max(top2[:, j, :], lg2[:, j, :])
                step.held(last, s_held)
                if ahead:
                    for j in range(CB):
                        v.bn_aggr(mv[:, j, :], stats[:, j, :])
                for j in range(CB):
                    last = v.max_index(idx2[:, j, :], top2[:, j, :], lg2[:, j, :])
                step(last)
                if ahead:
                    norm_var("F2")
                v.tensor_tensor(lg2[:, :, :], lg2[:, :, :], top2[:, :, 0:1].to_broadcast([P, CB, P]), ALU.subtract).then_inc(sem("F2_less_max"), 1)
                step(v.tensor_single_scalar(idx2[:, :, 0:1], idx2[:, :, 0:1], E2 - 1, ALU.bitwise_and))
                step(v.tensor_copy(idf2[:, :].unsqueeze(2), idx2[:, :, 0:1]))
                v.tensor_tensor(oh2[p][:, :, :], iota8[:, 0:E2].unsqueeze(1).to_broadcast([P, CB, E2]),
                                idf2[:, :].unsqueeze(2).to_broadcast([P, CB, E2]), ALU.is_equal).then_inc(sem("F2_onehot"), 1)

            def probability(c):
                dve.wait_ge(sem("F2_exp"), c + 1)
                step(v.tensor_reduce(ps2[:, :], ex2[:, :, :], AX, ALU.add))
                step(v.reciprocal(pg2[:, :], ps2[:, :]))
                step(v.tensor_scalar(pg2[:, :], pg2[:, :], gates[:, 6:7], None, ALU.mult))

            def selected(c, p, u0):
                dve.wait_ge(sem("F2_z"), c * (2 * CB) + (u0 + 2))
                before = [None, None]
                for q in range(4):
                    e = u0 // 2 % 2 * 4 + q
                    for t in range(2):
                        j = u0 // 4 * 2 + t
                        z = b4(2 + (u0 + t) % 4)[:, q, :]
                        if q:
                            step.until(before[t])
                        if e == 0:
                            before[t] = step.issue(v.tensor_scalar(acc2[:, j, :], z, oh2[p][:, j, 0:1], None, ALU.mult))
                        else:
                            before[t] = step.issue(v.scalar_tensor_tensor(acc2[:, j, :], z, oh2[p][:, j, e:e + 1], acc2[:, j, :], ALU.mult, ALU.add))
                step.until(before[1])
                dve.sem_inc(sem("F2_z_read"), 2)

            def f2(c, p, next1, next2):
                selected(c, p, 0)
                selected(c, p, 2)
                if next1:
                    choose(c + 1, 1 - p, next2)
                selected(c, p, 4)
                selected(c, p, 6)
                dve.wait_ge(sem("F2_bias"), c + 1)
                step(v.tensor_tensor(acc2[:, :, :], acc2[:, :, :], b4(7), ALU.add))
                step(v.tensor_scalar(acc2[:, :, :], acc2[:, :, :], 0.0, None, ALU.max))
                for j in range(CB):
                    last = v.scalar_tensor_tensor(xc(c)[:, j, :], acc2[:, j, :], pg2[:, j:j + 1], xc(c)[:, j, :], ALU.mult, ALU.add)
                last.then_inc(s_xdone, 1)
                if next2:
                    norm_apply("F2", c + 2, xc(c + 2), free=(sem("F2_xT"), c + 2))
                if next1:
                    probability(c + 1)

            for c in range(2):
                norm_stats(xc(c))
                norm_var("F2")
                norm_apply("F2", c, xc(c), free=(sem("F2_xT"), c) if c else None)
            choose(0, 0, False)
            probability(0)
            step.loop(2 * (4 + 3 + 2 * CB * 4 + 2))
            with dve.Fori(0, NC // 2 - 1) as i:
                step.turn(i)
                for p in range(2):
                    f2(i * 2 + p, p, True, True)
            step.end(NC // 2 - 1)
            f2(NC - 2, 0, True, False)
            f2(NC - 1, 1, False, False)

            stage_start(dve, STAGE["A3"])
            heads("A3")

            stage_start(dve, STAGE["F3"])
            for u in (6, 7, 9, 12):
                routing(NC - 1, u)
            dve.wait_ge(sem("F3_constants"), 2)
            v.memset(padu3[:, P:P + 1], int(NOWHERE))

            step(v.tensor_tensor(cum3[:, 0, :], run3[:, :], first3[:, :], ALU.subtract))
            step(v.tensor_scalar(cnt3[:, :], cum3[:, 0, :], float(P - 1), None, ALU.add))
            step(v.tensor_single_scalar(cnt3[:, :], cnt3[:, :], P.bit_length() - 1, ALU.arith_shift_right))
            step(v.tensor_copy(tl3[:, :], cnt3[:, :]))
            step(v.tensor_copy(cum3[:, 0, :], tl3[:, :]))
            n, lag = 0, 1
            while lag < E3:
                v.tensor_copy(cum3[:, 1 - n, 0:lag], cum3[:, n, 0:lag])
                step(v.tensor_tensor(cum3[:, 1 - n, lag:E3], cum3[:, n, lag:E3], cum3[:, n, 0:E3 - lag], ALU.add))
                n, lag = 1 - n, 2 * lag
            step(v.tensor_tensor(until3[:, :, :], cum3[0:1, n, :].unsqueeze(1).to_broadcast([1, NT, E3]),
                                 iota3[:, :].unsqueeze(2).to_broadcast([1, NT, E3]), ALU.is_le))
            step(v.tensor_reduce(tabf3[:, 0, :], until3[:, :, :], AX, ALU.add))
            step(v.tensor_scalar(tabf3[:, 0, :], tabf3[:, 0, :], float(E3 - 1), None, ALU.min))
            step(v.tensor_scalar(tl3[:, :], tl3[:, :], -float(P), float(REGION), ALU.mult, ALU.add))
            step(v.tensor_tensor(until3[:, :, :], until3[:, :, :], tl3[0:1, :].unsqueeze(1).to_broadcast([1, NT, E3]), ALU.mult))
            step(v.tensor_reduce(tabf3[:, 1, :], until3[:, :, :], AX, ALU.add))
            step(v.scalar_tensor_tensor(tabf3[:, 1, :], iota3[:, :], float(P), tabf3[:, 1, :], ALU.mult, ALU.add))
            step(v.tensor_scalar(tabf3[:, 1, :], tabf3[:, 1, :], float(UNUSED), None, ALU.min))
            v.tensor_copy(ends3[:, :], run3[0:1, :])
            v.tensor_copy(tab3[:, :, :], tabf3[:, :, :]).then_inc(sem("F3_table"), 1)
            dve.wait_ge(sem("F3_table"), 1)

            dve.wait_ge(sem("F3_w_sb"), 2 * E3 + 4)
            dve.wait_ge(sem("F3_b2_loaded"), 16)
            dve.sem_inc(sem("F3_down"), 3)
            dve.sem_inc(sem("F3_output"), 2)

            def weights(n, s):
                e = dve.value_load(tab3[0:1, 0, bass.ds(n, 1)], min_val=0, max_val=E3 - 1)
                if not isinstance(n, int) or n >= 4:
                    dve.wait_ge(sem("F3_down"), n)
                v.tensor_copy(w1c3[:, s % 4, :], w1T3[:, :, :].rearrange("p e f -> p (e f)")[:, bass.ds(e * H3, H3)])
                if not isinstance(n, int) or n >= 4:
                    dve.wait_ge(sem("F3_output"), n - 1)
                v.tensor_copy(b2c3[:, s % 4, :], b2b3[:, bass.ds(e * P, P)])
                v.tensor_copy(b1c3[:, s % 4, :], b13[:, :, :].rearrange("p e k -> p (e k)")[:, bass.ds(e * K3, K3)])
                v.tensor_copy(w2c3[:, s % 4, :], w2T3[:, :, :].rearrange("p e f -> p (e f)")[:, bass.ds(e * H3, H3)])\
                    .then_inc(sem("F3_tile_weights"), 1)

            def output(n, s, g):
                if g is None and n < 3:
                    dve.wait_ge(sem("F3_tile_weights"), n + 1)
                dve.wait_ge(sem("F3_down"), n + 4)
                if g is not None:
                    dve.wait_ge(sem(f"F3_scattered{s // GROUP3}"), g * (16 * GROUP3))
                v.tensor_tensor(yt3[:, s, :], bank[2 + s % 2][:, 0:P], b2c3[:, s % 4, :], ALU.add).then_inc(sem("F3_output"), 1)

            for n in range(3):
                weights(n, n)
            for s in range(SLOTS3):
                weights(s + 3, s + 3)
                output(s, s, None)
            with dve.Fori(1, GROUPS3 - 1) as g:
                for s in range(SLOTS3):
                    weights(g * SLOTS3 + (s + 3), s + 3)
                    output(g * SLOTS3 + s, s, g)
            for s in range(SLOTS3):
                n = NT - SLOTS3 + s
                if n + 3 < NT:
                    weights(n + 3, s + 3)
                output(n, s, GROUPS3 - 1)

            def combine(c, p, i):
                dve.wait_ge(sem(f"F3_outputs_loaded{p}"), i * (16 * TOP3) + 16 * TOP3)
                for k in range(TOP3):
                    for j in range(CB):
                        last = v.scalar_tensor_tensor(xc(c)[:, j, :], combined[:, p, k, j, :], wt3[:, bass.ds(c * SC + (j * TOP3 + k), 1)],
                                                      xc(c)[:, j, :], ALU.mult, ALU.add)
                    if k < TOP3 - 1:
                        step(last)
                last.then_inc(s_xdone, 1)

            step.loop(2 * (TOP3 - 1))
            with dve.Fori(0, NC // 2) as i:
                step.turn(i)
                for p in range(2):
                    combine(i * 2 + p, p, i)
            step.end(NC // 2)


_OUT = (B, P, P)


def kernel(**inputs):
    import numpy as _np
    import concourse.bacc as _bacc
    from concourse import mybir as _mybir
    from concourse.bass_utils import run_bass_kernel_spmd as _run

    nc = _bacc.Bacc("TRN2", target_bir_lowering=False, num_devices=1)
    arrays, aps = {}, {}
    for name, value in inputs.items():
        arr = _np.ascontiguousarray(value)
        arrays[f"in_{name}"] = arr
        aps[name] = nc.dram_tensor(f"in_{name}", arr.shape, _mybir.dt.from_np(arr.dtype), kind="ExternalInput").ap()
    out = nc.dram_tensor("out_x", _OUT, _mybir.dt.float32, kind="ExternalOutput").ap()
    flamingo(nc, aps, out)
    r = _run(nc, [arrays], core_ids=[0])
    return r.results[0]["out_x"]
```
